# Optimizing a Trainium2 kernel written in Bass

```python
import numpy as np
import jax
import jax.numpy as jnp

def _softmax(x, axis=-1):
    return jax.nn.softmax(x, axis=axis)
def _gelu(x):
    return jax.nn.gelu(x, approximate=True)
def _silu(x):
    return jax.nn.silu(x)
def _sigmoid(x):
    return jax.nn.sigmoid(x)
def _layernorm(x, axis=-1, eps=1e-5):
    m = jnp.mean(x, axis=axis, keepdims=True)
    v = jnp.var(x, axis=axis, keepdims=True)
    return (x - m) / jnp.sqrt(v + eps)
def _scatter_add(tgt, idx, src, axis=0):
    return tgt.at[idx].add(src)
def _segment_sum(src, seg, n):
    return jax.ops.segment_sum(src, seg, n)

kernel_name = 'mk_conv_attn_hybrid_d2_conv_nhwc256_8cb289'

def setup_inputs(seed: int = 0):
    np.random.seed(seed)
    _w = jnp.asarray
    def _rec_inputs():
        import jax
        import jax.numpy as jnp
        _gk = jax.random.key(seed)
        x = -0.0005207 + 1.001 * jax.random.normal(jax.random.fold_in(_gk, 1), (8, 32, 32, 256), jnp.float32)
        return x
    x = _rec_inputs()
    def _L0_conv_setup():
        import jax, jax.numpy as jnp
        import numpy as np
        from jax import lax
        NH = 8
        DK = 64
        DV = 64
        DKH = DK // NH
        DVH = DV // NH
        H = W = 32
        CIN = 256
        FILTERS = 256

        def rel_to_abs(x):
            B, N, L, _ = x.shape
            x = jnp.pad(x, ((0, 0), (0, 0), (0, 0), (0, 1)))
            flat = x.reshape(B, N, L * 2 * L)
            flat = jnp.pad(flat, ((0, 0), (0, 0), (0, L - 1)))
            final = flat.reshape(B, N, L + 1, 2 * L - 1)
            return final[:, :, :L, L - 1:]

        def rel_logits_1d(q, rel_k, h, w, perm):
            B = q.shape[0]
            rel = jnp.einsum('bnxyd,md->bnxym', q, rel_k)
            rel = rel.reshape(B, NH * h, w, 2 * w - 1)
            rel = rel_to_abs(rel)
            rel = rel.reshape(B, NH, h, w, w)[:, :, :, None]
            rel = jnp.broadcast_to(rel, (B, NH, h, h, w, w))
            rel = jnp.transpose(rel, perm)
            return rel.reshape(B, NH, h * w, h * w)
        key = jax.random.key(seed)
        ks = jax.random.split(key, 6)
        s = lambda fan_in: 1.0 / np.sqrt(fan_in)
        return {'x': jax.random.normal(ks[0], (8, H, W, CIN), jnp.float32), 'conv_w': jax.random.normal(ks[1], (3, 3, CIN, FILTERS - DV), jnp.float32) * s(9 * CIN), 'conv_b': jnp.zeros((FILTERS - DV,), jnp.float32), 'qkv_w': jax.random.normal(ks[2], (CIN, 2 * DK + DV), jnp.float32) * s(CIN), 'qkv_b': jnp.zeros((2 * DK + DV,), jnp.float32), 'attn_w': jax.random.normal(ks[3], (DV, DV), jnp.float32) * s(DV), 'attn_b': jnp.zeros((DV,), jnp.float32), 'key_rel_w': jax.random.normal(ks[4], (2 * W - 1, DKH), jnp.float32), 'key_rel_h': jax.random.normal(ks[5], (2 * H - 1, DKH), jnp.float32)}
    _L0_conv_all = _L0_conv_setup()
    _L0_conv_in = {k: v for k, v in _L0_conv_all.items() if k in ('conv_w', 'conv_b', 'qkv_w', 'qkv_b', 'attn_w', 'attn_b', 'key_rel_w', 'key_rel_h', )}
    del _L0_conv_all

    def _L1_attn_setup():
        import jax, jax.numpy as jnp
        import numpy as np
        B, S, D, U = (8, 2048, 256, 128)
        key = jax.random.key(seed)
        ks = jax.random.split(key, 5)
        inputs = jax.random.normal(ks[0], (B, S, D), dtype=jnp.float32)
        W_q = jax.random.normal(ks[1], (D, U), dtype=jnp.float32) * (1.0 / np.sqrt(D))
        W_k = jax.random.normal(ks[2], (D, U), dtype=jnp.float32) * (1.0 / np.sqrt(D))
        W_v = jax.random.normal(ks[3], (D, U), dtype=jnp.float32) * (1.0 / np.sqrt(D))
        W_o = jax.random.normal(ks[4], (U, D), dtype=jnp.float32) * (1.0 / np.sqrt(U))
        b_o = jnp.zeros((D,), dtype=jnp.float32)
        return {'inputs': inputs, 'W_q': W_q, 'W_k': W_k, 'W_v': W_v, 'W_o': W_o, 'b_o': b_o}
    _L1_attn_all = _L1_attn_setup()
    _L1_attn_in = {k: v for k, v in _L1_attn_all.items() if k in ('W_q', 'W_k', 'W_v', 'W_o', 'b_o', )}
    del _L1_attn_all

    def _L1_ffn_setup():
        import math
        import jax, jax.numpy as jnp
        import numpy as np
        CAPACITY_FACTOR = 1.25
        TOP_K = 2
        LN_EPS = 1e-05

        def _layer_norm(x, gamma, beta):
            mu = jnp.mean(x, axis=-1, keepdims=True)
            var = jnp.var(x, axis=-1, keepdims=True)
            return (x - mu) * jax.lax.rsqrt(var + LN_EPS) * gamma + beta
        key = jax.random.key(seed)
        ks = jax.random.split(key, 4)
        B, S, D, F, E = (8, 4096, 256, 512, 8)
        x = jax.random.normal(ks[0], (B, S, D), dtype=jnp.float32)
        Wr = jax.random.normal(ks[1], (D, E), dtype=jnp.float32) / np.sqrt(D)
        br = jnp.zeros((E,), jnp.float32)
        W1 = jax.random.normal(ks[2], (E, D, F), dtype=jnp.float32) / np.sqrt(D)
        b1 = jnp.zeros((E, F), jnp.float32)
        W2 = jax.random.normal(ks[3], (E, F, D), dtype=jnp.float32) / np.sqrt(F)
        b2 = jnp.zeros((E, D), jnp.float32)
        gamma = jnp.ones((D,), jnp.float32)
        beta = jnp.zeros((D,), jnp.float32)
        return {'x': x, 'Wr': Wr, 'br': br, 'W1': W1, 'b1': b1, 'W2': W2, 'b2': b2, 'gamma': gamma, 'beta': beta}
    _L1_ffn_all = _L1_ffn_setup()
    _L1_ffn_in = {k: v for k, v in _L1_ffn_all.items() if k in ('Wr', 'br', 'W1', 'b1', 'W2', 'b2', 'gamma', 'beta', )}
    del _L1_ffn_all

    return {
        "x": x,
        "L0_conv_conv_w": _L0_conv_in["conv_w"],
        "L0_conv_conv_b": _L0_conv_in["conv_b"],
        "L0_conv_qkv_w": _L0_conv_in["qkv_w"],
        "L0_conv_qkv_b": _L0_conv_in["qkv_b"],
        "L0_conv_attn_w": _L0_conv_in["attn_w"],
        "L0_conv_attn_b": _L0_conv_in["attn_b"],
        "L0_conv_key_rel_w": _L0_conv_in["key_rel_w"],
        "L0_conv_key_rel_h": _L0_conv_in["key_rel_h"],
        "L1_attn_W_q": _L1_attn_in["W_q"],
        "L1_attn_W_k": _L1_attn_in["W_k"],
        "L1_attn_W_v": _L1_attn_in["W_v"],
        "L1_attn_W_o": _L1_attn_in["W_o"],
        "L1_attn_b_o": _L1_attn_in["b_o"],
        "L1_ffn_Wr": _L1_ffn_in["Wr"],
        "L1_ffn_br": _L1_ffn_in["br"],
        "L1_ffn_W1": _L1_ffn_in["W1"],
        "L1_ffn_b1": _L1_ffn_in["b1"],
        "L1_ffn_W2": _L1_ffn_in["W2"],
        "L1_ffn_b2": _L1_ffn_in["b2"],
        "L1_ffn_gamma": _L1_ffn_in["gamma"],
        "L1_ffn_beta": _L1_ffn_in["beta"],
    }

def reference(x, L0_conv_conv_w, L0_conv_conv_b, L0_conv_qkv_w, L0_conv_qkv_b, L0_conv_attn_w, L0_conv_attn_b, L0_conv_key_rel_w, L0_conv_key_rel_h, L1_attn_W_q, L1_attn_W_k, L1_attn_W_v, L1_attn_W_o, L1_attn_b_o, L1_ffn_Wr, L1_ffn_br, L1_ffn_W1, L1_ffn_b1, L1_ffn_W2, L1_ffn_b2, L1_ffn_gamma, L1_ffn_beta):
    import jax
    import jax.numpy as jnp
    def _L0_conv_ref(x, conv_w, conv_b, qkv_w, qkv_b, attn_w, attn_b, key_rel_w, key_rel_h):
        import jax, jax.numpy as jnp
        import numpy as np
        from jax import lax
        NH = 8
        DK = 64
        DV = 64
        DKH = DK // NH
        DVH = DV // NH
        H = W = 32
        CIN = 256
        FILTERS = 256

        def rel_to_abs(x):
            B, N, L, _ = x.shape
            x = jnp.pad(x, ((0, 0), (0, 0), (0, 0), (0, 1)))
            flat = x.reshape(B, N, L * 2 * L)
            flat = jnp.pad(flat, ((0, 0), (0, 0), (0, L - 1)))
            final = flat.reshape(B, N, L + 1, 2 * L - 1)
            return final[:, :, :L, L - 1:]

        def rel_logits_1d(q, rel_k, h, w, perm):
            B = q.shape[0]
            rel = jnp.einsum('bnxyd,md->bnxym', q, rel_k)
            rel = rel.reshape(B, NH * h, w, 2 * w - 1)
            rel = rel_to_abs(rel)
            rel = rel.reshape(B, NH, h, w, w)[:, :, :, None]
            rel = jnp.broadcast_to(rel, (B, NH, h, h, w, w))
            rel = jnp.transpose(rel, perm)
            return rel.reshape(B, NH, h * w, h * w)
        B = x.shape[0]
        conv_out = lax.conv_general_dilated(x, conv_w, window_strides=(1, 1), padding='SAME', dimension_numbers=('NHWC', 'HWIO', 'NHWC')) + conv_b
        kqv = jnp.einsum('bhwc,co->bhwo', x, qkv_w) + qkv_b
        k = kqv[..., :DK]
        q = kqv[..., DK:2 * DK] * DKH ** (-0.5)
        v = kqv[..., 2 * DK:]

        def split_heads(t, d):
            return t.reshape(B, H, W, NH, d).transpose(0, 3, 1, 2, 4)
        qh = split_heads(q, DKH)
        kh = split_heads(k, DKH)
        vh = split_heads(v, DVH)
        qf = qh.reshape(B, NH, H * W, DKH)
        kf = kh.reshape(B, NH, H * W, DKH)
        vf = vh.reshape(B, NH, H * W, DVH)
        logits = jnp.einsum('bnid,bnjd->bnij', qf, kf)
        rel_w = rel_logits_1d(qh, key_rel_w, H, W, (0, 1, 2, 4, 3, 5))
        qh_t = qh.transpose(0, 1, 3, 2, 4)
        rel_h = rel_logits_1d(qh_t, key_rel_h, W, H, (0, 1, 4, 2, 5, 3))
        logits = logits + rel_w + rel_h
        weights = jax.nn.softmax(logits, axis=-1)
        attn = jnp.einsum('bnij,bnjd->bnid', weights, vf)
        attn = attn.reshape(B, NH, H, W, DVH).transpose(0, 2, 3, 1, 4).reshape(B, H, W, DV)
        attn = jnp.einsum('bhwc,co->bhwo', attn, attn_w) + attn_b
        return jnp.concatenate([conv_out, attn], axis=3)

    def _L1_attn_ref(inputs, W_q, W_k, W_v, W_o, b_o):
        import jax, jax.numpy as jnp
        import numpy as np
        B, S, D, U = (8, 2048, 256, 128)
        Q = jnp.einsum('bsd,du->bsu', inputs, W_q)
        K = jnp.einsum('bsd,du->bsu', inputs, W_k)
        V = jnp.einsum('bsd,du->bsu', inputs, W_v)
        scale = 1.0 / jnp.sqrt(jnp.asarray(U, dtype=inputs.dtype))
        attn = jnp.einsum('bqu,bku->bqk', Q, K) * scale
        w = jax.nn.softmax(attn, axis=-1)
        out = jnp.einsum('bqk,bku->bqu', w, V)
        return jnp.einsum('bsu,ud->bsd', out, W_o) + b_o + inputs

    def _L1_ffn_ref(x, Wr, br, W1, b1, W2, b2, gamma, beta):
        import math
        import jax, jax.numpy as jnp
        import numpy as np
        CAPACITY_FACTOR = 1.25
        TOP_K = 2
        LN_EPS = 1e-05

        def _layer_norm(x, gamma, beta):
            mu = jnp.mean(x, axis=-1, keepdims=True)
            var = jnp.var(x, axis=-1, keepdims=True)
            return (x - mu) * jax.lax.rsqrt(var + LN_EPS) * gamma + beta
        B, S, D = x.shape
        E = Wr.shape[1]
        N = B * S
        K = TOP_K
        logits = jnp.mean(x, axis=1) @ Wr + br
        routing_weights = jax.nn.softmax(logits, axis=-1)
        capacity = float(math.ceil(N * CAPACITY_FACTOR / E))
        expected_loads = routing_weights.sum(axis=0) * (N / B)
        scale = jnp.where(expected_loads > capacity, capacity / expected_loads, 1.0)
        routing_weights = jax.nn.softmax(routing_weights * scale, axis=-1)
        rw_tok = jnp.broadcast_to(routing_weights[:, None, :], (B, S, E)).reshape(N, E)
        top_w, top_i = jax.lax.top_k(rw_tok, K)
        top_w = jax.nn.softmax(top_w, axis=-1)
        xf = x.reshape(N, D)
        h = jax.nn.gelu(jnp.einsum('nd,edf->enf', xf, W1) + b1[:, None, :], approximate=False)
        y = jnp.einsum('enf,efd->end', h, W2) + b2[:, None, :]
        w_dense = jnp.zeros((N, E), x.dtype).at[jnp.arange(N)[:, None], top_i].add(top_w)
        out = jnp.einsum('ne,end->nd', w_dense, y).reshape(B, S, D)
        out = _layer_norm(out + x, gamma, beta)
        return out

    def _gn(v, G=32, eps=1e-5):
        B_, H_, W_, C_ = v.shape
        g = v.reshape(B_, H_, W_, G, C_ // G)
        m = jnp.mean(g, axis=(1, 2, 4), keepdims=True)
        s = jnp.var(g, axis=(1, 2, 4), keepdims=True)
        return ((g - m) / jnp.sqrt(s + eps)).reshape(v.shape)

    def _ln_c(v, eps=1e-6):
        m = jnp.mean(v, axis=-1, keepdims=True)
        s = jnp.var(v, axis=-1, keepdims=True)
        return (v - m) / jnp.sqrt(s + eps)

    def _ln_t(v, eps=1e-5):
        m = jnp.mean(v, axis=-1, keepdims=True)
        s = jnp.var(v, axis=-1, keepdims=True)
        return (v - m) / jnp.sqrt(s + eps)

    def _to_tokens(v):
        B_, H_, W_, C_ = v.shape
        return v.reshape(B_, H_ * W_, C_)
    def _from_tokens(t, like):
        return t.reshape(like.shape)

    x = x + _L0_conv_ref(_gn(x), L0_conv_conv_w, L0_conv_conv_b, L0_conv_qkv_w, L0_conv_qkv_b, L0_conv_attn_w, L0_conv_attn_b, L0_conv_key_rel_w, L0_conv_key_rel_h)
    t = _to_tokens(x)
    t = t + _L1_attn_ref(_ln_t(t), L1_attn_W_q, L1_attn_W_k, L1_attn_W_v, L1_attn_W_o, L1_attn_b_o)
    t = t + _L1_ffn_ref(_ln_t(t), L1_ffn_Wr, L1_ffn_br, L1_ffn_W1, L1_ffn_b1, L1_ffn_W2, L1_ffn_b2, L1_ffn_gamma, L1_ffn_beta)
    x = _from_tokens(t, x)
    return x


_drawn_inputs = setup_inputs


def setup_inputs(seed=0):
    import zlib

    import numpy as np

    out = dict(_drawn_inputs(seed))
    spreads = {'L0_conv_conv_b': (0.0, 0.1),
     'L0_conv_qkv_b': (0.0, 0.1),
     'L0_conv_attn_b': (0.0, 0.1),
     'L1_attn_b_o': (0.0, 0.1),
     'L1_ffn_br': (0.0, 0.1),
     'L1_ffn_b1': (0.0, 0.562),
     'L1_ffn_b2': (0.0, 0.434),
     'L1_ffn_gamma': (1.0, 0.2),
     'L1_ffn_beta': (0.0, 0.274)}
    factors = {}
    for name, (base, spread) in spreads.items():
        noise = np.random.default_rng([zlib.crc32(name.encode()), seed]).standard_normal(out[name].shape)
        drawn = base * np.exp(spread * noise) if base else spread * noise
        out[name] = jnp.asarray(drawn.astype(out[name].dtype))
    for name, factor in factors.items():
        out[name] = (out[name] * factor).astype(out[name].dtype)
    return out
```

```python
import concourse.bass as bass
from concourse import mybir
from contextlib import ExitStack

f32 = mybir.dt.float32
f32r = mybir.dt.float32r
ALU = mybir.AluOpType
ACT = mybir.ActivationFunctionType
AX = mybir.AxisListType

P = 128
B, H, W, C = 8, 32, 32, 256
TOK = H * W
TT = TOK // P
KC = C // P
NH, DH = 8, 8
DK = NH * DH
CONV_OUT = C - DK
TAPS = 9
HP, WP = H + 2, W + 2
HALF = TOK // 2
GROUPS = 2
HG = NH // GROUPS
REL = 2 * W - 1
GN_SIZE = 8
U = 128
E, F, TOPK = 8, 512, 2
FC = F // P


def bits(ap):
    return ap.bitcast(f32)


def make_identity(nc, pool, ident, made):
    nc.gpsimd.memset(ident, 0.0)
    pool.drain()
    nc.gpsimd.affine_select(out=ident, in_=ident, compare_op=ALU.not_equal, fill=1.0, base=0,
                            pattern=[[-1, P]], channel_multiplier=1).then_inc(made, 1)


def newton(nc, dve, rstd, var, tmp):
    nc.vector.tensor_tensor(tmp, rstd, rstd, ALU.mult)
    dve.drain()
    nc.vector.tensor_tensor(tmp, tmp, var, ALU.mult)
    dve.drain()
    nc.vector.tensor_scalar(tmp, tmp, -0.5, 1.5, ALU.mult, ALU.add)
    dve.drain()
    nc.vector.tensor_tensor(rstd, rstd, tmp, ALU.mult)
    dve.drain()


def conv_phase(nc, x, conv_w, conv_b, qkv_w, qkv_b, rel_w, rel_h, q_all, bd_hi, bd_lo, mixT_d, kq_d, va_d):
    with ExitStack() as ctx:
        sb = lambda name, shape, dt=f32: ctx.enter_context(nc.sbuf_tensor(name, shape, dt))
        sem = lambda name: ctx.enter_context(nc.semaphore(name))
        ident = sb("c_ident", [P, P])
        gavg = sb("c_gavg", [P, P])
        fold = sb("c_fold", [P, DK])
        w_st = sb("c_w_st", [P, KC, TAPS, CONV_OUT])
        w0_hi = sb("c_w0_hi", [P, KC, TAPS, P], f32r)
        w0_lo = sb("c_w0_lo", [P, KC, TAPS, P], f32r)
        w1_hl = sb("c_w1_hl", [P, KC, TAPS, P], f32r)
        q_st = sb("c_q_st", [P, KC, 3 * DK])
        wkq_hi = sb("c_wkq_hi", [P, KC, P], f32r)
        wkq_lo = sb("c_wkq_lo", [P, KC, P], f32r)
        wv_hl = sb("c_wv_hl", [P, KC, P], f32r)
        cb0, cb1 = sb("c_cb0", [P, 1]), sb("c_cb1", [DK, 1])
        kqb, kqs = sb("c_kqb", [P, 1]), sb("c_kqs", [P, 1])
        vb = sb("c_vb", [P, TT, DK])
        krT = sb("c_krT", [DH, 2, REL])
        kr_rows = sb("c_kr_rows", [P, 2, REL])
        own = sb("c_own", [P, 2, GROUPS, HG])
        bd = sb("c_bd", [P, REL, HG])
        xtok = sb("c_xtok", [P, TT, C])
        xT = sb("c_xT", [P, KC, TOK])
        y32 = sb("c_y32", [P, KC, TOK])
        y_hi = [sb(f"c_y_hi{i}", [P, KC, HP, WP], f32r) for i in range(2)]
        y_lo = [sb(f"c_y_lo{i}", [P, KC, HP, WP], f32r) for i in range(2)]
        st6 = sb("c_st6", [P, KC, 2, 6])
        cms = sb("c_cms", [P, 2, KC])
        cm2 = sb("c_cm2", [P, KC, 2])
        gms = sb("c_gms", [P, 2, KC])
        dev = sb("c_dev", [P, KC])
        gvar = sb("c_gvar", [P, KC])
        sd = sb("c_sd", [P, KC])
        rstd = sb("c_rstd", [P, KC])
        tmp = sb("c_tmp", [P, KC])
        cst = sb("c_cst", [P, KC, TOK])
        c1lo = sb("c_c1lo", [DK, 2, HALF])
        kq32 = sb("c_kq32", [P, TOK])
        kq_hi, kq_lo = sb("c_kq_hi", [P, TOK], f32r), sb("c_kq_lo", [P, TOK], f32r)
        vT = sb("c_vT", [P, TOK])
        va = sb("c_va", [P, TT, NH, 32])
        acc = [ctx.enter_context(nc.psum_tensor(f"c_acc{i}", [P, HALF], f32)) for i in range(4)]
        wide = [ctx.enter_context(nc.psum_tensor(f"c_wide{i}", [P, TOK], f32)) for i in range(2)]
        w_loaded, w_split, consts = sem("c_w_loaded"), sem("c_w_split"), sem("c_consts")
        kr_loaded, rows_loaded, masks = sem("c_kr_loaded"), sem("c_rows_loaded"), sem("c_masks")
        x_loaded, x_turned, xT_ready = sem("c_x_loaded"), sem("c_x_turned"), sem("c_xT_ready")
        stats_ready, gmean_ready, dev_ready, gdev_ready = sem("c_stats"), sem("c_gmean"), sem("c_dev_s"), sem("c_gdev")
        gvar_ready, sd_ready = sem("c_gvar_s"), sem("c_sd_s")
        y32_ready, yhi_ready, y_ready = sem("c_y32_s"), sem("c_yhi_s"), sem("c_y_s")
        unit_done = sem("c_unit_done")
        unit_read = [sem(f"c_unit_read{i}") for i in range(4)]
        c1lo_ready, cst_stored = sem("c_c1lo_s"), sem("c_cst_stored")
        kqhi_ready, kq_ready, kq_stored = sem("c_kqhi"), sem("c_kq_s"), sem("c_kq_stored")
        va_turned, va_ready, va_stored = sem("c_va_turned"), sem("c_va_s"), sem("c_va_stored")
        q_ready = sem("c_q_s")

        UNITS = [("kq", 0), ("conv0", 0), ("kq", 1), ("conv0", 1), ("v", 0), ("conv1", 0), ("v", 1), ("conv1", 1)]
        NU = len(UNITS)
        done = lambda b, what, t: b * NU + UNITS.index((what, t)) + 1
        bank = lambda what, t: UNITS.index((what, t)) % 4
        KQ_DMAS = 4 * GROUPS
        x_v = x.rearrange("b h w c -> b (h w) c").rearrange("b (t p) c -> b p t c", p=P)

        def image_rows(ap):
            return ap.rearrange("p (y x) -> p y x", x=W)

        def all_images(eng, image):
            with eng.Fori(0, B - 2, 2) as b:
                image(b, 0, True)
                image(b + 1, 1, True)
            image(B - 2, 0, True)
            image(B - 1, 1, False)

        with nc.Block() as block:
            @block.sync
            def _(sp):
                sp.dma_start(xtok[:], x_v[0]).then_inc(x_loaded, 16)
                for k in range(KC):
                    sp.dma_start(w_st[:, k], conv_w.rearrange("a b (k p) o -> p k (a b) o", p=P)[:, k]).then_inc(w_loaded, 16)
                sp.dma_start(q_st[:], qkv_w.rearrange("(k p) o -> p k o", p=P)).then_inc(w_loaded, 16)
                sp.dma_start(cb0[:], conv_b[0:P].rearrange("(p a) -> p a", a=1)).then_inc(w_loaded, 16)
                sp.dma_start(cb1[:], conv_b[P:CONV_OUT].rearrange("(p a) -> p a", a=1)).then_inc(w_loaded, 16)
                sp.dma_start(kqb[:], qkv_b[0:P].rearrange("(p a) -> p a", a=1)).then_inc(w_loaded, 16)
                sp.dma_start(vb[:], bass.AP(tensor=qkv_b.tensor, offset=P, ap=[[0, P], [0, TT], [1, DK]])).then_inc(w_loaded, 16)
                with nc.allow_non_contiguous_dma(reason="two small tables, transposed once"):
                    sp.dma_start(krT[:, 0, :], rel_w.rearrange("m d -> d m")).then_inc(kr_loaded, 16)
                    sp.dma_start(krT[:, 1, :], rel_h.rearrange("m d -> d m")).then_inc(kr_loaded, 16)
                sp.wait_ge(kr_loaded, 32)
                for h in range(P // DH):
                    sp.dma_start(kr_rows[DH * h:DH * (h + 1)], krT[:]).then_inc(rows_loaded, 16)
                sp.sem_inc(kq_stored, KQ_DMAS * 16)
                sp.sem_inc(cst_stored, 32)
                sp.sem_inc(va_stored, 16 * GROUPS)

                def load(p):
                    sp.wait_ge(x_turned, p * KC)
                    sp.dma_start(xtok[:], x_v[p]).then_inc(x_loaded, 16)

                def image(b, ahead):
                    sp.wait_ge(kq_ready, b + 1)
                    for part, buf in enumerate((kq_hi, kq_lo)):
                        for kq in range(2):
                            for g in range(GROUPS):
                                rows = kq * DK + g * HG * DH
                                sp.dma_start(kq_d[b, g, part, kq], bits(buf[rows:rows + HG * DH])).then_inc(kq_stored, 16)
                    if ahead:
                        load(b + 2)
                    sp.wait_ge(unit_read[bank("conv1", 1)], b * 2 + 3)
                    sp.dma_start(mixT_d[b, 0], cst[:, 0, :]).then_inc(cst_stored, 16)
                    sp.dma_start(mixT_d[b, 1, 0:CONV_OUT - P], cst[0:CONV_OUT - P, 1, :]).then_inc(cst_stored, 16)
                    sp.wait_ge(va_ready, b + 2)
                    for g in range(GROUPS):
                        sp.dma_start(va_d[b, g].rearrange("p (t c) -> p t c", t=TT),
                                     va[:, :, HG * g:HG * (g + 1), :].rearrange("p t h c -> p t (h c)")).then_inc(va_stored, 16)

                load(1)
                with sp.Fori(0, B - 2) as b:
                    image(b, True)
                image(B - 2, False)
                image(B - 1, False)
                sp.wait_ge(kq_stored, KQ_DMAS * 16 * (B + 1))
                sp.wait_ge(cst_stored, 32 * (B + 1))
                sp.wait_ge(va_stored, 16 * GROUPS * (B + 1))

            @block.gpsimd
            def _(pool):
                nc.gpsimd.memset(gavg[:], 1.0 / GN_SIZE)
                nc.gpsimd.memset(fold[:], 0.0)
                nc.gpsimd.memset(va[:], 0.0)
                make_identity(nc, pool, ident[:], consts)
                g3 = gavg[:].rearrange("p (g c) -> p g c", c=GN_SIZE)
                for base, sign in ((0, 1), (GN_SIZE - 1, -1)):
                    nc.gpsimd.affine_select(out=g3, in_=g3, compare_op=ALU.is_ge, fill=0.0, base=base,
                                            pattern=[[-sign * GN_SIZE, P // GN_SIZE], [0, GN_SIZE]],
                                            channel_multiplier=sign)
                    nc.gpsimd.affine_select(out=fold[:], in_=fold[:], compare_op=ALU.not_equal, fill=1.0,
                                            base=-DK if base else 0, pattern=[[-1, DK]], channel_multiplier=1)
                    pool.drain()
                nc.gpsimd.memset(va[:, :, :, DH:DH + 1], 1.0).then_inc(consts, 1)
                nc.gpsimd.memset(own[:], 1.0)
                pool.drain()
                for base, sign in ((0, 1), (DH - 1, -1)):
                    nc.gpsimd.affine_select(out=own[:], in_=own[:], compare_op=ALU.is_ge, fill=0.0, base=base,
                                            pattern=[[-sign * DK, 2], [-sign * HG * DH, GROUPS], [-sign * DH, HG]],
                                            channel_multiplier=sign)
                    pool.drain()
                nc.gpsimd.tensor_tensor(own[:, 0], own[:, 0], own[:, 1], ALU.add).then_inc(masks, 1)

            @block.scalar
            def _(act):
                def prep(p, first=False):
                    for c in range(KC):
                        act.wait_ge(x_turned, p * KC + c + 1)
                        if not first:
                            act.wait_ge(y32_ready, p * KC)
                        nc.scalar.activation(xT[:, c, :], wide[c][:], ACT.Copy).then_inc(xT_ready, 1)

                def round_y(p, s, first=False):
                    for c in range(KC):
                        act.wait_ge(y32_ready, p * KC + c + 1)
                        if not first:
                            act.wait_ge(va_turned, p)
                        nc.scalar.activation(y_hi[s][:, c, 1:H + 1, 1:W + 1], image_rows(y32[:, c, :]),
                                             ACT.Copy).then_inc(yhi_ready, 1)

                def spread(p):
                    act.wait_ge(gvar_ready, p + 1)
                    nc.scalar.activation(sd[:], gvar[:], ACT.Sqrt).then_inc(sd_ready, 1)

                def image(b, s, prefetch):
                    if prefetch:
                        prep(b + 1)
                    act.wait_ge(unit_read[bank("kq", 1)], b * 2 + 2)
                    act.wait_ge(kq_stored, (b + 1) * (KQ_DMAS * 16))
                    nc.scalar.activation(kq_hi[:], kq32[:], ACT.Copy).then_inc(kqhi_ready, 1)
                    nc.scalar.activation(q_all[DK:P, b, :], kq32[DK:P, :], ACT.Copy)
                    act.wait_ge(kq_ready, b + 1)
                    nc.scalar.activation(q_all[0:DK, b, :], bits(kq_lo[DK:P, :]), ACT.Copy).then_inc(q_ready, 1)
                    if prefetch:
                        spread(b + 1)
                    for t in range(2):
                        act.wait_ge(unit_done, done(b, "v", t))
                        nc.scalar.activation(vT[:, t * HALF:(t + 1) * HALF], acc[bank("v", t)][:], ACT.Copy
                                             ).then_inc(unit_read[bank("v", t)], 1)
                        if t == 0 and prefetch:
                            round_y(b + 1, 1 - s)
                        act.wait_ge(unit_done, done(b, "conv1", t))
                        nc.scalar.activation(c1lo[:, t, :], acc[bank("conv1", t)][DK:P, :], ACT.Copy).then_inc(c1lo_ready, 1)

                prep(0, first=True)
                spread(0)
                round_y(0, 0, first=True)
                all_images(act, image)

            @block.vector
            def _(dve):
                def prep_stats(p):
                    for c in range(KC):
                        dve.wait_ge(xT_ready, p * KC + c + 1)
                        for s in range(2):
                            nc.vector.bn_stats(st6[:, c, s, :], xT[:, c, s * HALF:(s + 1) * HALF])
                    dve.drain()
                    for c in range(KC):
                        nc.vector.bn_aggr(cm2[:, c, :], st6[:, c].rearrange("p s d -> p (s d)"))
                    dve.drain()
                    nc.vector.tensor_copy(cms[:].rearrange("p s c -> p c s"), cm2[:]).then_inc(stats_ready, 1)

                def prep_mean(p):
                    dve.wait_ge(gmean_ready, p + 1)
                    nc.vector.tensor_copy(gms[:].rearrange("p s c -> p (s c)"), wide[0][:, 0:2 * KC])
                    dve.drain()
                    nc.vector.tensor_tensor(dev[:], cms[:, 0, :], gms[:, 0, :], ALU.subtract)
                    dve.drain()
                    nc.vector.tensor_tensor(dev[:], dev[:], dev[:], ALU.mult).then_inc(dev_ready, 1)

                def prep_var(p):
                    dve.wait_ge(gdev_ready, p + 1)
                    nc.vector.scalar_tensor_tensor(gvar[:], wide[1][:, 0:KC], 1e-5, gms[:, 1, :], ALU.add, ALU.add
                                                   ).then_inc(gvar_ready, 1)

                def prep_y(p):
                    dve.wait_ge(sd_ready, p + 1)
                    nc.vector.reciprocal(rstd[:], sd[:])
                    dve.drain()
                    newton(nc, dve, rstd[:], gvar[:], tmp[:])
                    for c in range(KC):
                        nc.vector.tensor_scalar(y32[:, c, :], xT[:, c, :], gms[:, 0, c:c + 1], rstd[:, c:c + 1],
                                                ALU.subtract, ALU.mult).then_inc(y32_ready, 1)

                def low_y(p, s):
                    for c in range(KC):
                        dve.wait_ge(yhi_ready, p * KC + c + 1)
                        nc.vector.tensor_tensor(y_lo[s][:, c, 1:H + 1, 1:W + 1], image_rows(y32[:, c, :]),
                                                bits(y_hi[s][:, c, 1:H + 1, 1:W + 1]), ALU.subtract).then_inc(y_ready, 1)

                def relative_keys():
                    dve.wait_ge(masks, 1)
                    dve.wait_ge(rows_loaded, 16 * (P // DH))
                    for wh in range(2):
                        for g in range(GROUPS):
                            for h in range(HG):
                                nc.vector.tensor_scalar(bd[:, :, h], kr_rows[:, wh, :], own[:, 0, g, h:h + 1], None, ALU.mult)
                            dve.drain()
                            flat = bd[:].rearrange("p m h -> p (m h)")
                            nc.vector.tensor_copy(bd_hi[:, wh, g], flat)
                            dve.drain()
                            nc.vector.tensor_tensor(bd_lo[:, wh, g], flat, bits(bd_hi[:, wh, g]), ALU.subtract)
                            dve.drain()

                def kq(b, t):
                    dve.wait_ge(unit_done, done(b, "kq", t))
                    if t == 0:
                        dve.wait_ge(q_ready, b + 1)
                    nc.vector.tensor_scalar(kq32[:, t * HALF:(t + 1) * HALF], acc[bank("kq", t)][:], kqb[:], kqs[:],
                                            ALU.add, ALU.mult).then_inc(unit_read[bank("kq", t)], 1)

                def conv0(b, t):
                    dve.wait_ge(unit_done, done(b, "conv0", t))
                    if t == 0:
                        dve.wait_ge(cst_stored, b * 32 + 32)
                    nc.vector.tensor_scalar(cst[:, 0, t * HALF:(t + 1) * HALF], acc[bank("conv0", t)][:], cb0[:], None,
                                            ALU.add).then_inc(unit_read[bank("conv0", t)], 1)

                def conv1(b, t):
                    dve.wait_ge(c1lo_ready, b * 2 + t + 1)
                    nc.vector.scalar_tensor_tensor(cst[0:DK, 1, t * HALF:(t + 1) * HALF], acc[bank("conv1", t)][0:DK, :],
                                                   cb1[:], c1lo[:, t, :], ALU.add, ALU.add
                                                   ).then_inc(unit_read[bank("conv1", t)], 1)

                def image(b, s, prefetch):
                    kq(b, 0)
                    if prefetch:
                        prep_stats(b + 1)
                    conv0(b, 0)
                    if prefetch:
                        prep_mean(b + 1)
                    kq(b, 1)
                    dve.wait_ge(kqhi_ready, b + 1)
                    nc.vector.tensor_tensor(kq_lo[:], kq32[:], bits(kq_hi[:]), ALU.subtract).then_inc(kq_ready, 1)
                    conv0(b, 1)
                    if prefetch:
                        prep_var(b + 1)
                        prep_y(b + 1)
                        low_y(b + 1, 1 - s)
                    conv1(b, 0)
                    conv1(b, 1)
                    dve.wait_ge(va_turned, b + 2)
                    dve.wait_ge(va_stored, (b + 1) * (16 * GROUPS))
                    nc.vector.tensor_tensor(va[:, :, :, 0:DH],
                                            wide[1][:, 0:TT * DK].rearrange("p (t h d) -> p t h d", h=NH, d=DH),
                                            vb[:].rearrange("p t (h d) -> p t h d", d=DH), ALU.add).then_inc(va_ready, 1)

                nc.vector.memset(kqs[0:DK], 1.0)
                nc.vector.memset(kqs[DK:P], DH ** -0.5)
                for buf in y_hi + y_lo:
                    nc.vector.memset(bits(buf[:]), 0.0)
                dve.sem_inc(va_ready, 1)
                dve.sem_inc(q_ready, 1)
                dve.wait_ge(w_loaded, 16 * (KC + 5))
                dve.wait_ge(consts, 2)
                for src, hi, lo in ((w_st[:, :, :, 0:P], w0_hi[:], w0_lo[:]),
                                    (w_st[:, :, :, P:CONV_OUT], w1_hl[:, :, :, 0:DK], w1_hl[:, :, :, DK:P]),
                                    (q_st[:, :, 0:P], wkq_hi[:], wkq_lo[:]),
                                    (q_st[:, :, P:3 * DK], wv_hl[:, :, 0:DK], wv_hl[:, :, DK:P])):
                    for k in range(KC):
                        nc.vector.tensor_copy(hi[:, k], src[:, k])
                    dve.drain()
                    for k in range(KC):
                        last = nc.vector.tensor_tensor(lo[:, k], src[:, k], bits(hi[:, k]), ALU.subtract)
                    last.then_inc(w_split, 1)
                prep_stats(0)
                prep_mean(0)
                prep_var(0)
                prep_y(0)
                low_y(0, 0)
                relative_keys()
                all_images(dve, image)

            @block.tensor
            def _(pe):
                def turn(p, first=False):
                    pe.wait_ge(x_loaded, p * 16 + 16)
                    for c in range(KC):
                        if c == 1 and not first:
                            pe.wait_ge(va_ready, p)
                        for t in range(TT):
                            m = nc.tensor.transpose(wide[c][:, t * P:(t + 1) * P], xtok[:, t, c * P:(c + 1) * P], ident[:])
                        m.then_inc(x_turned, 1)

                def group_mean(p):
                    pe.wait_ge(stats_ready, p + 1)
                    nc.tensor.matmul(wide[0][:, 0:2 * KC], gavg[:], cms[:].rearrange("p s c -> p (s c)"),
                                     start=True, stop=True).then_inc(gmean_ready, 1)

                def group_dev(p):
                    pe.wait_ge(dev_ready, p + 1)
                    nc.tensor.matmul(wide[1][:, 0:KC], gavg[:], dev[:], start=True, stop=True).then_inc(gdev_ready, 1)

                all_taps = [(t // 3, t % 3, t) for t in range(TAPS)]
                centre = [(1, 1, None)]

                HI, LO = y_hi, y_lo
                parts = {"kq": (((wkq_hi, HI), (wkq_hi, LO), (wkq_lo, HI)), centre),
                         "conv0": (((w0_hi, HI), (w0_hi, LO), (w0_lo, HI)), all_taps),
                         "v": (((wv_hl, HI), (wv_hl, LO)), centre),
                         "conv1": (((w1_hl, HI), (w1_hl, LO)), all_taps)}

                def unit(b, s, what, t):
                    pairs, taps = parts[what]
                    u = UNITS.index((what, t))
                    pe.wait_ge(unit_read[u % 4], b * 2 + u // 4 + 1)
                    n, total = 0, len(pairs) * KC * len(taps)
                    rows = t * (H // 2)
                    for k in range(KC):
                        for dy, dx, tap in taps:
                            for wt, y in pairs:
                                m = nc.tensor.matmul(image_rows(acc[u % 4][:]), wt[:, k, :] if tap is None else wt[:, k, tap, :],
                                                     y[s][:, k, rows + dy:rows + dy + H // 2, dx:dx + W],
                                                     start=n == 0, stop=n == total - 1)
                                n += 1
                    m.then_inc(unit_done, 1)

                def image(b, s, prefetch):
                    pe.wait_ge(y_ready, b * KC + KC)
                    unit(b, s, "kq", 0)
                    if prefetch:
                        turn(b + 1)
                    unit(b, s, "conv0", 0)
                    if prefetch:
                        group_mean(b + 1)
                    unit(b, s, "kq", 1)
                    unit(b, s, "conv0", 1)
                    if prefetch:
                        group_dev(b + 1)
                    unit(b, s, "v", 0)
                    unit(b, s, "conv1", 0)
                    unit(b, s, "v", 1)
                    unit(b, s, "conv1", 1)
                    pe.wait_ge(unit_read[bank("v", 1)], b * 2 + 3)
                    if prefetch:
                        pe.wait_ge(gvar_ready, b + 2)
                    for t in range(TT):
                        m = nc.tensor.matmul(wide[1][:, t * DK:(t + 1) * DK], vT[:, t * P:(t + 1) * P], fold[:],
                                             start=True, stop=True)
                    m.then_inc(va_turned, 1)

                for free in unit_read:
                    pe.sem_inc(free, 1)
                pe.sem_inc(va_turned, 1)
                pe.wait_ge(consts, 2)
                turn(0, first=True)
                group_mean(0)
                group_dev(0)
                pe.wait_ge(w_split, 4)
                all_images(pe, image)


def relative_phase(nc, q_all, bd_hi, bd_lo, rel_d):
    with ExitStack() as ctx:
        sb = lambda name, shape, dt=f32: ctx.enter_context(nc.sbuf_tensor(name, shape, dt))
        sem = lambda name: ctx.enter_context(nc.semaphore(name))
        hl = [sb(f"r_hl{i}", [P, 2, B, TOK], f32r) for i in range(2)]
        ps = [ctx.enter_context(nc.psum_tensor(f"r_ps{i}", [P, 2, B, W], f32)) for i in range(8)]
        pair_done, hi_ready, lo_ready = sem("r_pair_done"), sem("r_hi_s"), sem("r_lo_s")
        stored = [sem(f"r_stored{i}") for i in range(2)]
        PAIRS = W // 2
        RELS = [(wh, g) for wh in range(2) for g in range(GROUPS)]

        def target(buf, wh, i):
            if wh == 0:
                return buf.rearrange("p b (y x) -> p x b y", x=W)[:, i:i + 2]
            return buf.rearrange("p b (y x) -> p y b x", x=W)[:, i:i + 2]

        with nc.Block() as block:
            @block.sync
            def _(sp):
                for r, (wh, g) in enumerate(RELS):
                    sp.wait_ge(lo_ready, PAIRS * (r + 1))
                    for part in range(2):
                        sp.dma_start(rel_d[:, g, wh, part].rearrange("b p n -> p b n"), bits(hl[r % 2][:, part])
                                     ).then_inc(stored[r % 2], 16)
                for s in stored:
                    sp.wait_ge(s, 64)

            @block.scalar
            def _(act):
                for r, (wh, g) in enumerate(RELS):
                    for n in range(PAIRS):
                        act.wait_ge(pair_done, r * PAIRS + n + 1)
                        if r >= 2 and n == 0:
                            act.wait_ge(stored[r % 2], 32)
                        nc.scalar.activation(target(hl[r % 2][:, 0], wh, 2 * n), ps[n % 8][:], ACT.Copy).then_inc(hi_ready, 1)

            @block.vector
            def _(dve):
                for r, (wh, g) in enumerate(RELS):
                    for n in range(PAIRS):
                        dve.wait_ge(hi_ready, r * PAIRS + n + 1)
                        nc.vector.tensor_tensor(target(hl[r % 2][:, 1], wh, 2 * n), ps[n % 8][:],
                                                target(bits(hl[r % 2][:, 0]), wh, 2 * n), ALU.subtract).then_inc(lo_ready, 1)

            @block.tensor
            def _(pe):
                for r, (wh, g) in enumerate(RELS):
                    for n in range(PAIRS):
                        if r * PAIRS + n >= 8:
                            pe.wait_ge(lo_ready, r * PAIRS + n - 7)
                        for j in range(2):
                            i = 2 * n + j
                            q = q_all[:, :, i::W] if wh == 0 else q_all[:, :, i * W:(i + 1) * W]
                            for k, bdp in enumerate((bd_hi, bd_lo)):
                                m = nc.tensor.matmul(ps[n % 8][:, j], bdp[:, wh, g, HG * (W - 1 - i):HG * (2 * W - 1 - i)], q,
                                                     start=k == 0, stop=k == 1, skip_group_check=True)
                        m.then_inc(pair_done, 1)


def front(nc, x, conv_w, conv_b, qkv_w, qkv_b, rel_w, rel_h, mixT_d, kq_d, rel_d, va_d):
    with (nc.sbuf_tensor("q_all", [P, B, TOK], f32r) as q_all,
          nc.sbuf_tensor("bd_hi", [P, 2, GROUPS, REL * HG], f32r) as bd_hi,
          nc.sbuf_tensor("bd_lo", [P, 2, GROUPS, REL * HG], f32r) as bd_lo):
        conv_phase(nc, x, conv_w, conv_b, qkv_w, qkv_b, rel_w, rel_h, q_all, bd_hi, bd_lo, mixT_d, kq_d, va_d)
        relative_phase(nc, q_all, bd_hi, bd_lo, rel_d)


def attention_phase(nc, kq_d, rel_d, va_d, att_d):
    NG = B * GROUPS
    BUFS = 3
    ROW_W, ROW_H = (0, W), (2 * W, 2 * W + H // 2)
    ROW_Q = 2 * W + H
    ROW_M = ROW_Q + 3 * DH
    with ExitStack() as ctx:
        sb = lambda name, shape, dt=f32: ctx.enter_context(nc.sbuf_tensor(name, shape, dt))
        sem = lambda name: ctx.enter_context(nc.semaphore(name))
        ident = sb("a_ident", [P, P])
        ones_hot = sb("a_ones_hot", [P, TOK])
        qf = [sb(f"a_qf{i}", [P, HG, 2, TOK], f32r) for i in range(BUFS)]
        kf = [sb(f"a_kf{i}", [P, HG, TOK], f32r) for i in range(BUFS)]
        va = [sb(f"a_va{i}", [P, TT, HG, 32]) for i in range(BUFS)]
        probs = sb("a_probs", [P, 2, HG, TOK])
        pmax = sb("a_pmax", [P, 2, TT, 2])
        nmax = sb("a_nmax", [P, HG, TT])
        mrow = sb("a_mrow", [TT, HG, P], f32r)
        out = sb("a_out", [P, TOK])
        st = [ctx.enter_context(nc.psum_tensor(f"a_st{i}", [P, TOK], f32)) for i in range(2)]
        sm = [ctx.enter_context(nc.psum_tensor(f"a_sm{i}", [P, HALF], f32)) for i in range(2)]
        pv = ctx.enter_context(nc.psum_tensor("a_pv", [P, TOK], f32))
        made, built = sem("a_made"), sem("a_built")
        loaded = [sem(f"a_loaded{i}") for i in range(BUFS)]
        max_loaded = [sem(f"a_max_loaded{h}") for h in range(HG)]
        sm_done, sm_read, nmax_ready = sem("a_sm_done"), sem("a_sm_read"), sem("a_nmax_s")
        st_done, exp_done, pv_done = sem("a_st_done"), sem("a_exp_done"), sem("a_pv_done")
        out_ready, out_stored = sem("a_out_s"), sem("a_out_stored")
        LOADS = 4 + 4 + 6 + 3 + 1

        LATE = 4
        units = []
        for h in range(HG):
            for n in range(2 * TT):
                units.append(("logits", h, n))
                if h and n == LATE - 1:
                    units.append(("turn", h - 1, 0))
        units.append(("turn", HG - 1, 0))
        NU = len(units)
        turn_at = {h: units.index(("turn", h, 0)) for h in range(HG)}
        STEPS = TT * HG

        def all_groups(eng, period):
            last = NG - 1
            full = (last - 1) // BUFS - 1
            with eng.Fori(0, full * BUFS, BUFS) as n:
                for j in range(BUFS):
                    period(n + j, j, True, True)
            for n in range(full * BUFS, NG):
                period(n, n % BUFS, n < last, n + 2 < NG)

        with nc.Block() as block:
            @block.sync
            def _(sp):
                def load(n, j):
                    if not (isinstance(n, int) and n < BUFS):
                        sp.wait_ge(pv_done, n * TT - 2 * TT + 2)
                    kq_g = kq_d.rearrange("b g a k (h d) n -> (b g) a k d h n", d=DH)[n]
                    rel_g = rel_d.rearrange("b g w a (j h) n -> (b g) w a j h n", h=HG)[n]
                    va_g = va_d.rearrange("b g p c -> (b g) p c")[n]
                    for part in range(2):
                        for half in range(2):
                            dst = bits(qf[j][:])
                            r = ROW_W[part]
                            sp.dma_start(dst[r:r + W, :, half, :], rel_g[0, part]).then_inc(loaded[j], 16)
                            r = ROW_H[part]
                            sp.dma_start(dst[r:r + H // 2, :, half, :], rel_g[1, part, half * H // 2:(half + 1) * H // 2]
                                         ).then_inc(loaded[j], 16)
                    for row, (qpart, kpart) in enumerate(((0, 0), (0, 1), (1, 0))):
                        r = ROW_Q + DH * row
                        for half in range(2):
                            sp.dma_start(bits(qf[j][:])[r:r + DH, :, half, :], kq_g[qpart, 1]).then_inc(loaded[j], 16)
                        sp.dma_start(bits(kf[j][:])[r:r + DH], kq_g[kpart, 0]).then_inc(loaded[j], 16)
                    sp.dma_start(va[j][:].rearrange("p t h c -> p (t h c)"), va_g).then_inc(loaded[j], 16)

                def maxima(n, j):
                    for h in range(HG):
                        for half in range(2):
                            if half == 0:
                                sp.wait_ge(sm_read, n * NU + turn_at[h] + 1)
                            sp.dma_start(bits(qf[j][:])[ROW_M:ROW_M + 1, h, half, :].rearrange("a (t p) -> a t p", p=P),
                                         bits(mrow[:, h, :])).then_inc(max_loaded[h], 16)

                def period(n, j, more, ahead):
                    if ahead:
                        load(n + 2, (j + 2) % BUFS)
                    if more:
                        maxima(n + 1, (j + 1) % BUFS)
                    sp.wait_ge(out_ready, n + 2)
                    sp.dma_start(att_d.rearrange("b g p n -> (b g) p n")[n], out[:]).then_inc(out_stored, 16)

                sp.sem_inc(out_stored, 16)
                sp.wait_ge(built, 1)
                load(0, 0)
                load(1, 1)
                maxima(0, 0)
                all_groups(sp, period)
                sp.wait_ge(out_stored, 16 * (NG + 1))

            @block.gpsimd
            def _(pool):
                make_identity(nc, pool, ident[:], made)
                nc.gpsimd.memset(ones_hot[:], 0.0)
                pool.drain()
                xs, ys = [[0, H], [-1, W]], [[0, 2], [-1, H // 2], [0, W]]
                for base, pattern in ((ROW_W[0], xs), (ROW_W[1], xs), (ROW_H[0], ys), (ROW_H[1], ys), (ROW_M, [[0, TOK]])):
                    nc.gpsimd.affine_select(out=ones_hot[:], in_=ones_hot[:], compare_op=ALU.not_equal, fill=1.0, base=-base,
                                            pattern=pattern, channel_multiplier=1)
                    pool.drain()
                nc.gpsimd.sem_inc(made, 1)

            @block.scalar
            def _(act):
                def period(n, j, more, ahead):
                    for s in range(STEPS):
                        t, h = s // HG, s % HG
                        act.wait_ge(st_done, n * STEPS + s + 1)
                        if h == 0:
                            act.wait_ge(pv_done, n * TT + t + 1)
                        nc.scalar.activation(probs[:, t % 2, h, :], st[s % 2][:], ACT.Exp).then_inc(exp_done, 1)
                    act.wait_ge(pv_done, n * TT + TT + 2)
                    act.wait_ge(out_stored, n * 16 + 16)
                    nc.scalar.activation(out[:], pv[:], ACT.Copy).then_inc(out_ready, 1)

                all_groups(act, period)

            @block.vector
            def _(dve):
                def first_pass(n, first=False):
                    for k, (what, h, u) in enumerate(units):
                        dve.wait_ge(sm_done, n * NU + k + 1)
                        if what == "logits":
                            nc.vector.tensor_reduce(pmax[:, h % 2, u // 2, u % 2:u % 2 + 1], sm[k % 2][:], axis=AX.X, op=ALU.max
                                                    ).then_inc(sm_read, 1)
                            if u == 2 * TT - 1:
                                dve.drain()
                                nc.vector.tensor_reduce(nmax[:, h, :], pmax[:, h % 2], axis=AX.X, op=ALU.max, negate=True
                                                        ).then_inc(nmax_ready, 1)
                        else:
                            if not first:
                                dve.wait_ge(max_loaded[h], n * 32)
                            nc.vector.tensor_copy(mrow[:, h, :], sm[k % 2][0:TT, 0:P]).then_inc(sm_read, 1)

                def period(n, j, more, ahead):
                    if more:
                        first_pass(n + 1)

                dve.wait_ge(made, 2)
                for buf in kf:
                    for h in range(HG):
                        last = nc.vector.tensor_copy(buf[:, h, :], ones_hot[:])
                last.then_inc(built, 1)
                first_pass(0, first=True)
                all_groups(dve, period)

            @block.tensor
            def _(pe):
                def first_pass_unit(n, j, k):
                    what, h, u = units[k]
                    if not (isinstance(n, int) and n == 0 and k < 2):
                        pe.wait_ge(sm_read, n * NU + k - 1)
                    if what == "logits":
                        t, half = u // 2, u % 2
                        nc.tensor.matmul(sm[k % 2][:], qf[j][0:ROW_M, h, half, t * P:(t + 1) * P],
                                         kf[j][0:ROW_M, h, half * HALF:(half + 1) * HALF], start=True, stop=True).then_inc(sm_done, 1)
                    else:
                        pe.wait_ge(nmax_ready, n * HG + h + 1)
                        nc.tensor.transpose(sm[k % 2][0:TT, 0:P], nmax[:, h, :], ident[:]).then_inc(sm_done, 1)

                def weighted(n, j, t, quarter):
                    if quarter == 0:
                        pe.wait_ge(exp_done, n * STEPS + HG * (t + 1) + 2)
                        if t == 0:
                            pe.wait_ge(out_ready, n + 1)
                    cols = slice(quarter * TOK // HG, (quarter + 1) * TOK // HG)
                    for h in range(HG):
                        m = nc.tensor.matmul(pv[32 * h:32 * h + 32, cols], va[j][:, t, h, :], probs[:, t % 2, h, cols],
                                             start=t == 0 and quarter % 2 == 0, stop=t == TT - 1, skip_group_check=True)
                    if quarter == HG - 1:
                        m.then_inc(pv_done, 1)

                def period(n, j, more, ahead):
                    j1 = (j + 1) % BUFS
                    if more:
                        pe.wait_ge(loaded[j1], (n - j + BUFS * ((j + 1) // BUFS + 1)) * (16 * LOADS // BUFS))
                    for s in range(STEPS):
                        t, h = s // HG, s % HG
                        pe.wait_ge(exp_done, n * STEPS + s + 1)
                        if t == 0:
                            pe.wait_ge(max_loaded[h], n * 32 + 32)
                        for half in range(2):
                            cols = slice(half * HALF, (half + 1) * HALF)
                            m = nc.tensor.matmul(st[s % 2][:, cols], kf[j][0:ROW_M + 1, h, t * P:(t + 1) * P],
                                                 qf[j][0:ROW_M + 1, h, 2 * t // TT, cols], start=True, stop=True)
                        m.then_inc(st_done, 1)
                        if more:
                            first_pass_unit(n + 1, j1, 2 * s)
                        if t:
                            weighted(n, j, t - 1, h)
                        if more:
                            first_pass_unit(n + 1, j1, 2 * s + 1)
                    for quarter in range(HG):
                        weighted(n, j, TT - 1, quarter)
                        if more:
                            first_pass_unit(n + 1, j1, 2 * STEPS + quarter)

                pe.sem_inc(exp_done, 2)
                pe.sem_inc(pv_done, 2)
                pe.sem_inc(out_ready, 1)
                pe.wait_ge(made, 1)
                pe.wait_ge(loaded[0], 16 * LOADS)
                for k in range(NU):
                    first_pass_unit(0, 0, k)
                all_groups(pe, period)


def self_attention_phase(nc, x, attn_w, attn_b, w_q, w_k, w_v, w_o, b_o, mixT_d, att_d, rsum_d, t_d, vT_d, vsum_d):
    with ExitStack() as ctx:
        sb = lambda name, shape, dt=f32: ctx.enter_context(nc.sbuf_tensor(name, shape, dt))
        ps = lambda name, n: ctx.enter_context(nc.psum_tensor(name, [P, n], f32))
        sem = lambda name: ctx.enter_context(nc.semaphore(name))
        QT = TT // 2
        ident = sb("b_ident", [P, P])
        wp = sb("b_wp", [P, GROUPS, DK])
        pb = sb("b_pb", [P, 1])
        w_st = sb("b_w_st", [P, KC, 3, U])
        w_hi, w_lo = sb("b_w_hi", [P, KC, 3, U], f32r), sb("b_w_lo", [P, KC, 3, U], f32r)
        wo = sb("b_wo", [P, C])
        bo = sb("b_bo", [P, C])
        rs = sb("b_rs", [P, B, TOK // 16])
        att = [sb(f"b_att{j}", [P, GROUPS, HALF]) for j in range(2)]
        rsb = [sb(f"b_rsb{j}", [P, GROUPS, HALF]) for j in range(2)]
        mixT = sb("b_mixT", [P, KC, TOK])
        xb = [sb(f"b_xb{s}", [P, TT, C]) for s in range(2)]
        st6, mv = sb("b_st6", [P, QT, 6]), sb("b_mv", [P, QT, 2])
        var, rstd, tmp, shift = (sb(f"b_{n}", [P, 2, QT]) for n in ("var", "rstd", "tmp", "shift"))
        u = sb("b_u", [P, QT, C])
        uT_hi, uT_lo = sb("b_uT_hi", [P, KC, TOK], f32r), sb("b_uT_lo", [P, KC, TOK], f32r)
        q_hi = [sb(f"b_q_hi{s}", [P, TOK], f32r) for s in range(2)]
        q_lo = [sb(f"b_q_lo{s}", [P, TOK], f32r) for s in range(2)]
        k_hi = [sb(f"b_k_hi{s}", [P, TOK], f32r) for s in range(2)]
        k_lo = [sb(f"b_k_lo{s}", [P, TOK], f32r) for s in range(2)]
        vT32 = sb("b_vT32", [P, HALF])
        v_sb = [sb(f"b_v{s}", [P, TT, U]) for s in range(2)]
        nmax, ssum, rsum = sb("b_nmax", [P, TT]), sb("b_ssum", [P, TT]), sb("b_rsum", [P, TT])
        probs = [sb(f"b_probs{i}", [P, TOK]) for i in range(2)]
        pT = [sb(f"b_pT{i}", [P, TT, 2 * P]) for i in range(2)]
        oT = [sb(f"b_oT{i}", [P, 2 * P]) for i in range(2)]
        t_sb = [sb(f"b_t{j}", [P, QT, C]) for j in range(2)]
        st6t, mvt = sb("b_st6t", [P, QT, 6]), sb("b_mvt", [P, QT, 2])
        vart, rstdt, tmpt = (sb(f"b_{n}", [P, 2, QT]) for n in ("vart", "rstdt", "tmpt"))
        v2 = sb("b_v2", [P, QT, C])
        v2T = sb("b_v2T", [P, KC, HALF])
        vsum = sb("b_vsum", [P, KC, TT // 2])
        s_ps, pT_ps, o_ps = ps("b_s_ps", TOK), ps("b_pT_ps", TOK), ps("b_o_ps", 2 * P)
        a_ps, b_ps, c_ps = ps("b_a_ps", 2 * C), ps("b_b_ps", HALF), ps("b_c_ps", 2 * C)
        consts, w_loaded, w_split = sem("b_consts"), sem("b_w_loaded"), sem("b_w_split")
        sums_loaded, sums_inv, sums_stored = sem("b_sums_loaded"), sem("b_sums_inv"), sem("b_sums_stored")
        att_loaded = [sem(f"b_att_loaded{j}") for j in range(2)]
        x_loaded = [sem(f"b_x_loaded{j}") for j in range(2)]
        mix_loaded, norm_ready = sem("b_mix_loaded"), sem("b_norm_s")
        a_done, a_read, b_done, b_read, c_done = (sem(f"b_{n}") for n in ("a_done", "a_read", "b_done", "b_read", "c_done"))
        c_read = sem("b_c_read")
        var_ready, rstd_ready, shift_ready, u_ready, res_ready = (sem(f"b_{n}_s") for n in ("var", "rstd", "shift", "u", "res"))
        uhi_ready, bhi_ready = sem("b_uhi_s"), sem("b_bhi_s")
        s_done, max_ready, exp_done = sem("b_s_done"), sem("b_max_s"), sem("b_exp_done")
        pT_done, pT_ready = sem("b_pT_done"), sem("b_pT_s")
        o_done, o_read = sem("b_o_done"), sem("b_o_read")
        vart_ready, rstdt_ready, v_ready = (sem(f"b_{n}_s") for n in ("vart", "rstdt", "v"))
        t_stored = [sem(f"b_t_stored{j}") for j in range(2)]
        vT_stored, vsum_stored = sem("b_vT_stored"), sem("b_vsum_stored")

        A_STEPS = [("mix", 0), ("mix", 1), ("mix", 2), ("mix", 3), ("ut", 0), ("ut", 1), ("v", 0), ("vt", 0),
                   ("ut", 2), ("ut", 3), ("v", 1), ("vt", 1)]
        B_STEPS = [("proj", 0), ("proj", 1), ("q", 0), ("k", 0), ("q", 1), ("k", 1)]
        HI_STEPS = B_STEPS[2:]
        C_STEPS = [("out", 0), ("out", 1), ("out", 2), ("turn", 0), ("turn", 1), ("out", 3), ("turn", 2), ("turn", 3)]
        PAIRS = TT // 2
        NA, NB, NCS = len(A_STEPS), len(B_STEPS), len(C_STEPS)
        a_at = lambda what, j: A_STEPS.index((what, j))
        b_at = lambda what, j: B_STEPS.index((what, j))
        c_at = lambda what, t: C_STEPS.index((what, t))
        W_OF = {"q": 0, "k": 1, "v": 2}
        SCALE = U ** -0.5

        BETWEEN = [
            [("probs", 7, -1), ("v", 1, 0), ("out", 2, -1), ("proj", 0, 1), ("turn", 0, -1)],
            [("probs", 0, 0), ("values", 3, -1), ("vt", 1, 0), ("turn", 1, -1), ("mix", 0, 1)],
            [("probs", 1, 0), ("out", 3, -1), ("mix", 1, 1), ("vvar", 1, -1), ("proj", 1, 1)],
            [("probs", 2, 0), ("var", 0, 1), ("values", 0, 0), ("mix", 2, 1), ("apply", 0, 1), ("mix", 3, 1)],
            [("probs", 3, 0), ("vapply", 1, -1), ("ut", 0, 1), ("ut", 1, 1), ("q", 0, 1), ("turn", 2, -1), ("k", 0, 1)],
            [("probs", 4, 0), ("var", 1, 1), ("turn", 3, -1), ("values", 1, 0), ("apply", 1, 1), ("v", 0, 1)],
            [("probs", 5, 0), ("vt", 0, 1), ("out", 0, 0), ("ut", 2, 1), ("out", 1, 0), ("ut", 3, 1), ("q", 1, 1)],
            [("probs", 6, 0), ("vvar", 0, 0), ("k", 1, 1), ("values", 2, 0), ("vapply", 0, 0)]]

        def period(b, s, before, after):
            steps = []
            for i in range(TT):
                steps.append(("scores", i, b, s))
                steps += [(what, k, b + d, s if d == 0 else 1 - s) for what, k, d in BETWEEN[i]
                          if d == 0 or (d == 1 and after) or (d == -1 and before)]
            return steps

        def all_images(eng, run):
            run([(what, k, 0, 0) for slot in BETWEEN for what, k, d in slot if d == 1])
            run(period(0, 0, False, True))
            with eng.Fori(1, B - 1, 2) as b:
                run(period(b, 1, True, True))
                run(period(b + 1, 0, True, True))
            run(period(B - 1, 1, True, False))
            run([(what, k, B - 1, 1) for slot in BETWEEN for what, k, d in slot if d == -1])

        half = lambda j: slice(j * HALF, (j + 1) * HALF)
        tile = lambda t: slice(t * P, (t + 1) * P)
        pair = lambda t: slice(2 * t, 2 * t + 2)
        cols = lambda t: slice(2 * t * P, 2 * (t + 1) * P)
        by_tile = lambda ap: ap.rearrange("p (t c) -> p t c", t=2)
        by_chunk = lambda ap: ap.rearrange("p (c n) -> p c n", c=KC)

        with nc.Block() as block:
            @block.sync
            def _(sp):
                x_v = x.rearrange("b h w c -> b (h w) c").rearrange("b (t p) c -> b p t c", p=P)
                t_v = t_d.rearrange("b (t p) c -> b p t c", p=P)
                vT_v = vT_d.rearrange("b c p n -> b p c n")
                heads = [(g, h) for g in range(GROUPS) for h in range(HG)]

                def load_att(n, j, wait=True):
                    if wait:
                        sp.wait_ge(b_done, n * NB - NB + j + 1)
                        sp.nop(nofuse=True)
                    sp.dma_start(att[j][:], att_d[n].rearrange("g p n -> p g n")[:, :, half(j)]).then_inc(att_loaded[j], 16)
                    for h in range(HG):
                        src = rsum_d[n].rearrange("(a g) h n -> a g h n", a=1)[:, :, h, half(j)]
                        sp.dma_start(rsb[j][32 * h:32 * h + 32], src.to_broadcast([32, GROUPS, HALF])).then_inc(att_loaded[j], 16)

                def load_mix(n, wait=True):
                    if wait:
                        sp.wait_ge(a_done, n * NA - NA + a_at("mix", 3) + 1)
                        sp.nop(nofuse=True)
                    sp.dma_start(mixT[:, 0, :], mixT_d[n, 0]).then_inc(mix_loaded, 16)
                    sp.dma_start(mixT[0:CONV_OUT - P, 1, :], mixT_d[n, 1, 0:CONV_OUT - P]).then_inc(mix_loaded, 16)

                def load_x(n, s, j, wait=True):
                    if wait:
                        sp.wait_ge(c_read, (n - 2) * NCS + c_at("out", 2 * j + 1) + 2)
                        sp.nop(nofuse=True)
                    sp.dma_start(xb[s][:, j * QT:(j + 1) * QT, :], x_v[n, :, j * QT:(j + 1) * QT, :]).then_inc(x_loaded[j], 16)

                def store_t(n, j):
                    sp.wait_ge(c_read, n * NCS + c_at("out", 2 * j + 1) + 2)
                    sp.nop(nofuse=True)
                    sp.dma_start(t_v[n, :, j * QT:(j + 1) * QT, :], t_sb[j][:]).then_inc(t_stored[j], 16)

                def store_v(n, j):
                    sp.wait_ge(c_read, n * NCS + c_at("turn", 2 * j + 1) + 2)
                    sp.nop(nofuse=True)
                    sp.dma_start(vT_v[n, :, :, half(j)], v2T[:]).then_inc(vT_stored, 16)
                    if j == 1:
                        sp.dma_start(vsum_d[n], vsum[:]).then_inc(vsum_stored, 16)

                def image(b, s, before, after, ahead):
                    if before:
                        store_v(b - 1, 0)
                        if after:
                            load_x(b + 1, 1 - s, 1)
                        store_t(b - 1, 1)
                    if ahead:
                        load_att(b + 2, 0)
                        load_att(b + 2, 1)
                        load_mix(b + 2)
                    if before:
                        store_v(b - 1, 1)
                    store_t(b, 0)
                    if ahead:
                        load_x(b + 2, s, 0)

                for g, h in heads:
                    r = (g * HG + h) * 16
                    sp.dma_start(rs[r:r + 16], att_d[:, g, 32 * h + DH].rearrange("b (j c) -> j b c", j=16)).then_inc(sums_loaded, 16)
                load_mix(0, False)
                for j in range(2):
                    load_x(0, 0, j, False)
                sp.wait_ge(consts, 2)
                for g, h in heads:
                    sp.dma_start(wp[32 * h:32 * h + DH, g], attn_w[(g * HG + h) * DH:(g * HG + h + 1) * DH]).then_inc(w_loaded, 16)
                sp.dma_start(pb[DK:P], attn_b.rearrange("(p a) -> p a", a=1)).then_inc(w_loaded, 16)
                for i, w in enumerate((w_q, w_k, w_v)):
                    sp.dma_start(w_st[:, :, i], w.rearrange("(k p) u -> p k u", p=P)).then_inc(w_loaded, 16)
                sp.dma_start(wo[:], w_o).then_inc(w_loaded, 16)
                sp.dma_start(bo[:], b_o.rearrange("(a c) -> a c", a=1).to_broadcast([P, C])).then_inc(w_loaded, 16)
                sp.wait_ge(sums_inv, 1)
                for i, (g, h) in enumerate(heads):
                    sp.dma_start(rsum_d[:, g, h].rearrange("b (j c) -> j b c", j=16), rs[16 * i:16 * i + 16]).then_inc(sums_stored, 16)
                for stored in t_stored:
                    sp.sem_inc(stored, 16)
                sp.sem_inc(vT_stored, 16)
                sp.sem_inc(vsum_stored, 16)
                sp.wait_ge(sums_stored, 16 * NH)
                for j in range(2):
                    load_att(0, j, False)
                    load_x(1, 1, j, False)
                for j in range(2):
                    load_att(1, j)
                load_mix(1)
                image(0, 0, False, True, True)
                with sp.Fori(1, B - 3, 2) as b:
                    image(b, 1, True, True, True)
                    image(b + 1, 0, True, True, True)
                image(B - 3, 1, True, True, True)
                image(B - 2, 0, True, True, False)
                image(B - 1, 1, True, False, False)
                store_v(B - 1, 0)
                store_t(B - 1, 1)
                store_v(B - 1, 1)
                for stored in t_stored:
                    sp.wait_ge(stored, 16 * (B + 1))
                sp.wait_ge(vT_stored, 16 * (2 * B + 1))
                sp.wait_ge(vsum_stored, 16 * (B + 1))

            @block.gpsimd
            def _(pool):
                nc.gpsimd.memset(wp[:], 0.0).then_inc(consts, 1)
                make_identity(nc, pool, ident[:], consts)

                def run(steps):
                    for what, k, n, s in steps:
                        if what == "proj":
                            pool.wait_ge(att_loaded[k], n * (16 * (1 + HG)) + 16 * (1 + HG))
                            nc.gpsimd.tensor_tensor(att[k][:], att[k][:], rsb[k][:], ALU.mult).then_inc(norm_ready, 1)
                        if what == "apply":
                            x1 = xb[s][:, k * QT:(k + 1) * QT, :]
                            pool.wait_ge(u_ready, n * 2 + k + 1)
                            nc.gpsimd.tensor_tensor(x1, x1, u[:], ALU.add)
                            pool.drain()
                            nc.gpsimd.tensor_tensor(x1, x1, bo_all, ALU.add).then_inc(res_ready, 1)

                bo_all = bo[:].rearrange("p (a c) -> p a c", a=1).to_broadcast([P, QT, C])
                pool.wait_ge(w_loaded, 16 * (NH + 6))
                all_images(pool, run)

            @block.scalar
            def _(act):
                def rsqrt(out, in_):
                    nc.scalar.activation(out, in_, ACT.Ln)
                    act.drain()
                    return nc.scalar.activation(out, out, ACT.Exp, scale=-0.5)

                def run(steps):
                    for what, k, n, s in steps:
                        if what == "scores":
                            act.wait_ge(max_ready, n * TT + k + 1)
                            nc.scalar.activation(probs[k % 2][:], s_ps[:], ACT.Exp, bias=nmax[:, k:k + 1], accum_out=ssum[:, k:k + 1]
                                                 ).then_inc(exp_done, 1)
                        elif what == "probs":
                            act.wait_ge(pT_done, n * TT + k + 1)
                            nc.scalar.activation(pT[k // 2 % 2][:, :, tile(k % 2)], pT_ps[:].rearrange("p (t q) -> p t q", t=TT),
                                                 ACT.Copy).then_inc(pT_ready, 1)
                        elif what == "values":
                            act.wait_ge(o_done, n * PAIRS + k + 1)
                            nc.scalar.activation(oT[k % 2][:], o_ps[:], ACT.Copy).then_inc(o_read, 1)
                        elif what == "proj":
                            act.wait_ge(b_done, n * NB + b_at("proj", k) + 1)
                            nc.scalar.activation(mixT[DK:P, 1, half(k)], b_ps[DK:P, :], ACT.Identity, bias=pb[DK:P]
                                                 ).then_inc(b_read, 1)
                        elif what == "var":
                            act.wait_ge(var_ready, n * 2 + k + 1)
                            rsqrt(rstd[:, k], var[:, k]).then_inc(rstd_ready, 1)
                        elif what == "vvar":
                            act.wait_ge(vart_ready, n * 2 + k + 1)
                            rsqrt(rstdt[:, k], vart[:, k]).then_inc(rstdt_ready, 1)
                        elif what == "apply":
                            act.wait_ge(shift_ready, n * 2 + k + 1)
                            act.wait_ge(res_ready, n * 2 + k + 1)
                            if k:
                                act.wait_ge(a_done, n * NA + a_at("ut", 1) + 1)
                            for i in range(QT):
                                last = nc.scalar.activation(u[:, i, :], xb[s][:, k * QT + i, :], ACT.Identity,
                                                            bias=shift[:, k, i:i + 1], scale=rstd[:, k, i:i + 1])
                            last.then_inc(u_ready, 1)
                        elif what == "ut":
                            act.wait_ge(a_done, n * NA + a_at("ut", k) + 1)
                            nc.scalar.activation(uT_hi[:, :, cols(k)], by_chunk(a_ps[:]), ACT.Copy).then_inc(uhi_ready, 1)
                        elif what in ("q", "k"):
                            act.wait_ge(b_done, n * NB + b_at(what, k) + 1)
                            hi = q_hi if what == "q" else k_hi
                            nc.scalar.activation(hi[s][:, half(k)], b_ps[:], ACT.Copy, scale=SCALE if what == "q" else 1.0
                                                 ).then_inc(bhi_ready, 1)
                        elif what == "v":
                            act.wait_ge(a_done, n * NA + a_at("v", k) + 1)
                            nc.scalar.activation(vT32[:], a_ps[:], ACT.Copy).then_inc(a_read, 1)
                        elif what == "vt":
                            act.wait_ge(a_done, n * NA + a_at("vt", k) + 1)
                            nc.scalar.activation(v_sb[s][:, k * QT:(k + 1) * QT, :], a_ps[:].rearrange("p (t u) -> p t u", u=U),
                                                 ACT.Copy).then_inc(a_read, 1)
                        elif what == "turn":
                            act.wait_ge(c_done, n * NCS + c_at("turn", k) + 1)
                            if k % 2 == 0:
                                act.wait_ge(vT_stored, n * 32 + 16 * (k // 2) + 16)
                            if k == 0:
                                act.wait_ge(vsum_stored, n * 16 + 16)
                            for c in range(KC):
                                last = nc.scalar.activation(v2T[:, c, cols(k % 2)], by_chunk(c_ps[:])[:, c], ACT.Copy,
                                                            accum_out=vsum[:, c, k:k + 1])
                            last.then_inc(c_read, 1)

                nc.scalar.preload_act_table_set("natural_log_exp_and_others")
                act.wait_ge(w_loaded, 16 * (NH + 6))
                all_images(act, run)

            @block.vector
            def _(dve):
                def spread(buf, st, m, v, ready):
                    dve.drain()
                    for i in range(QT):
                        nc.vector.bn_stats(st[:, i, :], buf[:, i, :])
                    dve.drain()
                    for i in range(QT):
                        nc.vector.bn_aggr(m[:, i, :], st[:, i, :])
                    dve.drain()
                    nc.vector.tensor_scalar(v, m[:, :, 1], 1e-5, None, ALU.add).then_inc(ready, 1)

                def scales(m, r, v, tm, sh, ready):
                    newton(nc, dve, r, v, tm)
                    nc.vector.scalar_tensor_tensor(sh, m[:, :, 0], -1.0, r, ALU.mult, ALU.mult).then_inc(ready, 1)

                def run(steps):
                    for what, k, n, s in steps:
                        if what == "scores":
                            dve.wait_ge(s_done, n * TT + k + 1)
                            nc.vector.tensor_reduce(nmax[:, k:k + 1], s_ps[:], axis=AX.X, op=ALU.max, negate=True).then_inc(max_ready, 1)
                        elif what == "values":
                            dve.wait_ge(exp_done, n * TT + (k + 1) * 2 + 1)
                            nc.vector.reciprocal(rsum[:, pair(k)], ssum[:, pair(k)])
                            dve.drain()
                        elif what == "mix":
                            dve.wait_ge(a_done, n * NA + a_at("mix", k) + 1)
                            dve.wait_ge(x_loaded[k // 2], n * 16 + 16)
                            nc.vector.tensor_tensor(xb[s][:, pair(k), :], by_tile(a_ps[:]), xb[s][:, pair(k), :], ALU.add).then_inc(a_read, 1)
                        elif what == "var":
                            spread(xb[s][:, k * QT:(k + 1) * QT, :], st6, mv, var[:, k], var_ready)
                        elif what == "vvar":
                            spread(t_sb[k], st6t, mvt, vart[:, k], vart_ready)
                        elif what == "apply":
                            dve.wait_ge(rstd_ready, n * 2 + k + 1)
                            scales(mv, rstd[:, k], var[:, k], tmp[:, k], shift[:, k], shift_ready)
                        elif what == "vapply":
                            dve.wait_ge(rstdt_ready, n * 2 + k + 1)
                            newton(nc, dve, rstdt[:, k], vart[:, k], tmpt[:, k])
                            for i in range(QT):
                                last = nc.vector.tensor_scalar(v2[:, i, :], t_sb[k][:, i, :], mvt[:, i, 0:1], rstdt[:, k, i:i + 1],
                                                               ALU.subtract, ALU.mult)
                            last.then_inc(v_ready, 1)
                        elif what == "ut":
                            dve.wait_ge(uhi_ready, n * PAIRS + k + 1)
                            nc.vector.tensor_tensor(uT_lo[:, :, cols(k)], by_chunk(a_ps[:]), bits(uT_hi[:, :, cols(k)]), ALU.subtract).then_inc(a_read, 1)
                        elif what in ("q", "k"):
                            dve.wait_ge(bhi_ready, n * len(HI_STEPS) + HI_STEPS.index((what, k)) + 1)
                            hi, lo = (q_hi, q_lo) if what == "q" else (k_hi, k_lo)
                            nc.vector.scalar_tensor_tensor(lo[s][:, half(k)], b_ps[:], SCALE if what == "q" else 1.0,
                                                           bits(hi[s][:, half(k)]), ALU.mult, ALU.subtract).then_inc(b_read, 1)
                        elif what == "out":
                            dve.wait_ge(c_done, n * NCS + c_at("out", k) + 1)
                            if k % 2 == 0:
                                dve.wait_ge(res_ready, n * 2 + k // 2 + 2)
                                dve.wait_ge(t_stored[k // 2], n * 16 + 16)
                            for t in range(2 * k, 2 * k + 2):
                                last = nc.vector.scalar_tensor_tensor(t_sb[k // 2][:, t % QT, :], by_tile(c_ps[:])[:, t % 2, :], rsum[:, t:t + 1],
                                                                      xb[s][:, t, :], ALU.mult, ALU.add)
                            last.then_inc(c_read, 1)

                dve.sem_inc(res_ready, 1)
                dve.wait_ge(sums_loaded, 16 * NH)
                nc.vector.reciprocal(rs[:], rs[:]).then_inc(sums_inv, 1)
                dve.wait_ge(w_loaded, 16 * (NH + 6))
                nc.vector.tensor_copy(w_hi[:], w_st[:])
                dve.drain()
                nc.vector.tensor_tensor(w_lo[:], w_st[:], bits(w_hi[:]), ALU.subtract).then_inc(w_split, 1)
                all_images(dve, run)

            @block.tensor
            def _(pe):
                def run(steps):
                    for what, k, n, s in steps:
                        if what == "scores":
                            pe.wait_ge(exp_done, n * TT + k + 1)
                            if k == 0:
                                pe.wait_ge(b_read, n * NB + b_at("k", 1) + 2)
                            for j in range(2):
                                for i, (q, kk) in enumerate(((q_hi, k_hi), (q_hi, k_lo), (q_lo, k_hi))):
                                    m = nc.tensor.matmul(s_ps[:, half(j)], q[s][:, tile(k)], kk[s][:, half(j)], start=i == 0, stop=i == 2)
                            m.then_inc(s_done, 1)
                        elif what == "probs":
                            pe.wait_ge(exp_done, n * TT + k + 2)
                            pe.wait_ge(pT_ready, n * TT + k + 1)
                            for t in range(TT):
                                m = nc.tensor.transpose(pT_ps[:, tile(t)], probs[k % 2][:, tile(t)], ident[:])
                            m.then_inc(pT_done, 1)
                        elif what == "values":
                            pe.wait_ge(pT_ready, n * TT + (k + 1) * 2 + 1)
                            pe.wait_ge(o_read, n * PAIRS + k + 1)
                            pe.wait_ge(a_read, n * NA + NA + 1)
                            for t in range(TT):
                                m = nc.tensor.matmul(o_ps[:], v_sb[s][:, t, :], pT[k % 2][:, t, :], start=t == 0, stop=t == TT - 1)
                            m.then_inc(o_done, 1)
                        elif what == "proj":
                            pe.wait_ge(norm_ready, n * 2 + k + 1)
                            pe.wait_ge(b_read, n * NB + b_at("proj", k) + 1)
                            for g in range(GROUPS):
                                m = nc.tensor.matmul(b_ps[DK:P, :], wp[:, g, :], att[k][:, g, :], start=g == 0, stop=g == GROUPS - 1)
                            m.then_inc(b_done, 1)
                        elif what == "mix":
                            pe.wait_ge(a_read, n * NA + a_at("mix", k) + 1)
                            if k == 0:
                                pe.wait_ge(mix_loaded, n * 32 + 32)
                            pe.wait_ge(b_read, n * NB + b_at("proj", k // 2) + 2)
                            for t in range(2):
                                for c in range(KC):
                                    m = nc.tensor.transpose(by_tile(a_ps[:])[:, t, tile(c)], mixT[:, c, tile(2 * k + t)], ident[:])
                            m.then_inc(a_done, 1)
                        elif what == "ut":
                            pe.wait_ge(a_read, n * NA + a_at("ut", k) + 1)
                            pe.wait_ge(u_ready, n * 2 + k // 2 + 1)
                            for t in range(2):
                                for c in range(KC):
                                    m = nc.tensor.transpose(by_chunk(a_ps[:])[:, c, tile(t)], u[:, (2 * k + t) % QT, tile(c)], ident[:])
                            m.then_inc(a_done, 1)
                        elif what in W_OF:
                            pe.wait_ge(a_read, n * NA + a_at("ut", 2 * k + 1) + 2)
                            if what == "v":
                                bank, done = a_ps, a_done
                                pe.wait_ge(a_read, n * NA + a_at("v", k) + 1)
                            else:
                                bank, done = b_ps, b_done
                                pe.wait_ge(b_read, n * NB + b_at(what, k) + 1)
                            i, total = 0, 3 * KC
                            for c in range(KC):
                                for w, uT in ((w_hi, uT_hi), (w_hi, uT_lo), (w_lo, uT_hi)):
                                    m = nc.tensor.matmul(bank[:], w[:, c, W_OF[what], :], uT[:, c, half(k)], start=i == 0, stop=i == total - 1)
                                    i += 1
                            m.then_inc(done, 1)
                        elif what == "vt":
                            pe.wait_ge(a_read, n * NA + a_at("vt", k) + 1)
                            for t in range(QT):
                                m = nc.tensor.transpose(a_ps[:, tile(t)], vT32[:, tile(t)], ident[:])
                            m.then_inc(a_done, 1)
                        elif what == "out":
                            pe.wait_ge(o_read, n * PAIRS + k + 2)
                            pe.wait_ge(c_read, n * NCS + c_at("out", k) + 1)
                            for t in range(2):
                                m = nc.tensor.matmul(by_tile(c_ps[:])[:, t], oT[k % 2][:, tile(t)], wo[:], start=True, stop=True)
                            m.then_inc(c_done, 1)
                        elif what == "turn":
                            pe.wait_ge(v_ready, n * 2 + k // 2 + 1)
                            pe.wait_ge(c_read, n * NCS + c_at("turn", k) + 1)
                            for t in range(2):
                                for c in range(KC):
                                    m = nc.tensor.transpose(by_chunk(c_ps[:])[:, c, tile(t)], v2[:, (2 * k + t) % QT, tile(c)], ident[:])
                            m.then_inc(c_done, 1)

                pe.sem_inc(exp_done, 1)
                pe.sem_inc(pT_ready, 1)
                pe.sem_inc(o_read, 1)
                pe.sem_inc(a_read, 1)
                pe.sem_inc(b_read, 1)
                pe.sem_inc(c_read, 1)
                pe.wait_ge(consts, 2)
                pe.wait_ge(w_loaded, 16 * (NH + 6))
                pe.wait_ge(w_split, 1)
                all_images(pe, run)


def router_phase(nc, w_r, b_r, vsum_d, wts_d, idx_d):
    CAPACITY = float(-(-B * TOK * 5 // (4 * E)))
    with ExitStack() as ctx:
        sb = lambda name, shape, dt=f32: ctx.enter_context(nc.sbuf_tensor(name, shape, dt))
        sem = lambda name: ctx.enter_context(nc.semaphore(name))
        parts = sb("r2_parts", [P, B, KC, TT // 2])
        vm = sb("r2_vm", [P, KC, B])
        wr = sb("r2_wr", [P, KC, E])
        br = sb("r2_br", [B, E])
        ones = sb("r2_ones", [B, B])
        lg, rw, scale = sb("r2_lg", [B, E]), sb("r2_rw", [B, E]), sb("r2_scale", [B, E])
        nmax, total = sb("r2_nmax", [B, 1]), sb("r2_total", [B, 1])
        best, idx = sb("r2_best", [B, 8]), sb("r2_idx", [B, 8], mybir.dt.uint32)
        wts = sb("r2_wts", [B, TOPK])
        logits = ctx.enter_context(nc.psum_tensor("r2_logits", [B, E], f32))
        loads = ctx.enter_context(nc.psum_tensor("r2_loads", [B, E], f32))
        loaded, made, vm_ready, logits_done = sem("r2_loaded"), sem("r2_made"), sem("r2_vm_s"), sem("r2_logits_done")
        max_ready, exp_ready, rw_ready, loads_done = sem("r2_max_s"), sem("r2_exp_s"), sem("r2_rw_s"), sem("r2_loads_done")
        chosen, stored = sem("r2_chosen"), sem("r2_stored")

        with nc.Block() as block:
            @block.sync
            def _(sp):
                sp.dma_start(parts[:].rearrange("p b c f -> p b (c f)"), vsum_d.rearrange("b p c f -> p b (c f)")).then_inc(loaded, 16)
                sp.dma_start(wr[:], w_r.rearrange("(c p) e -> p c e", p=P)).then_inc(loaded, 16)
                sp.dma_start(br[:], b_r.rearrange("(a e) -> a e", a=1).to_broadcast([B, E])).then_inc(loaded, 16)
                sp.wait_ge(chosen, 1)
                sp.dma_start(wts_d, wts[:]).then_inc(stored, 16)
                sp.dma_start(idx_d, idx[:, 0:TOPK]).then_inc(stored, 16)
                sp.wait_ge(stored, 32)

            @block.scalar
            def _(act):
                for i, (out, in_) in enumerate(((rw, lg), (rw, lg), (wts, best[:, 0:TOPK]))):
                    act.wait_ge(max_ready, i + 1)
                    nc.scalar.activation(out[:], in_ if i == 2 else in_[:], ACT.Exp, bias=nmax[:], accum_out=total[:]
                                         ).then_inc(exp_ready, 1)

            @block.vector
            def _(dve):
                def softmax(out, in_, i):
                    nc.vector.tensor_reduce(nmax[:], in_, axis=AX.X, op=ALU.max, negate=True).then_inc(max_ready, 1)
                    dve.wait_ge(exp_ready, i + 1)
                    nc.vector.reciprocal(total[:], total[:])
                    dve.drain()
                    return nc.vector.tensor_scalar(out, out, total[:], None, ALU.mult)

                nc.vector.memset(ones[:], 1.0).then_inc(made, 1)
                dve.wait_ge(loaded, 48)
                nc.vector.tensor_reduce(vm[:].rearrange("p c b -> p b c"), parts[:], axis=AX.X, op=ALU.add).then_inc(vm_ready, 1)
                dve.wait_ge(logits_done, 1)
                nc.vector.scalar_tensor_tensor(lg[:], logits[:], 1.0 / TOK, br[:], ALU.mult, ALU.add)
                dve.drain()
                softmax(rw[:], lg[:], 0).then_inc(rw_ready, 1)
                dve.wait_ge(loads_done, 1)
                nc.vector.tensor_scalar(scale[:], loads[:], float(TOK), None, ALU.mult)
                dve.drain()
                nc.vector.reciprocal(scale[:], scale[:])
                dve.drain()
                nc.vector.tensor_scalar(scale[:], scale[:], CAPACITY, 1.0, ALU.mult, ALU.min)
                dve.drain()
                nc.vector.tensor_tensor(lg[:], rw[:], scale[:], ALU.mult)
                dve.drain()
                softmax(rw[:], lg[:], 1)
                dve.drain()
                nc.vector.max(best[:], rw[:])
                dve.drain()
                nc.vector.max_index(idx[:], best[:], rw[:])
                softmax(wts[:], best[:, 0:TOPK], 2).then_inc(chosen, 1)

            @block.tensor
            def _(pe):
                pe.wait_ge(vm_ready, 1)
                for c in range(KC):
                    m = nc.tensor.matmul(logits[:], vm[:, c, :], wr[:, c, :], start=c == 0, stop=c == KC - 1)
                m.then_inc(logits_done, 1)
                pe.wait_ge(made, 1)
                pe.wait_ge(rw_ready, 1)
                nc.tensor.matmul(loads[:], ones[:], rw[:], start=True, stop=True).then_inc(loads_done, 1)


def expert_phase(nc, w1, b1, w2, b2, gamma, beta, t_d, vT_d, wts_d, idx_d, out):
    with ExitStack() as ctx:
        sb = lambda name, shape, dt=f32: ctx.enter_context(nc.sbuf_tensor(name, shape, dt))
        ps = lambda name, n: ctx.enter_context(nc.psum_tensor(name, [P, n], f32))
        sem = lambda name: ctx.enter_context(nc.semaphore(name))
        HT = TT // 2
        UNITS = 2 * TOPK * FC
        LATE = 2
        NW = 2 * TOPK
        HB = 4
        ident = sb("x_ident", [P, P])
        gam, bet = sb("x_gam", [P, C]), sb("x_bet", [P, C])
        idx = sb("x_idx", [1, TOPK], mybir.dt.uint32)
        w1_st, w2_st = sb("x_w1_st", [P, TOPK, KC, F]), sb("x_w2_st", [P, TOPK, FC, C])
        w1_hi = [sb(f"x_w1_hi{s}", [P, TOPK, KC, F], f32r) for s in range(2)]
        w1_lo = [sb(f"x_w1_lo{s}", [P, TOPK, KC, F], f32r) for s in range(2)]
        w2_hi = [sb(f"x_w2_hi{s}", [P, TOPK, FC, C], f32r) for s in range(2)]
        w2_lo = [sb(f"x_w2_lo{s}", [P, TOPK, FC, C], f32r) for s in range(2)]
        b1_sb = [sb(f"x_b1{s}", [P, TOPK, FC]) for s in range(2)]
        b2_sb = [sb(f"x_b2{s}", [P, TOPK, KC]) for s in range(2)]
        wts = [sb(f"x_wts{s}", [P, TOPK]) for s in range(2)]
        b2w = [sb(f"x_b2w{s}", [P, KC]) for s in range(2)]
        vT = [sb(f"x_vT{s}", [P, KC, TOK]) for s in range(2)]
        v_hi = [sb(f"x_v_hi{s}", [P, KC, TOK], f32r) for s in range(2)]
        v_lo = [sb(f"x_v_lo{s}", [P, KC, TOK], f32r) for s in range(2)]
        t_sb = sb("x_t", [P, HT, C])
        hid = [sb(f"x_hid{i}", [P, HALF]) for i in range(2)]
        h_hi = [sb(f"x_h_hi{i}", [P, HALF], f32r) for i in range(HB)]
        h_lo = [sb(f"x_h_lo{i}", [P, HALF], f32r) for i in range(HB)]
        z = sb("x_z", [P, KC, HALF])
        zt = sb("x_zt", [P, HT, C])
        st6, mv = sb("x_st6", [P, HT, 6]), sb("x_mv", [P, HT, 2])
        var, rstd, tmp = sb("x_var", [P, HT]), sb("x_rstd", [P, HT]), sb("x_tmp", [P, HT])
        h_ps = [ps(f"x_h_ps{i}", HALF) for i in range(2)]
        y_ps = [[ps(f"x_y_ps{j}{c}", HALF) for c in range(KC)] for j in range(2)]
        z_ps = [ps(f"x_z_ps{i}", 2 * C) for i in range(2)]
        consts, idx_loaded, w_loaded, small_loaded, v_loaded = (sem(f"x_{n}") for n in ("consts", "idx_l", "w_l", "small_l", "v_l"))
        rows_loaded, t_loaded = sem("x_rows_l"), sem("x_t_l")
        whi_ready, w_split, vhi_ready, v_split = sem("x_whi_s"), sem("x_w_split"), sem("x_vhi_s"), sem("x_v_split")
        h_done, hid_ready, h_split, y_done = sem("x_h_done"), sem("x_hid_s"), sem("x_h_split"), sem("x_y_done")
        z_ready, turned, zt_ready = sem("x_z_s"), sem("x_turned"), sem("x_zt_s")
        var_ready, rstd_ready, normed_ready, out_ready, out_stored = (sem(f"x_{n}") for n in ("var_s", "rstd_s", "normed_s", "out_s", "out_stored"))

        def period(b, s, before, after):
            steps = []
            for k in range(UNITS):
                steps.append(("hidden", k, b, s))
                if k >= LATE:
                    steps.append(("expert", k - LATE, b, s))
                elif before:
                    steps.append(("expert", UNITS - LATE + k, b - 1, 1 - s))
                j = k // (UNITS // 2)
                if before or j:
                    n, q = (b, s) if j else (b - 1, 1 - s)
                    what = {LATE - 1: "sum", LATE + 1: "turn", LATE + 2: "norm"}.get(k % (UNITS // 2))
                    if what:
                        steps.append((what, 1 - j, n, q))
                if k == LATE + 4 and after:
                    steps.append(("split", 0, b + 1, 1 - s))
                if 0 <= k - LATE - 5 < NW and after:
                    steps.append(("weights", k - LATE - 5, b + 1, 1 - s))
            return steps

        def all_images(eng, run):
            run([("split", 0, 0, 0)] + [("weights", i, 0, 0) for i in range(NW)])
            run(period(0, 0, False, True))
            with eng.Fori(1, B - 1, 2) as b:
                run(period(b, 1, True, True))
                run(period(b + 1, 0, True, True))
            run(period(B - 1, 1, True, False))
            run([("expert", UNITS - LATE + k, B - 1, 1) for k in range(LATE)])
            run([(what, 1, B - 1, 1) for what in ("sum", "turn", "norm")])

        half = lambda j: slice(j * HALF, (j + 1) * HALF)
        tile = lambda t: slice(t * P, (t + 1) * P)
        def weight(i, s):
            k, second = i // 2, i % 2
            return [w[:, k] for w in ((w2_st, w2_hi[s], w2_lo[s]) if second else (w1_st, w1_hi[s], w1_lo[s]))]

        unit = lambda k: (k // (UNITS // 2), k // FC % TOPK, k % FC)

        with nc.Block() as block:
            @block.sync
            def _(sp):
                out_v = out.rearrange("b h w c -> b (h w) c").rearrange("b (t p) c -> b p t c", p=P)
                t_v = t_d.rearrange("b (t p) c -> b p t c", p=P)

                def load_experts(n, s, first=False):
                    sp.dma_start(idx[:], idx_d[n].rearrange("(a k) -> a k", a=1)).then_inc(idx_loaded, 16)
                    sp.wait_ge(idx_loaded, n * 16 + 16)
                    sp.nop(nofuse=True)
                    chosen = [sp.value_load(idx[0:1, k:k + 1], min_val=0, max_val=E - 1) for k in range(TOPK)]
                    if not first:
                        sp.wait_ge(w_split, n * NW)
                        sp.nop(nofuse=True)
                    for k, e in enumerate(chosen):
                        sp.dma_start(w1_st[:, k], w1[e].rearrange("(c p) f -> p c f", p=P)).then_inc(w_loaded, 16)
                        sp.dma_start(w2_st[:, k], w2[e].rearrange("(c p) d -> p c d", p=P)).then_inc(w_loaded, 16)
                    if not first:
                        sp.wait_ge(z_ready, n * 2)
                        sp.nop(nofuse=True)
                    sp.dma_start(vT[s][:], vT_d[n].rearrange("c p n -> p c n")).then_inc(v_loaded, 16)
                    sp.dma_start(wts[s][:], wts_d[n].rearrange("(a k) -> a k", a=1).to_broadcast([P, TOPK])).then_inc(small_loaded, 16)
                    with nc.allow_non_contiguous_dma(reason="biases of an expert, a word per partition"):
                        for k, e in enumerate(chosen):
                            sp.dma_start(b1_sb[s][:, k], b1[e].rearrange("(c p) -> p c", p=P)).then_inc(small_loaded, 16)
                            sp.dma_start(b2_sb[s][:, k], b2[e].rearrange("(c p) -> p c", p=P)).then_inc(small_loaded, 16)

                def load_t(n, j, first=False):
                    if not first:
                        sp.wait_ge(out_stored, n * 32 + j * 16)
                        sp.nop(nofuse=True)
                    sp.dma_start(t_sb[:], t_v[n, :, j * HT:(j + 1) * HT, :]).then_inc(t_loaded, 16)

                def store(n, j):
                    sp.wait_ge(out_ready, n * 2 + j + 2)
                    sp.nop(nofuse=True)
                    sp.dma_start(out_v[n, :, j * HT:(j + 1) * HT, :], t_sb[:]).then_inc(out_stored, 16)

                def image(b, s, before, after):
                    if after:
                        load_experts(b + 1, 1 - s)
                    if before:
                        store(b - 1, 1)
                        load_t(b, 0)
                    store(b, 0)
                    load_t(b, 1)

                load_experts(0, 0, first=True)
                load_t(0, 0, first=True)
                sp.dma_start(gam[:], gamma.rearrange("(a c) -> a c", a=1).to_broadcast([P, C])).then_inc(rows_loaded, 16)
                sp.dma_start(bet[:], beta.rearrange("(a c) -> a c", a=1).to_broadcast([P, C])).then_inc(rows_loaded, 16)
                image(0, 0, False, True)
                with sp.Fori(1, B - 2, 2) as b:
                    image(b, 1, True, True)
                    image(b + 1, 0, True, True)
                image(B - 1, 1, True, False)
                store(B - 1, 1)
                sp.wait_ge(out_stored, 32 * B)

            @block.gpsimd
            def _(pool):
                wide = lambda row: row[:].rearrange("p (a c) -> p a c", a=1).to_broadcast([P, HT, C])

                def run(steps):
                    for what, k, n, s in steps:
                        if what == "weights":
                            pool.wait_ge(whi_ready, n * NW + k + 1)
                            st, hi, lo = weight(k, s)
                            nc.gpsimd.tensor_tensor(lo, st, bits(hi), ALU.subtract).then_inc(w_split, 1)
                        if what == "norm":
                            pool.wait_ge(normed_ready, n * 2 + k + 1)
                            nc.gpsimd.tensor_tensor(zt[:], zt[:], wide(gam), ALU.mult)
                            pool.drain()
                            nc.gpsimd.tensor_tensor(zt[:], zt[:], wide(bet), ALU.add)
                            pool.drain()
                            pool.wait_ge(t_loaded, n * 32 + k * 16 + 16)
                            nc.gpsimd.tensor_tensor(t_sb[:], t_sb[:], zt[:], ALU.add).then_inc(out_ready, 1)

                make_identity(nc, pool, ident[:], consts)
                pool.wait_ge(rows_loaded, 32)
                all_images(pool, run)

            @block.scalar
            def _(act):
                def run(steps):
                    for what, k, n, s in steps:
                        if what == "split":
                            act.wait_ge(v_loaded, n * 16 + 16)
                            if not (isinstance(n, int) and n == 0):
                                act.wait_ge(y_done, n * UNITS - UNITS + HB)
                            nc.scalar.activation(v_hi[s][:], vT[s][:], ACT.Copy).then_inc(vhi_ready, 1)
                        if what == "weights":
                            if k == 0:
                                act.wait_ge(w_loaded, n * (16 * NW) + 16 * NW)
                            st, hi, lo = weight(k, s)
                            nc.scalar.activation(hi, st, ACT.Copy).then_inc(whi_ready, 1)
                        if what == "hidden":
                            j, e, f = unit(k)
                            act.wait_ge(h_done, n * UNITS + k + 1)
                            act.wait_ge(h_split, n * UNITS + k + 1)
                            if k == 0:
                                act.wait_ge(small_loaded, n * (16 * (2 * TOPK + 1)) + 16 * (2 * TOPK + 1))
                            nc.scalar.activation(hid[k % 2][:], h_ps[k % 2][:], ACT.Gelu, bias=b1_sb[s][:, e, f:f + 1]
                                                 ).then_inc(hid_ready, 1)
                        if what == "turn":
                            for i in range(2):
                                act.wait_ge(turned, n * 4 + k * 2 + i + 1)
                                if i == 0:
                                    act.wait_ge(out_ready, n * 2 + k + 1)
                                nc.scalar.activation(zt[:, 2 * i:2 * i + 2, :], z_ps[i][:].rearrange("p (t c) -> p t c", t=2),
                                                     ACT.Copy).then_inc(zt_ready, 1)
                        if what == "norm":
                            nc.scalar.preload_act_table_set("natural_log_exp_and_others")
                            act.wait_ge(var_ready, n * 2 + k + 1)
                            nc.scalar.activation(rstd[:], var[:], ACT.Ln)
                            act.drain()
                            nc.scalar.activation(rstd[:], rstd[:], ACT.Exp, scale=-0.5).then_inc(rstd_ready, 1)

                all_images(act, run)

            @block.vector
            def _(dve):
                def run(steps):
                    for what, k, n, s in steps:
                        if what == "split":
                            dve.wait_ge(vhi_ready, n + 1)
                            nc.vector.tensor_tensor(v_lo[s][:], vT[s][:], bits(v_hi[s][:]), ALU.subtract).then_inc(v_split, 1)
                            dve.wait_ge(small_loaded, n * (16 * (2 * TOPK + 1)) + 16 * (2 * TOPK + 1))
                            nc.vector.tensor_scalar(b2w[s][:], b2_sb[s][:, 0], wts[s][:, 0:1], None, ALU.mult)
                            dve.drain()
                            nc.vector.scalar_tensor_tensor(b2w[s][:], b2_sb[s][:, 1], wts[s][:, 1:2], b2w[s][:], ALU.mult, ALU.add)
                        if what == "hidden":
                            j, e, f = unit(k)
                            dve.wait_ge(hid_ready, n * UNITS + k + 3)
                            dve.wait_ge(y_done, n * UNITS + k + 1)
                            nc.vector.tensor_scalar(h_hi[k % HB][:], hid[k % 2][:], wts[s][:, e:e + 1], None, ALU.mult)
                            dve.drain()
                            nc.vector.scalar_tensor_tensor(h_lo[k % HB][:], hid[k % 2][:], wts[s][:, e:e + 1], bits(h_hi[k % HB][:]),
                                                           ALU.mult, ALU.subtract).then_inc(h_split, 1)
                        if what == "sum":
                            dve.wait_ge(y_done, n * UNITS + (k + 1) * (UNITS // 2) + HB)
                            for c in range(KC):
                                last = nc.vector.scalar_tensor_tensor(z[:, c, :], y_ps[k][c][:], b2w[s][:, c:c + 1], vT[s][:, c, half(k)],
                                                                      ALU.add, ALU.add)
                            last.then_inc(z_ready, 1)
                        if what == "norm":
                            dve.wait_ge(zt_ready, n * 4 + k * 2 + 4)
                            for i in range(HT):
                                nc.vector.bn_stats(st6[:, i, :], zt[:, i, :])
                            dve.drain()
                            for i in range(HT):
                                nc.vector.bn_aggr(mv[:, i, :], st6[:, i, :])
                            dve.drain()
                            nc.vector.tensor_scalar(var[:], mv[:, :, 1], 1e-5, None, ALU.add).then_inc(var_ready, 1)
                            dve.wait_ge(rstd_ready, n * 2 + k + 1)
                            newton(nc, dve, rstd[:], var[:], tmp[:])
                            for i in range(HT):
                                last = nc.vector.tensor_scalar(zt[:, i, :], zt[:, i, :], mv[:, i, 0:1], rstd[:, i:i + 1], ALU.subtract, ALU.mult)
                            last.then_inc(normed_ready, 1)

                all_images(dve, run)

            @block.tensor
            def _(pe):
                def run(steps):
                    for what, k, n, s in steps:
                        if what == "hidden":
                            j, e, f = unit(k)
                            if k == 0:
                                pe.wait_ge(w_split, n * NW + NW)
                                pe.wait_ge(v_split, n + 1)
                            pe.wait_ge(hid_ready, n * UNITS + k + 1)
                            i = 0
                            for c in range(KC):
                                for w, v in ((w1_hi, v_hi), (w1_hi, v_lo), (w1_lo, v_hi)):
                                    m = nc.tensor.matmul(h_ps[k % 2][:], w[s][:, e, c, tile(f)], v[s][:, c, half(j)],
                                                         start=i == 0, stop=i == 3 * KC - 1)
                                    i += 1
                            m.then_inc(h_done, 1)
                        if what == "expert":
                            j, e, f = unit(k)
                            pe.wait_ge(h_split, n * UNITS + k + 3)
                            if k % (UNITS // 2) == 0:
                                pe.wait_ge(z_ready, n * 2 + j + 1)
                            first, last = e + f == 0, e == TOPK - 1 and f == FC - 1
                            for c in range(KC):
                                for i, (w, h) in enumerate(((w2_hi, h_hi), (w2_hi, h_lo), (w2_lo, h_hi))):
                                    m = nc.tensor.matmul(y_ps[j][c][:], w[s][:, e, f, tile(c)], h[k % HB][:],
                                                         start=first and i == 0, stop=last and i == 2)
                            m.then_inc(y_done, 1)
                        if what == "turn":
                            pe.wait_ge(z_ready, n * 2 + k + 3)
                            for i in range(2):
                                pe.wait_ge(zt_ready, n * 4 + k * 2 + i + 1)
                                for t in range(2):
                                    for c in range(KC):
                                        m = nc.tensor.transpose(z_ps[i][:, t * C + c * P:t * C + (c + 1) * P], z[:, c, tile(2 * i + t)], ident[:])
                                m.then_inc(turned, 1)

                pe.sem_inc(hid_ready, 2)
                pe.sem_inc(h_split, 2)
                pe.sem_inc(y_done, HB)
                pe.sem_inc(z_ready, 2)
                pe.sem_inc(zt_ready, 2)
                pe.sem_inc(out_ready, 1)
                pe.wait_ge(consts, 1)
                all_images(pe, run)


_INS = ["x"] + ["L0_conv_" + n for n in ("conv_w", "conv_b", "qkv_w", "qkv_b", "attn_w", "attn_b", "key_rel_w", "key_rel_h")] + \
    ["L1_attn_" + n for n in ("W_q", "W_k", "W_v", "W_o", "b_o")] + \
    ["L1_ffn_" + n for n in ("Wr", "br", "W1", "b1", "W2", "b2", "gamma", "beta")]


def build(nc, a, out):
    def scratch(name, shape, dt=f32):
        return nc.dram_tensor(name, shape, dt, kind="Internal").ap()

    mixT_d = scratch("mixT_d", (B, KC, P, TOK))
    kq_d = scratch("kq_d", (B, GROUPS, 2, 2, HG * DH, TOK))
    rel_d = scratch("rel_d", (B, GROUPS, 2, 2, P, TOK))
    va_d = scratch("va_d", (B, GROUPS, P, TT * HG * 32))
    att_d = scratch("att_d", (B, GROUPS, P, TOK))
    rsum_d = scratch("rsum_d", (B, GROUPS, HG, TOK))
    t_d = scratch("t_d", (B, TOK, C))
    vT_d = scratch("vT_d", (B, KC, P, TOK))
    vsum_d = scratch("vsum_d", (B, P, KC, TT // 2))
    wts_d, idx_d = scratch("wts_d", (B, TOPK)), scratch("idx_d", (B, TOPK), mybir.dt.uint32)
    front(nc, a["x"], *[a["L0_conv_" + n] for n in ("conv_w", "conv_b", "qkv_w", "qkv_b", "key_rel_w", "key_rel_h")],
          mixT_d, kq_d, rel_d, va_d)
    attention_phase(nc, kq_d, rel_d, va_d, att_d)
    self_attention_phase(nc, a["x"], a["L0_conv_attn_w"], a["L0_conv_attn_b"],
                         *[a["L1_attn_" + n] for n in ("W_q", "W_k", "W_v", "W_o", "b_o")],
                         mixT_d, att_d, rsum_d, t_d, vT_d, vsum_d)
    router_phase(nc, a["L1_ffn_Wr"], a["L1_ffn_br"], vsum_d, wts_d, idx_d)
    expert_phase(nc, *[a["L1_ffn_" + n] for n in ("W1", "b1", "W2", "b2", "gamma", "beta")], t_d, vT_d, wts_d, idx_d, out)


def kernel(**inputs):
    import numpy as _np
    import concourse.bacc as _bacc
    from concourse.bass_utils import run_bass_kernel_spmd as _run

    nc = _bacc.Bacc("TRN2", target_bir_lowering=False, num_devices=1)
    arrays, args = {}, {}
    for name in _INS:
        arrays["in_" + name] = _np.ascontiguousarray(inputs[name])
        args[name] = nc.dram_tensor("in_" + name, arrays["in_" + name].shape, f32, kind="ExternalInput").ap()
    out = nc.dram_tensor("out_0", (B, H, W, C), f32, kind="ExternalOutput").ap()
    build(nc, args, out)
    r = _run(nc, [arrays], core_ids=[0])
    return r.results[0]["out_0"]
```

```python
import concourse.bass as bass
from concourse import mybir
from contextlib import ExitStack

f32 = mybir.dt.float32
f32r = mybir.dt.float32r
ALU = mybir.AluOpType
ACT = mybir.ActivationFunctionType
AX = mybir.AxisListType

P = 128
B, H, W, C = 8, 32, 32, 256
TOK = H * W
TT = TOK // P
KC = C // P
NH, DH = 8, 8
DK = NH * DH
CONV_OUT = C - DK
TAPS = 9
HP, WP = H + 2, W + 2
HALF = TOK // 2
GROUPS = 2
HG = NH // GROUPS
REL = 2 * W - 1
GN_SIZE = 8
U = 128
E, F, TOPK = 8, 512, 2
FC = F // P
FIRST = B // 2


def bits(ap):
    return ap.bitcast(f32)


def make_identity(nc, pool, ident, made):
    nc.gpsimd.memset(ident, 0.0)
    pool.drain()
    nc.gpsimd.affine_select(out=ident, in_=ident, compare_op=ALU.not_equal, fill=1.0, base=0,
                            pattern=[[-1, P]], channel_multiplier=1).then_inc(made, 1)


def newton(nc, dve, rstd, var, tmp):
    nc.vector.tensor_tensor(tmp, rstd, rstd, ALU.mult)
    dve.drain()
    nc.vector.tensor_tensor(tmp, tmp, var, ALU.mult)
    dve.drain()
    nc.vector.tensor_scalar(tmp, tmp, -0.5, 1.5, ALU.mult, ALU.add)
    dve.drain()
    nc.vector.tensor_tensor(rstd, rstd, tmp, ALU.mult)
    dve.drain()


def conv_phase(nc, x, conv_w, conv_b, qkv_w, qkv_b, rel_w, rel_h, q_all, bd_hi, bd_lo, hl, rel_stored, mixT_d, kq_d, rel_d, va_d):
    with ExitStack() as ctx:
        sb = lambda name, shape, dt=f32: ctx.enter_context(nc.sbuf_tensor(name, shape, dt))
        sem = lambda name: ctx.enter_context(nc.semaphore(name))
        ident = sb("c_ident", [P, P])
        gavg = sb("c_gavg", [P, P])
        fold = sb("c_fold", [P, DK])
        w_st = bits(hl[:]).rearrange("p a b n -> p (a b n)")[:, 0:KC * TAPS * CONV_OUT].rearrange(
            "p (k t o) -> p k t o", k=KC, t=TAPS)
        w0_hi = sb("c_w0_hi", [P, KC, TAPS, P], f32r)
        w0_lo = sb("c_w0_lo", [P, KC, TAPS, P], f32r)
        w1_hl = sb("c_w1_hl", [P, KC, TAPS, P], f32r)
        q_st = sb("c_q_st", [P, KC, 3 * DK])
        wkq_hi = sb("c_wkq_hi", [P, KC, P], f32r)
        wkq_lo = sb("c_wkq_lo", [P, KC, P], f32r)
        wv_hl = sb("c_wv_hl", [P, KC, P], f32r)
        cb0, cb1 = sb("c_cb0", [P, 1]), sb("c_cb1", [DK, 1])
        kqb, kqs = sb("c_kqb", [P, 1]), sb("c_kqs", [P, 1])
        vb = sb("c_vb", [P, TT, DK])
        krT = sb("c_krT", [DH, 2, REL])
        kr_rows = sb("c_kr_rows", [P, 2, REL])
        own = sb("c_own", [P, 2, GROUPS, HG])
        bd = sb("c_bd", [P, REL, HG])
        xtok = sb("c_xtok", [P, TT, C])
        xT = sb("c_xT", [P, KC, TOK])
        y32 = sb("c_y32", [P, KC, TOK])
        y_hi = [sb(f"c_y_hi{i}", [P, KC, HP, WP], f32r) for i in range(2)]
        y_lo = [sb(f"c_y_lo{i}", [P, KC, HP, WP], f32r) for i in range(2)]
        st6 = sb("c_st6", [P, KC, 2, 6])
        cms = sb("c_cms", [P, 2, KC])
        cm2 = sb("c_cm2", [P, KC, 2])
        gms = sb("c_gms", [P, 2, KC])
        dev = sb("c_dev", [P, KC])
        gvar = sb("c_gvar", [P, KC])
        sd = sb("c_sd", [P, KC])
        rstd = sb("c_rstd", [P, KC])
        tmp = sb("c_tmp", [P, KC])
        cst = sb("c_cst", [P, KC, TOK])
        c1lo = sb("c_c1lo", [DK, 2, HALF])
        kq32 = sb("c_kq32", [P, TOK])
        kq_hi, kq_lo = sb("c_kq_hi", [P, TOK], f32r), sb("c_kq_lo", [P, TOK], f32r)
        vT = sb("c_vT", [P, TOK])
        va = sb("c_va", [P, TT, NH, 32])
        acc = [ctx.enter_context(nc.psum_tensor(f"c_acc{i}", [P, HALF], f32)) for i in range(4)]
        wide = [ctx.enter_context(nc.psum_tensor(f"c_wide{i}", [P, TOK], f32)) for i in range(2)]
        w_loaded, w_split, consts = sem("c_w_loaded"), sem("c_w_split"), sem("c_consts")
        kr_loaded, rows_loaded, masks = sem("c_kr_loaded"), sem("c_rows_loaded"), sem("c_masks")
        x_loaded, x_turned, xT_ready = sem("c_x_loaded"), sem("c_x_turned"), sem("c_xT_ready")
        stats_ready, gmean_ready, dev_ready, gdev_ready = sem("c_stats"), sem("c_gmean"), sem("c_dev_s"), sem("c_gdev")
        gvar_ready, sd_ready = sem("c_gvar_s"), sem("c_sd_s")
        y32_ready, yhi_ready, y_ready = sem("c_y32_s"), sem("c_yhi_s"), sem("c_y_s")
        unit_done = sem("c_unit_done")
        unit_read = [sem(f"c_unit_read{i}") for i in range(4)]
        c1lo_ready, cst_stored = sem("c_c1lo_s"), sem("c_cst_stored")
        kqhi_ready, kq_ready, kq_stored = sem("c_kqhi"), sem("c_kq_s"), sem("c_kq_stored")
        va_turned, va_ready, va_stored = sem("c_va_turned"), sem("c_va_s"), sem("c_va_stored")
        q_ready, bd_ready = sem("c_q_s"), sem("c_bd_s")
        rel_hi = sem("c_rel_hi")

        UNITS = [("kq", 0), ("conv0", 0), ("kq", 1), ("conv0", 1), ("v", 0), ("conv1", 0), ("v", 1), ("conv1", 1)]
        UNITS_REL = UNITS[:5] + [("rel", 0), ("rel", 1), UNITS[5], ("rel", 2), ("rel", 3), UNITS[6], ("rel", 4), ("rel", 5),
                                 UNITS[7], ("rel", 6), ("rel", 7)]
        RU = len(UNITS_REL) - len(UNITS)
        later = lambda b: isinstance(b, int) and b >= FIRST
        units = lambda b: UNITS_REL if later(b) else UNITS
        before = lambda b: FIRST * len(UNITS) + (b - FIRST) * len(UNITS_REL) if later(b) else b * len(UNITS)
        done = lambda b, what, t: before(b) + units(b).index((what, t)) + 1
        bank = lambda b, what, t: units(b).index((what, t)) % 4
        read = lambda b, what, t: before(b) // 4 + units(b).index((what, t)) // 4 + 2
        KQ_DMAS = 4 * GROUPS
        x_v = x.rearrange("b h w c -> b (h w) c").rearrange("b (t p) c -> b p t c", p=P)

        def rel_target(part, wh, n):
            if wh == 0:
                return part.rearrange("p b (y x) -> p x b y", x=W)[:, 4 * n:4 * n + 4]
            return part.rearrange("p b (y x) -> p y b x", x=W)[:, 4 * n:4 * n + 4]

        def rel_bank(u):
            return acc[u][:].rearrange("p (i b n) -> p i b n", i=4, b=FIRST)

        def image_rows(ap):
            return ap.rearrange("p (y x) -> p y x", x=W)

        def all_images(eng, image):
            with eng.Fori(0, FIRST, 2) as b:
                image(b, 0, True)
                image(b + 1, 1, True)
            for b in range(FIRST, B):
                image(b, b % 2, b + 1 < B)

        with nc.Block() as block:
            @block.sync
            def _(sp):
                sp.dma_start(xtok[:], x_v[0]).then_inc(x_loaded, 16)
                for k in range(KC):
                    sp.dma_start(w_st[:, k], conv_w.rearrange("a b (k p) o -> p k (a b) o", p=P)[:, k]).then_inc(w_loaded, 16)
                sp.dma_start(q_st[:], qkv_w.rearrange("(k p) o -> p k o", p=P)).then_inc(w_loaded, 16)
                sp.dma_start(cb0[:], conv_b[0:P].rearrange("(p a) -> p a", a=1)).then_inc(w_loaded, 16)
                sp.dma_start(cb1[:], conv_b[P:CONV_OUT].rearrange("(p a) -> p a", a=1)).then_inc(w_loaded, 16)
                sp.dma_start(kqb[:], qkv_b[0:P].rearrange("(p a) -> p a", a=1)).then_inc(w_loaded, 16)
                sp.dma_start(vb[:], bass.AP(tensor=qkv_b.tensor, offset=P, ap=[[0, P], [0, TT], [1, DK]])).then_inc(w_loaded, 16)
                with nc.allow_non_contiguous_dma(reason="two small tables, transposed once"):
                    sp.dma_start(krT[:, 0, :], rel_w.rearrange("m d -> d m")).then_inc(kr_loaded, 16)
                    sp.dma_start(krT[:, 1, :], rel_h.rearrange("m d -> d m")).then_inc(kr_loaded, 16)
                sp.wait_ge(kr_loaded, 32)
                for h in range(P // DH):
                    sp.dma_start(kr_rows[DH * h:DH * (h + 1)], krT[:]).then_inc(rows_loaded, 16)
                sp.sem_inc(kq_stored, KQ_DMAS * 16)
                sp.sem_inc(cst_stored, 32)
                sp.sem_inc(va_stored, 16 * GROUPS)

                def load(p):
                    sp.wait_ge(x_turned, p * KC)
                    sp.dma_start(xtok[:], x_v[p]).then_inc(x_loaded, 16)

                def image(b, ahead):
                    sp.wait_ge(kq_ready, b + 1)
                    for part, buf in enumerate((kq_hi, kq_lo)):
                        for kq in range(2):
                            for g in range(GROUPS):
                                rows = kq * DK + g * HG * DH
                                sp.dma_start(kq_d[b, g, part, kq], bits(buf[rows:rows + HG * DH])).then_inc(kq_stored, 16)
                    if ahead:
                        load(b + 2)
                    sp.wait_ge(unit_read[bank(b, "conv1", 1)], read(b, "conv1", 1))
                    sp.dma_start(mixT_d[b, 0], cst[:, 0, :]).then_inc(cst_stored, 16)
                    sp.dma_start(mixT_d[b, 1, 0:CONV_OUT - P], cst[0:CONV_OUT - P, 1, :]).then_inc(cst_stored, 16)
                    sp.wait_ge(va_ready, b + 2)
                    for g in range(GROUPS):
                        sp.dma_start(va_d[b, g].rearrange("p (t c) -> p t c", t=TT),
                                     va[:, :, HG * g:HG * (g + 1), :].rearrange("p t h c -> p t (h c)")).then_inc(va_stored, 16)
                    if later(b):
                        sp.wait_ge(unit_read[bank(b, "rel", RU - 1)], read(b, "rel", RU - 1))
                        wh, g = (b - FIRST) % 2, (b - FIRST) // 2
                        for part in range(2):
                            sp.dma_start(rel_d[0:FIRST, g, wh, part].rearrange("b p n -> p b n"), bits(hl[:, part])).then_inc(rel_stored, 16)

                load(1)
                with sp.Fori(0, FIRST) as b:
                    image(b, True)
                for b in range(FIRST, B):
                    image(b, b + 2 < B)
                sp.wait_ge(kq_stored, KQ_DMAS * 16 * (B + 1))
                sp.wait_ge(cst_stored, 32 * (B + 1))
                sp.wait_ge(va_stored, 16 * GROUPS * (B + 1))

            @block.gpsimd
            def _(pool):
                nc.gpsimd.memset(gavg[:], 1.0 / GN_SIZE)
                nc.gpsimd.memset(fold[:], 0.0)
                nc.gpsimd.memset(va[:], 0.0)
                make_identity(nc, pool, ident[:], consts)
                g3 = gavg[:].rearrange("p (g c) -> p g c", c=GN_SIZE)
                for base, sign in ((0, 1), (GN_SIZE - 1, -1)):
                    nc.gpsimd.affine_select(out=g3, in_=g3, compare_op=ALU.is_ge, fill=0.0, base=base,
                                            pattern=[[-sign * GN_SIZE, P // GN_SIZE], [0, GN_SIZE]],
                                            channel_multiplier=sign)
                    nc.gpsimd.affine_select(out=fold[:], in_=fold[:], compare_op=ALU.not_equal, fill=1.0,
                                            base=-DK if base else 0, pattern=[[-1, DK]], channel_multiplier=1)
                    pool.drain()
                nc.gpsimd.memset(va[:, :, :, DH:DH + 1], 1.0).then_inc(consts, 1)
                nc.gpsimd.memset(own[:], 1.0)
                pool.drain()
                for base, sign in ((0, 1), (DH - 1, -1)):
                    nc.gpsimd.affine_select(out=own[:], in_=own[:], compare_op=ALU.is_ge, fill=0.0, base=base,
                                            pattern=[[-sign * DK, 2], [-sign * HG * DH, GROUPS], [-sign * DH, HG]],
                                            channel_multiplier=sign)
                    pool.drain()
                nc.gpsimd.tensor_tensor(own[:, 0], own[:, 0], own[:, 1], ALU.add).then_inc(masks, 1)

            @block.scalar
            def _(act):
                def prep(p, first=False):
                    for c in range(KC):
                        act.wait_ge(x_turned, p * KC + c + 1)
                        if not first:
                            act.wait_ge(y32_ready, p * KC)
                        nc.scalar.activation(xT[:, c, :], wide[c][:], ACT.Copy).then_inc(xT_ready, 1)

                def round_y(p, s, first=False):
                    for c in range(KC):
                        act.wait_ge(y32_ready, p * KC + c + 1)
                        if not first:
                            act.wait_ge(va_turned, p)
                        nc.scalar.activation(y_hi[s][:, c, 1:H + 1, 1:W + 1], image_rows(y32[:, c, :]),
                                             ACT.Copy).then_inc(yhi_ready, 1)

                def spread(p):
                    act.wait_ge(gvar_ready, p + 1)
                    nc.scalar.activation(sd[:], gvar[:], ACT.Sqrt).then_inc(sd_ready, 1)

                def image(b, s, prefetch):
                    if prefetch:
                        prep(b + 1)
                    act.wait_ge(unit_read[bank(b, "kq", 1)], read(b, "kq", 1))
                    act.wait_ge(kq_stored, (b + 1) * (KQ_DMAS * 16))
                    nc.scalar.activation(kq_hi[:], kq32[:], ACT.Copy).then_inc(kqhi_ready, 1)
                    nc.scalar.activation(q_all[DK:P, b, :], kq32[DK:P, :], ACT.Copy)
                    act.wait_ge(kq_ready, b + 1)
                    nc.scalar.activation(q_all[0:DK, b, :], bits(kq_lo[DK:P, :]), ACT.Copy).then_inc(q_ready, 1)
                    if prefetch:
                        spread(b + 1)
                    for what, t in units(b)[units(b).index(("v", 0)):]:
                        act.wait_ge(unit_done, done(b, what, t))
                        u = bank(b, what, t)
                        if what == "v":
                            nc.scalar.activation(vT[:, t * HALF:(t + 1) * HALF], acc[u][:], ACT.Copy).then_inc(unit_read[u], 1)
                            if t == 0 and prefetch:
                                round_y(b + 1, 1 - s)
                        elif what == "conv1":
                            nc.scalar.activation(c1lo[:, t, :], acc[u][DK:P, :], ACT.Copy).then_inc(c1lo_ready, 1)
                        else:
                            if t == 0 and b > FIRST:
                                act.wait_ge(rel_stored, 32 * (b - FIRST))
                            nc.scalar.activation(rel_target(hl[:, 0], (b - FIRST) % 2, t), rel_bank(u), ACT.Copy).then_inc(rel_hi, 1)

                prep(0, first=True)
                spread(0)
                round_y(0, 0, first=True)
                all_images(act, image)

            @block.vector
            def _(dve):
                def prep_stats(p):
                    for c in range(KC):
                        dve.wait_ge(xT_ready, p * KC + c + 1)
                        for s in range(2):
                            nc.vector.bn_stats(st6[:, c, s, :], xT[:, c, s * HALF:(s + 1) * HALF])
                    dve.drain()
                    for c in range(KC):
                        nc.vector.bn_aggr(cm2[:, c, :], st6[:, c].rearrange("p s d -> p (s d)"))
                    dve.drain()
                    nc.vector.tensor_copy(cms[:].rearrange("p s c -> p c s"), cm2[:]).then_inc(stats_ready, 1)

                def prep_mean(p):
                    dve.wait_ge(gmean_ready, p + 1)
                    nc.vector.tensor_copy(gms[:].rearrange("p s c -> p (s c)"), wide[0][:, 0:2 * KC])
                    dve.drain()
                    nc.vector.tensor_tensor(dev[:], cms[:, 0, :], gms[:, 0, :], ALU.subtract)
                    dve.drain()
                    nc.vector.tensor_tensor(dev[:], dev[:], dev[:], ALU.mult).then_inc(dev_ready, 1)

                def prep_var(p):
                    dve.wait_ge(gdev_ready, p + 1)
                    nc.vector.scalar_tensor_tensor(gvar[:], wide[1][:, 0:KC], 1e-5, gms[:, 1, :], ALU.add, ALU.add
                                                   ).then_inc(gvar_ready, 1)

                def prep_y(p):
                    dve.wait_ge(sd_ready, p + 1)
                    nc.vector.reciprocal(rstd[:], sd[:])
                    dve.drain()
                    newton(nc, dve, rstd[:], gvar[:], tmp[:])
                    for c in range(KC):
                        nc.vector.tensor_scalar(y32[:, c, :], xT[:, c, :], gms[:, 0, c:c + 1], rstd[:, c:c + 1],
                                                ALU.subtract, ALU.mult).then_inc(y32_ready, 1)

                def low_y(p, s):
                    for c in range(KC):
                        dve.wait_ge(yhi_ready, p * KC + c + 1)
                        nc.vector.tensor_tensor(y_lo[s][:, c, 1:H + 1, 1:W + 1], image_rows(y32[:, c, :]),
                                                bits(y_hi[s][:, c, 1:H + 1, 1:W + 1]), ALU.subtract).then_inc(y_ready, 1)

                def relative_keys():
                    dve.wait_ge(masks, 1)
                    dve.wait_ge(rows_loaded, 16 * (P // DH))
                    for wh in range(2):
                        for g in range(GROUPS):
                            for h in range(HG):
                                nc.vector.tensor_scalar(bd[:, :, h], kr_rows[:, wh, :], own[:, 0, g, h:h + 1], None, ALU.mult)
                            dve.drain()
                            flat = bd[:].rearrange("p m h -> p (m h)")
                            nc.vector.tensor_copy(bd_hi[:, wh, g], flat)
                            dve.drain()
                            nc.vector.tensor_tensor(bd_lo[:, wh, g], flat, bits(bd_hi[:, wh, g]), ALU.subtract).then_inc(bd_ready, 1)
                            dve.drain()

                def kq(b, t):
                    dve.wait_ge(unit_done, done(b, "kq", t))
                    if t == 0:
                        dve.wait_ge(q_ready, b + 1)
                    nc.vector.tensor_scalar(kq32[:, t * HALF:(t + 1) * HALF], acc[bank(b, "kq", t)][:], kqb[:], kqs[:],
                                            ALU.add, ALU.mult).then_inc(unit_read[bank(b, "kq", t)], 1)

                def conv0(b, t):
                    dve.wait_ge(unit_done, done(b, "conv0", t))
                    if t == 0:
                        dve.wait_ge(cst_stored, b * 32 + 32)
                    nc.vector.tensor_scalar(cst[:, 0, t * HALF:(t + 1) * HALF], acc[bank(b, "conv0", t)][:], cb0[:], None,
                                            ALU.add).then_inc(unit_read[bank(b, "conv0", t)], 1)

                def conv1(b, t):
                    dve.wait_ge(c1lo_ready, b * 2 + t + 1)
                    nc.vector.scalar_tensor_tensor(cst[0:DK, 1, t * HALF:(t + 1) * HALF], acc[bank(b, "conv1", t)][0:DK, :],
                                                   cb1[:], c1lo[:, t, :], ALU.add, ALU.add
                                                   ).then_inc(unit_read[bank(b, "conv1", t)], 1)

                def relative(b, n):
                    wh, u = (b - FIRST) % 2, bank(b, "rel", n)
                    dve.wait_ge(rel_hi, (b - FIRST) * RU + n + 1)
                    nc.vector.tensor_tensor(rel_target(hl[:, 1], wh, n), rel_bank(u), rel_target(bits(hl[:, 0]), wh, n), ALU.subtract
                                            ).then_inc(unit_read[u], 1)

                def image(b, s, prefetch):
                    kq(b, 0)
                    if prefetch:
                        prep_stats(b + 1)
                    conv0(b, 0)
                    if prefetch:
                        prep_mean(b + 1)
                    kq(b, 1)
                    dve.wait_ge(kqhi_ready, b + 1)
                    nc.vector.tensor_tensor(kq_lo[:], kq32[:], bits(kq_hi[:]), ALU.subtract).then_inc(kq_ready, 1)
                    conv0(b, 1)
                    if prefetch:
                        prep_var(b + 1)
                        prep_y(b + 1)
                        low_y(b + 1, 1 - s)
                    for what, t in units(b)[units(b).index(("v", 0)):]:
                        if what == "conv1":
                            conv1(b, t)
                        if what == "rel":
                            relative(b, t)
                    dve.wait_ge(va_turned, b + 2)
                    dve.wait_ge(va_stored, (b + 1) * (16 * GROUPS))
                    nc.vector.tensor_tensor(va[:, :, :, 0:DH],
                                            wide[1][:, 0:TT * DK].rearrange("p (t h d) -> p t h d", h=NH, d=DH),
                                            vb[:].rearrange("p t (h d) -> p t h d", d=DH), ALU.add).then_inc(va_ready, 1)

                nc.vector.memset(kqs[0:DK], 1.0)
                nc.vector.memset(kqs[DK:P], DH ** -0.5)
                for buf in y_hi + y_lo:
                    nc.vector.memset(bits(buf[:]), 0.0)
                dve.sem_inc(va_ready, 1)
                dve.sem_inc(q_ready, 1)
                dve.wait_ge(w_loaded, 16 * (KC + 5))
                dve.wait_ge(consts, 2)
                for src, hi, lo in ((w_st[:, :, :, 0:P], w0_hi[:], w0_lo[:]),
                                    (w_st[:, :, :, P:CONV_OUT], w1_hl[:, :, :, 0:DK], w1_hl[:, :, :, DK:P]),
                                    (q_st[:, :, 0:P], wkq_hi[:], wkq_lo[:]),
                                    (q_st[:, :, P:3 * DK], wv_hl[:, :, 0:DK], wv_hl[:, :, DK:P])):
                    for k in range(KC):
                        nc.vector.tensor_copy(hi[:, k], src[:, k])
                    dve.drain()
                    for k in range(KC):
                        last = nc.vector.tensor_tensor(lo[:, k], src[:, k], bits(hi[:, k]), ALU.subtract)
                    last.then_inc(w_split, 1)
                prep_stats(0)
                prep_mean(0)
                prep_var(0)
                prep_y(0)
                low_y(0, 0)
                relative_keys()
                all_images(dve, image)

            @block.tensor
            def _(pe):
                def turn(p, first=False):
                    pe.wait_ge(x_loaded, p * 16 + 16)
                    for c in range(KC):
                        if c == 1 and not first:
                            pe.wait_ge(va_ready, p)
                        for t in range(TT):
                            m = nc.tensor.transpose(wide[c][:, t * P:(t + 1) * P], xtok[:, t, c * P:(c + 1) * P], ident[:])
                        m.then_inc(x_turned, 1)

                def group_mean(p):
                    pe.wait_ge(stats_ready, p + 1)
                    nc.tensor.matmul(wide[0][:, 0:2 * KC], gavg[:], cms[:].rearrange("p s c -> p (s c)"),
                                     start=True, stop=True).then_inc(gmean_ready, 1)

                def group_dev(p):
                    pe.wait_ge(dev_ready, p + 1)
                    nc.tensor.matmul(wide[1][:, 0:KC], gavg[:], dev[:], start=True, stop=True).then_inc(gdev_ready, 1)

                all_taps = [(t // 3, t % 3, t) for t in range(TAPS)]
                centre = [(1, 1, None)]

                HI, LO = y_hi, y_lo
                parts = {"kq": (((wkq_hi, HI), (wkq_hi, LO), (wkq_lo, HI)), centre),
                         "conv0": (((w0_hi, HI), (w0_hi, LO), (w0_lo, HI)), all_taps),
                         "v": (((wv_hl, HI), (wv_hl, LO)), centre),
                         "conv1": (((w1_hl, HI), (w1_hl, LO)), all_taps)}

                def relative(b, n, u):
                    wh, g = (b - FIRST) % 2, (b - FIRST) // 2
                    pe.wait_ge(q_ready, FIRST + 1)
                    pe.wait_ge(bd_ready, 2 * GROUPS)
                    for j in range(4):
                        i = 4 * n + j
                        q = q_all[:, 0:FIRST, i::W] if wh == 0 else q_all[:, 0:FIRST, i * W:(i + 1) * W]
                        for k, bdp in enumerate((bd_hi, bd_lo)):
                            m = nc.tensor.matmul(rel_bank(u)[:, j], bdp[:, wh, g, HG * (W - 1 - i):HG * (2 * W - 1 - i)], q,
                                                 start=k == 0, stop=k == 1, skip_group_check=True)
                    m.then_inc(unit_done, 1)

                def unit(b, s, what, t):
                    u = bank(b, what, t)
                    pe.wait_ge(unit_read[u], read(b, what, t) - 1)
                    if what == "rel":
                        relative(b, t, u)
                        return
                    pairs, taps = parts[what]
                    n, total = 0, len(pairs) * KC * len(taps)
                    rows = t * (H // 2)
                    for k in range(KC):
                        for dy, dx, tap in taps:
                            for wt, y in pairs:
                                m = nc.tensor.matmul(image_rows(acc[u][:]), wt[:, k, :] if tap is None else wt[:, k, tap, :],
                                                     y[s][:, k, rows + dy:rows + dy + H // 2, dx:dx + W],
                                                     start=n == 0, stop=n == total - 1)
                                n += 1
                    m.then_inc(unit_done, 1)

                def image(b, s, prefetch):
                    pe.wait_ge(y_ready, b * KC + KC)
                    for what, t in units(b):
                        unit(b, s, what, t)
                        if prefetch and (what, t) == ("kq", 0):
                            turn(b + 1)
                        if prefetch and (what, t) == ("conv0", 0):
                            group_mean(b + 1)
                        if prefetch and (what, t) == ("conv0", 1):
                            group_dev(b + 1)
                    pe.wait_ge(unit_read[bank(b, "v", 1)], read(b, "v", 1))
                    if prefetch:
                        pe.wait_ge(gvar_ready, b + 2)
                    for t in range(TT):
                        m = nc.tensor.matmul(wide[1][:, t * DK:(t + 1) * DK], vT[:, t * P:(t + 1) * P], fold[:],
                                             start=True, stop=True)
                    m.then_inc(va_turned, 1)

                for free in unit_read:
                    pe.sem_inc(free, 1)
                pe.sem_inc(va_turned, 1)
                pe.wait_ge(consts, 2)
                turn(0, first=True)
                group_mean(0)
                group_dev(0)
                pe.wait_ge(w_split, 4)
                all_images(pe, image)


def relative_phase(nc, q_all, bd_hi, bd_lo, first_stored, rel_d):
    LAST = B - FIRST
    with ExitStack() as ctx:
        sb = lambda name, shape, dt=f32: ctx.enter_context(nc.sbuf_tensor(name, shape, dt))
        sem = lambda name: ctx.enter_context(nc.semaphore(name))
        hl = [sb(f"r_hl{i}", [P, 2, LAST, TOK], f32r) for i in range(4)]
        ps = [ctx.enter_context(nc.psum_tensor(f"r_ps{i}", [P, 4, LAST, W], f32)) for i in range(8)]
        unit_done, hi_ready, lo_ready, stored = sem("r_unit_done"), sem("r_hi_s"), sem("r_lo_s"), sem("r_stored")
        UNITS = W // 4
        RELS = [(wh, g) for g in range(GROUPS) for wh in range(2)]

        def target(buf, wh, n):
            if wh == 0:
                return buf.rearrange("p b (y x) -> p x b y", x=W)[:, 4 * n:4 * n + 4]
            return buf.rearrange("p b (y x) -> p y b x", x=W)[:, 4 * n:4 * n + 4]

        with nc.Block() as block:
            @block.sync
            def _(sp):
                for r, (wh, g) in enumerate(RELS):
                    sp.wait_ge(lo_ready, UNITS * (r + 1))
                    for part in range(2):
                        sp.dma_start(rel_d[FIRST:B, g, wh, part].rearrange("b p n -> p b n"), bits(hl[r][:, part])).then_inc(stored, 16)
                sp.wait_ge(stored, 32 * len(RELS))
                sp.wait_ge(first_stored, 32 * len(RELS))

            @block.scalar
            def _(act):
                for r, (wh, g) in enumerate(RELS):
                    for n in range(UNITS):
                        act.wait_ge(unit_done, r * UNITS + n + 1)
                        nc.scalar.activation(target(hl[r][:, 0], wh, n), ps[n][:], ACT.Copy).then_inc(hi_ready, 1)

            @block.vector
            def _(dve):
                for r, (wh, g) in enumerate(RELS):
                    for n in range(UNITS):
                        dve.wait_ge(hi_ready, r * UNITS + n + 1)
                        nc.vector.tensor_tensor(target(hl[r][:, 1], wh, n), ps[n][:], target(bits(hl[r][:, 0]), wh, n), ALU.subtract
                                                ).then_inc(lo_ready, 1)

            @block.tensor
            def _(pe):
                for r, (wh, g) in enumerate(RELS):
                    for n in range(UNITS):
                        if r:
                            pe.wait_ge(lo_ready, (r - 1) * UNITS + n + 1)
                        for j in range(4):
                            i = 4 * n + j
                            q = q_all[:, FIRST:B, i::W] if wh == 0 else q_all[:, FIRST:B, i * W:(i + 1) * W]
                            for k, bdp in enumerate((bd_hi, bd_lo)):
                                m = nc.tensor.matmul(ps[n][:, j], bdp[:, wh, g, HG * (W - 1 - i):HG * (2 * W - 1 - i)], q,
                                                     start=k == 0, stop=k == 1, skip_group_check=True)
                        m.then_inc(unit_done, 1)


def front(nc, x, conv_w, conv_b, qkv_w, qkv_b, rel_w, rel_h, mixT_d, kq_d, rel_d, va_d):
    with (nc.sbuf_tensor("q_all", [P, B, TOK], f32r) as q_all,
          nc.sbuf_tensor("bd_hi", [P, 2, GROUPS, REL * HG], f32r) as bd_hi,
          nc.sbuf_tensor("bd_lo", [P, 2, GROUPS, REL * HG], f32r) as bd_lo,
          nc.sbuf_tensor("rel_first", [P, 2, FIRST, TOK], f32r) as hl,
          nc.semaphore("rel_first_stored") as rel_stored):
        conv_phase(nc, x, conv_w, conv_b, qkv_w, qkv_b, rel_w, rel_h, q_all, bd_hi, bd_lo, hl, rel_stored, mixT_d, kq_d, rel_d, va_d)
        relative_phase(nc, q_all, bd_hi, bd_lo, rel_stored, rel_d)


def attention_phase(nc, kq_d, rel_d, va_d, att_d):
    NG = B * GROUPS
    BUFS = 3
    ROW_W, ROW_H = (0, W), (2 * W, 2 * W + H // 2)
    ROW_Q = 2 * W + H
    ROW_M = ROW_Q + 3 * DH
    with ExitStack() as ctx:
        sb = lambda name, shape, dt=f32: ctx.enter_context(nc.sbuf_tensor(name, shape, dt))
        sem = lambda name: ctx.enter_context(nc.semaphore(name))
        ident = sb("a_ident", [P, P])
        ones_hot = sb("a_ones_hot", [P, TOK])
        qf = [sb(f"a_qf{i}", [P, HG, 2, TOK], f32r) for i in range(BUFS)]
        kf = [sb(f"a_kf{i}", [P, HG, TOK], f32r) for i in range(BUFS)]
        va = [sb(f"a_va{i}", [P, TT, HG, 32]) for i in range(BUFS)]
        probs = sb("a_probs", [P, 2, HG, TOK])
        pmax = sb("a_pmax", [P, 2, TT, 2])
        nmax = sb("a_nmax", [P, HG, TT])
        mrow = sb("a_mrow", [TT, HG, P], f32r)
        out = sb("a_out", [P, TOK])
        banks = ctx.enter_context(nc.psum_tensor("a_banks", [P, 6, HALF], f32))
        st, sm = [banks[:, i] for i in range(3)], [banks[:, i] for i in range(3, 6)]
        wide = [banks[:, 2 * i:2 * i + 2] for i in range(2)]
        pv = ctx.enter_context(nc.psum_tensor("a_pv", [P, TOK], f32))
        made = sem("a_made")
        built = [sem(f"a_built{i}") for i in range(BUFS)]
        loaded = [sem(f"a_loaded{i}") for i in range(BUFS)]
        max_loaded = [sem(f"a_max_loaded{h}") for h in range(HG)]
        sm_done, sm_read, nmax_ready = sem("a_sm_done"), sem("a_sm_read"), sem("a_nmax_s")
        wide_done, wide_read = sem("a_wide_done"), sem("a_wide_read")
        st_done, exp_done, pv_done = sem("a_st_done"), sem("a_exp_done"), sem("a_pv_done")
        out_ready, out_stored = sem("a_out_s"), sem("a_out_stored")
        LOADS = 4 + 4 + 6 + 3 + 1

        LATE = 4
        units = []
        for h in range(HG):
            for n in range(2 * TT):
                units.append(("logits", h, n))
                if h and n == LATE - 1:
                    units.append(("turn", h - 1, 0))
        units.append(("turn", HG - 1, 0))
        NU = len(units)
        turn_at = {h: units.index(("turn", h, 0)) for h in range(HG)}
        STEPS = TT * HG
        NS = 2 * STEPS
        first_bank = lambda j, k: sm[(j * NU + k) % 3]
        second_bank = lambda j, u: st[(j * NS + u) % 3]

        def all_groups(eng, period):
            last = NG - 1
            full = (last - 1) // BUFS - 1
            with eng.Fori(0, full * BUFS, BUFS) as n:
                for j in range(BUFS):
                    period(n + j, j, True, True)
            for n in range(full * BUFS, NG):
                period(n, n % BUFS, n < last, n + 2 < NG)

        with nc.Block() as block:
            @block.sync
            def _(sp):
                def load(n, j):
                    if not (isinstance(n, int) and n < BUFS):
                        sp.wait_ge(pv_done, n * TT - 2 * TT + 2)
                    load_queries(n, j)
                    load_keys(n, j)

                def load_queries(n, j):
                    kq_g = kq_d.rearrange("b g a k (h d) n -> (b g) a k d h n", d=DH)[n]
                    rel_g = rel_d.rearrange("b g w a (j h) n -> (b g) w a j h n", h=HG)[n]
                    va_g = va_d.rearrange("b g p c -> (b g) p c")[n]
                    for part in range(2):
                        for half in range(2):
                            dst = bits(qf[j][:])
                            r = ROW_W[part]
                            sp.dma_start(dst[r:r + W, :, half, :], rel_g[0, part]).then_inc(loaded[j], 16)
                            r = ROW_H[part]
                            sp.dma_start(dst[r:r + H // 2, :, half, :], rel_g[1, part, half * H // 2:(half + 1) * H // 2]
                                         ).then_inc(loaded[j], 16)
                    for row, qpart in enumerate((0, 0, 1)):
                        r = ROW_Q + DH * row
                        for half in range(2):
                            sp.dma_start(bits(qf[j][:])[r:r + DH, :, half, :], kq_g[qpart, 1]).then_inc(loaded[j], 16)
                    sp.dma_start(va[j][:].rearrange("p t h c -> p (t h c)"), va_g).then_inc(loaded[j], 16)

                def load_keys(n, j):
                    kq_g = kq_d.rearrange("b g a k (h d) n -> (b g) a k d h n", d=DH)[n]
                    for row, kpart in enumerate((0, 1, 0)):
                        r = ROW_Q + DH * row
                        sp.dma_start(bits(kf[j][:])[r:r + DH], kq_g[kpart, 0]).then_inc(loaded[j], 16)

                def maxima(n, j, opening=False):
                    for h in range(HG):
                        for half in range(2):
                            if half == 0:
                                sp.wait_ge(sm_read, NU - HG + h + 1 if opening else n * NU + turn_at[h] + 1)
                            sp.dma_start(bits(qf[j][:])[ROW_M:ROW_M + 1, h, half, :].rearrange("a (t p) -> a t p", p=P),
                                         bits(mrow[:, h, :])).then_inc(max_loaded[h], 16)

                def period(n, j, more, ahead):
                    if ahead:
                        load(n + 2, (j + 2) % BUFS)
                    if more:
                        maxima(n + 1, (j + 1) % BUFS)
                    sp.wait_ge(out_ready, n + 2)
                    sp.dma_start(att_d.rearrange("b g p n -> (b g) p n")[n], out[:]).then_inc(out_stored, 16)

                sp.sem_inc(out_stored, 16)
                load_queries(0, 0)
                sp.wait_ge(built[0], 1)
                load_keys(0, 0)
                load_queries(1, 1)
                for buf in built[1:]:
                    sp.wait_ge(buf, 1)
                load_keys(1, 1)
                maxima(0, 0, opening=True)
                all_groups(sp, period)
                sp.wait_ge(out_stored, 16 * (NG + 1))

            @block.gpsimd
            def _(pool):
                nc.gpsimd.memset(ones_hot[:], 0.0)
                pool.drain()
                xs, ys = [[0, H], [-1, W]], [[0, 2], [-1, H // 2], [0, W]]
                for base, pattern in ((ROW_W[0], xs), (ROW_W[1], xs), (ROW_H[0], ys), (ROW_H[1], ys), (ROW_M, [[0, TOK]])):
                    nc.gpsimd.affine_select(out=ones_hot[:], in_=ones_hot[:], compare_op=ALU.not_equal, fill=1.0, base=-base,
                                            pattern=pattern, channel_multiplier=1)
                    pool.drain()
                nc.gpsimd.sem_inc(made, 1)
                make_identity(nc, pool, ident[:], made)

            @block.scalar
            def _(act):
                def period(n, j, more, ahead):
                    for u in range(NS):
                        t, h, half = u // (2 * HG), u // 2 % HG, u % 2
                        act.wait_ge(st_done, n * NS + u + 1)
                        if h == half == 0:
                            act.wait_ge(pv_done, n * TT + t + 1)
                        nc.scalar.activation(probs[:, t % 2, h, half * HALF:(half + 1) * HALF], second_bank(j, u), ACT.Exp
                                             ).then_inc(exp_done, 1)
                    act.wait_ge(pv_done, n * TT + TT + 2)
                    act.wait_ge(out_stored, n * 16 + 16)
                    nc.scalar.activation(out[:], pv[:], ACT.Copy).then_inc(out_ready, 1)

                act.wait_ge(made, 1)
                for buf, done in zip(kf[1:], built[1:]):
                    for h in range(HG):
                        last = nc.scalar.activation(buf[:, h, :], ones_hot[:], ACT.Copy)
                    last.then_inc(done, 1)
                all_groups(act, period)

            @block.vector
            def _(dve):
                def opening():
                    for k in range(STEPS):
                        dve.wait_ge(wide_done, k + 1)
                        h, t = k // TT, k % TT
                        nc.vector.tensor_reduce(nmax[:, h, t:t + 1], wide[k % 2].rearrange("p a n -> p (a n)"), axis=AX.X, op=ALU.max, negate=True).then_inc(wide_read, 1)
                        if t == LATE and h:
                            maximum_row(h - 1)
                    maximum_row(HG - 1)

                def maximum_row(h):
                    dve.wait_ge(sm_done, NU - HG + h + 1)
                    nc.vector.tensor_copy(mrow[:, h, :], sm[1 + h % 2][0:TT, 0:P]).then_inc(sm_read, 1)

                def first_pass(n, j):
                    for k, (what, h, u) in enumerate(units):
                        dve.wait_ge(sm_done, n * NU + k + 1)
                        if what == "logits":
                            nc.vector.tensor_reduce(pmax[:, h % 2, u // 2, u % 2:u % 2 + 1], first_bank(j, k), axis=AX.X, op=ALU.max
                                                    ).then_inc(sm_read, 1)
                            if u == 2 * TT - 1:
                                dve.drain()
                                nc.vector.tensor_reduce(nmax[:, h, :], pmax[:, h % 2], axis=AX.X, op=ALU.max, negate=True
                                                        ).then_inc(nmax_ready, 1)
                        else:
                            dve.wait_ge(max_loaded[h], n * 32)
                            nc.vector.tensor_copy(mrow[:, h, :], first_bank(j, k)[0:TT, 0:P]).then_inc(sm_read, 1)

                def period(n, j, more, ahead):
                    if more:
                        first_pass(n + 1, (j + 1) % BUFS)

                dve.wait_ge(made, 1)
                for h in range(HG):
                    last = nc.vector.tensor_copy(kf[0][:, h, :], ones_hot[:])
                last.then_inc(built[0], 1)
                opening()
                all_groups(dve, period)

            @block.tensor
            def _(pe):
                def opening():
                    for k in range(STEPS):
                        h, t = k // TT, k % TT
                        if k >= 2:
                            pe.wait_ge(wide_read, k - 1)
                        for half in range(2):
                            cols = slice(half * HALF, (half + 1) * HALF)
                            m = nc.tensor.matmul(wide[k % 2][:, half], qf[0][0:ROW_M, h, half, t * P:(t + 1) * P],
                                                 kf[0][0:ROW_M, h, cols], start=True, stop=True)
                        m.then_inc(wide_done, 1)
                        if t == LATE and h:
                            turn(h - 1)
                    turn(HG - 1)
                    pe.wait_ge(wide_read, STEPS)

                def turn(h):
                    pe.wait_ge(wide_read, (h + 1) * TT)
                    pe.wait_ge(sm_read, NU - HG + h - 1)
                    nc.tensor.transpose(sm[1 + h % 2][0:TT, 0:P], nmax[:, h, :], ident[:]).then_inc(sm_done, 1)

                def first_pass_unit(n, j, k):
                    what, h, u = units[k]
                    pe.wait_ge(sm_read, n * NU + k - 2)
                    if what == "logits":
                        t, half = u // 2, u % 2
                        nc.tensor.matmul(first_bank(j, k), qf[j][0:ROW_M, h, half, t * P:(t + 1) * P],
                                         kf[j][0:ROW_M, h, half * HALF:(half + 1) * HALF], start=True, stop=True).then_inc(sm_done, 1)
                    else:
                        pe.wait_ge(nmax_ready, n * HG + h + 1)
                        nc.tensor.transpose(first_bank(j, k)[0:TT, 0:P], nmax[:, h, :], ident[:]).then_inc(sm_done, 1)

                def weighted(n, j, t, quarter):
                    if quarter == 0:
                        pe.wait_ge(exp_done, n * NS + 2 * HG * (t + 1) + 3)
                        if t == 0:
                            pe.wait_ge(out_ready, n + 1)
                    cols = slice(quarter * TOK // HG, (quarter + 1) * TOK // HG)
                    for h in range(HG):
                        m = nc.tensor.matmul(pv[32 * h:32 * h + 32, cols], va[j][:, t, h, :], probs[:, t % 2, h, cols],
                                             start=t == 0 and quarter % 2 == 0, stop=t == TT - 1, skip_group_check=True)
                    if quarter == HG - 1:
                        m.then_inc(pv_done, 1)

                def period(n, j, more, ahead):
                    j1 = (j + 1) % BUFS
                    if more:
                        pe.wait_ge(loaded[j1], (n - j + BUFS * ((j + 1) // BUFS + 1)) * (16 * LOADS // BUFS))
                    for s in range(STEPS):
                        t, h = s // HG, s % HG
                        for half in range(2):
                            pe.wait_ge(exp_done, n * NS + 2 * s + half + 1)
                            if t == half == 0:
                                pe.wait_ge(max_loaded[h], n * 32 + 32)
                            nc.tensor.matmul(second_bank(j, 2 * s + half), kf[j][0:ROW_M + 1, h, t * P:(t + 1) * P],
                                             qf[j][0:ROW_M + 1, h, 2 * t // TT, half * HALF:(half + 1) * HALF],
                                             start=True, stop=True).then_inc(st_done, 1)
                        if more:
                            first_pass_unit(n + 1, j1, 2 * s)
                        if t:
                            weighted(n, j, t - 1, h)
                        if more:
                            first_pass_unit(n + 1, j1, 2 * s + 1)
                    for quarter in range(HG):
                        weighted(n, j, TT - 1, quarter)
                        if more:
                            first_pass_unit(n + 1, j1, 2 * STEPS + quarter)

                pe.sem_inc(exp_done, 3)
                pe.sem_inc(pv_done, 2)
                pe.sem_inc(out_ready, 1)
                pe.sem_inc(sm_done, NU - HG)
                pe.sem_inc(sm_read, NU - HG)
                pe.sem_inc(nmax_ready, HG)
                pe.wait_ge(made, 2)
                pe.wait_ge(loaded[0], 16 * LOADS)
                opening()
                pe.wait_ge(sm_read, NU)
                all_groups(pe, period)


def self_attention_phase(nc, x, attn_w, attn_b, w_q, w_k, w_v, w_o, b_o, mixT_d, att_d, rsum_d, t_d, vT_d, vsum_d):
    with ExitStack() as ctx:
        sb = lambda name, shape, dt=f32: ctx.enter_context(nc.sbuf_tensor(name, shape, dt))
        ps = lambda name, n: ctx.enter_context(nc.psum_tensor(name, [P, n], f32))
        sem = lambda name: ctx.enter_context(nc.semaphore(name))
        QT = TT // 2
        ident = sb("b_ident", [P, P])
        wp = sb("b_wp", [P, GROUPS, DK])
        pb = sb("b_pb", [P, 1])
        w_st = sb("b_w_st", [P, KC, 3, U])
        w_hi, w_lo = sb("b_w_hi", [P, KC, 3, U], f32r), sb("b_w_lo", [P, KC, 3, U], f32r)
        wo = sb("b_wo", [P, C])
        bo = sb("b_bo", [P, C])
        rs = sb("b_rs", [P, B, TOK // 16])
        att = [sb(f"b_att{j}", [P, GROUPS, HALF]) for j in range(2)]
        rsb = [sb(f"b_rsb{j}", [P, GROUPS, HALF]) for j in range(2)]
        mixT = sb("b_mixT", [P, KC, TOK])
        xb = [sb(f"b_xb{s}", [P, TT, C]) for s in range(2)]
        st6, mv = sb("b_st6", [P, QT, 6]), sb("b_mv", [P, QT, 2])
        var, rstd, tmp, shift = (sb(f"b_{n}", [P, 2, QT]) for n in ("var", "rstd", "tmp", "shift"))
        u = sb("b_u", [P, QT, C])
        uT_hi, uT_lo = sb("b_uT_hi", [P, KC, TOK], f32r), sb("b_uT_lo", [P, KC, TOK], f32r)
        q_hi = [sb(f"b_q_hi{s}", [P, TOK], f32r) for s in range(2)]
        q_lo = [sb(f"b_q_lo{s}", [P, TOK], f32r) for s in range(2)]
        k_hi = [sb(f"b_k_hi{s}", [P, TOK], f32r) for s in range(2)]
        k_lo = [sb(f"b_k_lo{s}", [P, TOK], f32r) for s in range(2)]
        vT32 = sb("b_vT32", [P, HALF])
        v_sb = [sb(f"b_v{s}", [P, TT, U]) for s in range(2)]
        nmax, ssum, rsum = sb("b_nmax", [P, TT]), sb("b_ssum", [P, TT]), sb("b_rsum", [P, TT])
        probs = [sb(f"b_probs{i}", [P, TOK]) for i in range(2)]
        pT = [sb(f"b_pT{i}", [P, TT, 2 * P]) for i in range(2)]
        oT = [sb(f"b_oT{i}", [P, 2 * P]) for i in range(2)]
        t_sb = [sb(f"b_t{j}", [P, QT, C]) for j in range(2)]
        st6t, mvt = sb("b_st6t", [P, QT, 6]), sb("b_mvt", [P, QT, 2])
        vart, rstdt, tmpt = (sb(f"b_{n}", [P, 2, QT]) for n in ("vart", "rstdt", "tmpt"))
        v2 = sb("b_v2", [P, QT, C])
        v2T = sb("b_v2T", [P, KC, HALF])
        vsum = sb("b_vsum", [P, KC, TT // 2])
        s_ps, pT_ps, o_ps = ps("b_s_ps", TOK), ps("b_pT_ps", TOK), ps("b_o_ps", 2 * P)
        a_ps, b_ps, c_ps = ps("b_a_ps", 2 * C), ps("b_b_ps", HALF), ps("b_c_ps", 2 * C)
        consts, w_loaded, w_split = sem("b_consts"), sem("b_w_loaded"), sem("b_w_split")
        sums_loaded = [sem(f"b_sums_loaded{i}") for i in range(2)]
        sums_inv, sums_stored = sem("b_sums_inv"), sem("b_sums_stored")
        att_loaded = [sem(f"b_att_loaded{j}") for j in range(2)]
        x_loaded = [sem(f"b_x_loaded{j}") for j in range(2)]
        mix_loaded, norm_ready = sem("b_mix_loaded"), sem("b_norm_s")
        a_done, a_read, b_done, b_read, c_done = (sem(f"b_{n}") for n in ("a_done", "a_read", "b_done", "b_read", "c_done"))
        c_read = sem("b_c_read")
        var_ready, rstd_ready, shift_ready, u_ready, res_ready = (sem(f"b_{n}_s") for n in ("var", "rstd", "shift", "u", "res"))
        uhi_ready, bhi_ready = sem("b_uhi_s"), sem("b_bhi_s")
        s_done, max_ready, exp_done = sem("b_s_done"), sem("b_max_s"), sem("b_exp_done")
        pT_done, pT_ready = sem("b_pT_done"), sem("b_pT_s")
        o_done, o_read = sem("b_o_done"), sem("b_o_read")
        vart_ready, rstdt_ready, v_ready = (sem(f"b_{n}_s") for n in ("vart", "rstdt", "v"))
        t_stored = [sem(f"b_t_stored{j}") for j in range(2)]
        vT_stored, vsum_stored = sem("b_vT_stored"), sem("b_vsum_stored")

        A_STEPS = [("mix", 0), ("mix", 1), ("mix", 2), ("mix", 3), ("ut", 0), ("ut", 1), ("v", 0), ("vt", 0),
                   ("ut", 2), ("ut", 3), ("v", 1), ("vt", 1)]
        B_STEPS = [("proj", 0), ("proj", 1), ("q", 0), ("k", 0), ("q", 1), ("k", 1)]
        HI_STEPS = B_STEPS[2:]
        C_STEPS = [("out", 0), ("out", 1), ("out", 2), ("turn", 0), ("turn", 1), ("out", 3), ("turn", 2), ("turn", 3)]
        PAIRS = TT // 2
        NA, NB, NCS = len(A_STEPS), len(B_STEPS), len(C_STEPS)
        a_at = lambda what, j: A_STEPS.index((what, j))
        b_at = lambda what, j: B_STEPS.index((what, j))
        c_at = lambda what, t: C_STEPS.index((what, t))
        W_OF = {"q": 0, "k": 1, "v": 2}
        SCALE = U ** -0.5

        BETWEEN = [
            [("probs", 7, -1), ("out", 2, -1), ("vt", 1, 0), ("proj", 0, 1), ("turn", 0, -1)],
            [("probs", 0, 0), ("half", 3, -1), ("values", 3, -1), ("mix", 0, 1), ("turn", 1, -1)],
            [("probs", 1, 0), ("out", 3, -1), ("mix", 1, 1), ("vvar", 1, -1), ("proj", 1, 1)],
            [("probs", 2, 0), ("var", 0, 1), ("half", 0, 0), ("mix", 2, 1), ("apply", 0, 1), ("values", 0, 0), ("mix", 3, 1)],
            [("probs", 3, 0), ("vapply", 1, -1), ("ut", 0, 1), ("turn", 2, -1), ("ut", 1, 1), ("turn", 3, -1), ("q", 0, 1)],
            [("probs", 4, 0), ("var", 1, 1), ("v", 0, 1), ("k", 0, 1), ("half", 1, 0), ("values", 1, 0), ("apply", 1, 1), ("vt", 0, 1)],
            [("probs", 5, 0), ("out", 0, 0), ("ut", 2, 1), ("out", 1, 0), ("ut", 3, 1)],
            [("probs", 6, 0), ("vvar", 0, 0), ("q", 1, 1), ("half", 2, 0), ("values", 2, 0), ("k", 1, 1), ("vapply", 0, 0), ("v", 1, 1)]]

        FRONT = [("proj", 0), ("proj", 1), ("mix", 0), ("mix", 1), ("mix", 2), ("var", 0), ("mix", 3), ("apply", 0), ("var", 1),
                 ("ut", 0), ("ut", 1), ("apply", 1), ("q", 0), ("k", 0), ("v", 0), ("vt", 0), ("ut", 2), ("ut", 3), ("q", 1), ("k", 1), ("v", 1)]

        def period(b, s, before, after):
            steps = []
            for i in range(TT):
                steps.append(("scores", i, b, s))
                steps += [(what, k, b + d, s if d == 0 else 1 - s) for what, k, d in BETWEEN[i]
                          if d == 0 or (d == 1 and after) or (d == -1 and before)]
            return steps

        def all_images(eng, run):
            run([(what, k, 0, 0) for what, k in FRONT])
            run(period(0, 0, False, True))
            with eng.Fori(1, B - 1, 2) as b:
                run(period(b, 1, True, True))
                run(period(b + 1, 0, True, True))
            run(period(B - 1, 1, True, False))
            run([(what, k, B - 1, 1) for slot in BETWEEN for what, k, d in slot if d == -1])

        half = lambda j: slice(j * HALF, (j + 1) * HALF)
        tile = lambda t: slice(t * P, (t + 1) * P)
        pair = lambda t: slice(2 * t, 2 * t + 2)
        cols = lambda t: slice(2 * t * P, 2 * (t + 1) * P)
        by_tile = lambda ap: ap.rearrange("p (t c) -> p t c", t=2)
        by_chunk = lambda ap: ap.rearrange("p (c n) -> p c n", c=KC)

        with nc.Block() as block:
            @block.sync
            def _(sp):
                x_v = x.rearrange("b h w c -> b (h w) c").rearrange("b (t p) c -> b p t c", p=P)
                t_v = t_d.rearrange("b (t p) c -> b p t c", p=P)
                vT_v = vT_d.rearrange("b c p n -> b p c n")
                def load_att(n, j, wait=True):
                    if wait:
                        sp.wait_ge(b_done, n * NB - NB + j + 1)
                        sp.nop(nofuse=True)
                    sp.dma_start(att[j][:], att_d[n].rearrange("g p n -> p g n")[:, :, half(j)]).then_inc(att_loaded[j], 16)
                    for g in range(GROUPS):
                        src = rsum_d[n, g].rearrange("h (a n) -> h a n", a=1)[:, :, half(j)]
                        sp.dma_start(rsb[j][:, g], src.to_broadcast([HG, 32, HALF])).then_inc(att_loaded[j], 16)

                def load_mix(n, wait=True):
                    if wait:
                        sp.wait_ge(a_done, n * NA - NA + a_at("mix", 3) + 1)
                        sp.nop(nofuse=True)
                    sp.dma_start(mixT[:, 0, :], mixT_d[n, 0]).then_inc(mix_loaded, 16)
                    sp.dma_start(mixT[0:CONV_OUT - P, 1, :], mixT_d[n, 1, 0:CONV_OUT - P]).then_inc(mix_loaded, 16)

                def load_x(n, s, j, wait=True):
                    if wait:
                        sp.wait_ge(c_read, (n - 2) * NCS + c_at("out", 2 * j + 1) + 2)
                        sp.nop(nofuse=True)
                    sp.dma_start(xb[s][:, j * QT:(j + 1) * QT, :], x_v[n, :, j * QT:(j + 1) * QT, :]).then_inc(x_loaded[j], 16)

                def store_t(n, j):
                    sp.wait_ge(c_read, n * NCS + c_at("out", 2 * j + 1) + 2)
                    sp.nop(nofuse=True)
                    sp.dma_start(t_v[n, :, j * QT:(j + 1) * QT, :], t_sb[j][:]).then_inc(t_stored[j], 16)

                def store_v(n, j):
                    sp.wait_ge(c_read, n * NCS + c_at("turn", 2 * j + 1) + 2)
                    sp.nop(nofuse=True)
                    sp.dma_start(vT_v[n, :, :, half(j)], v2T[:]).then_inc(vT_stored, 16)
                    if j == 1:
                        sp.dma_start(vsum_d[n], vsum[:]).then_inc(vsum_stored, 16)

                def image(b, s, before, after, ahead):
                    if before:
                        store_v(b - 1, 0)
                        if after:
                            load_x(b + 1, 1 - s, 1)
                        store_t(b - 1, 1)
                    if ahead:
                        load_att(b + 2, 0)
                        load_att(b + 2, 1)
                        load_mix(b + 2)
                    if before:
                        store_v(b - 1, 1)
                    store_t(b, 0)
                    if ahead:
                        load_x(b + 2, s, 0)

                def load_sums(b):
                    src = att_d[b].rearrange("g (h r) n -> (g h) r n", r=32)[:, DH].rearrange("q (j c) -> q j c", j=16)
                    sp.dma_start(rs[:, b], src).then_inc(sums_loaded[min(b, 1)], 16)

                load_sums(0)
                load_mix(0, False)
                for j in range(2):
                    load_x(0, 0, j, False)
                sp.wait_ge(sums_inv, 1)
                sp.dma_start(rsum_d[0].rearrange("g h (j c) -> (g h j) c", j=16), rs[:, 0]).then_inc(sums_stored, 16)
                for b in range(1, B):
                    load_sums(b)
                for stored in t_stored:
                    sp.sem_inc(stored, 16)
                sp.sem_inc(vT_stored, 16)
                sp.sem_inc(vsum_stored, 16)
                sp.wait_ge(sums_stored, 16)
                for j in range(2):
                    load_att(0, j, False)
                sp.wait_ge(sums_inv, 2)
                sp.dma_start(rsum_d[1:B].rearrange("b g h (j c) -> (g h j) b c", j=16), rs[:, 1:B]).then_inc(sums_stored, 16)
                for j in range(2):
                    load_x(1, 1, j, False)
                sp.wait_ge(sums_stored, 32)
                for j in range(2):
                    load_att(1, j)
                load_mix(1)
                image(0, 0, False, True, True)
                with sp.Fori(1, B - 3, 2) as b:
                    image(b, 1, True, True, True)
                    image(b + 1, 0, True, True, True)
                image(B - 3, 1, True, True, True)
                image(B - 2, 0, True, True, False)
                image(B - 1, 1, True, False, False)
                store_v(B - 1, 0)
                store_t(B - 1, 1)
                store_v(B - 1, 1)
                for stored in t_stored:
                    sp.wait_ge(stored, 16 * (B + 1))
                sp.wait_ge(vT_stored, 16 * (2 * B + 1))
                sp.wait_ge(vsum_stored, 16 * (B + 1))

            @block.gpsimd
            def _(pool):
                nc.gpsimd.memset(wp[:], 0.0).then_inc(consts, 1)
                make_identity(nc, pool, ident[:], consts)

                def run(steps):
                    for what, k, n, s in steps:
                        if what == "proj":
                            pool.wait_ge(att_loaded[k], n * (16 * (1 + GROUPS)) + 16 * (1 + GROUPS))
                            nc.gpsimd.tensor_tensor(att[k][:], att[k][:], rsb[k][:], ALU.mult).then_inc(norm_ready, 1)
                        if what == "apply":
                            x1 = xb[s][:, k * QT:(k + 1) * QT, :]
                            pool.wait_ge(u_ready, n * 2 + k + 1)
                            nc.gpsimd.tensor_tensor(x1, x1, u[:], ALU.add)
                            pool.drain()
                            nc.gpsimd.tensor_tensor(x1, x1, bo_all, ALU.add).then_inc(res_ready, 1)

                bo_all = bo[:].rearrange("p (a c) -> p a c", a=1).to_broadcast([P, QT, C])
                pool.wait_ge(w_loaded, 16 * (NH + 6))
                all_images(pool, run)

            @block.scalar
            def _(act):
                def rsqrt(out, in_):
                    nc.scalar.activation(out, in_, ACT.Ln)
                    act.drain()
                    return nc.scalar.activation(out, out, ACT.Exp, scale=-0.5)

                def run(steps):
                    for what, k, n, s in steps:
                        if what == "scores":
                            act.wait_ge(max_ready, n * TT + k + 1)
                            nc.scalar.activation(probs[k % 2][:], s_ps[:], ACT.Exp, bias=nmax[:, k:k + 1], accum_out=ssum[:, k:k + 1]
                                                 ).then_inc(exp_done, 1)
                        elif what == "probs":
                            act.wait_ge(pT_done, n * TT + k + 1)
                            nc.scalar.activation(pT[k // 2 % 2][:, :, tile(k % 2)], pT_ps[:].rearrange("p (t q) -> p t q", t=TT),
                                                 ACT.Copy).then_inc(pT_ready, 1)
                        elif what == "values":
                            act.wait_ge(o_done, n * PAIRS + k + 1)
                            nc.scalar.activation(oT[k % 2][:], o_ps[:], ACT.Copy).then_inc(o_read, 1)
                        elif what == "proj":
                            act.wait_ge(b_done, n * NB + b_at("proj", k) + 1)
                            nc.scalar.activation(mixT[DK:P, 1, half(k)], b_ps[DK:P, :], ACT.Identity, bias=pb[DK:P]
                                                 ).then_inc(b_read, 1)
                        elif what == "var":
                            act.wait_ge(var_ready, n * 2 + k + 1)
                            rsqrt(rstd[:, k], var[:, k]).then_inc(rstd_ready, 1)
                        elif what == "vvar":
                            act.wait_ge(vart_ready, n * 2 + k + 1)
                            rsqrt(rstdt[:, k], vart[:, k]).then_inc(rstdt_ready, 1)
                        elif what == "apply":
                            act.wait_ge(shift_ready, n * 2 + k + 1)
                            act.wait_ge(res_ready, n * 2 + k + 1)
                            if k:
                                act.wait_ge(a_done, n * NA + a_at("ut", 1) + 1)
                            for i in range(QT):
                                last = nc.scalar.activation(u[:, i, :], xb[s][:, k * QT + i, :], ACT.Identity,
                                                            bias=shift[:, k, i:i + 1], scale=rstd[:, k, i:i + 1])
                            last.then_inc(u_ready, 1)
                        elif what == "ut":
                            act.wait_ge(a_done, n * NA + a_at("ut", k) + 1)
                            nc.scalar.activation(uT_hi[:, :, cols(k)], by_chunk(a_ps[:]), ACT.Copy).then_inc(uhi_ready, 1)
                        elif what in ("q", "k"):
                            act.wait_ge(b_done, n * NB + b_at(what, k) + 1)
                            hi = q_hi if what == "q" else k_hi
                            nc.scalar.activation(hi[s][:, half(k)], b_ps[:], ACT.Copy, scale=SCALE if what == "q" else 1.0
                                                 ).then_inc(bhi_ready, 1)
                        elif what == "v":
                            act.wait_ge(a_done, n * NA + a_at("v", k) + 1)
                            nc.scalar.activation(vT32[:], a_ps[:], ACT.Copy).then_inc(a_read, 1)
                        elif what == "vt":
                            act.wait_ge(a_done, n * NA + a_at("vt", k) + 1)
                            nc.scalar.activation(v_sb[s][:, k * QT:(k + 1) * QT, :], a_ps[:].rearrange("p (t u) -> p t u", u=U),
                                                 ACT.Copy).then_inc(a_read, 1)
                        elif what == "turn":
                            act.wait_ge(c_done, n * NCS + c_at("turn", k) + 1)
                            if k % 2 == 0:
                                act.wait_ge(vT_stored, n * 32 + 16 * (k // 2) + 16)
                            if k == 0:
                                act.wait_ge(vsum_stored, n * 16 + 16)
                            for c in range(KC):
                                last = nc.scalar.activation(v2T[:, c, cols(k % 2)], by_chunk(c_ps[:])[:, c], ACT.Copy,
                                                            accum_out=vsum[:, c, k:k + 1])
                            last.then_inc(c_read, 1)

                act.wait_ge(consts, 2)
                for g in range(GROUPS):
                    for h in range(HG):
                        act.dma_start(wp[32 * h:32 * h + DH, g], attn_w[(g * HG + h) * DH:(g * HG + h + 1) * DH]).then_inc(w_loaded, 16)
                act.dma_start(pb[DK:P], attn_b.rearrange("(p a) -> p a", a=1)).then_inc(w_loaded, 16)
                for i, w in enumerate((w_q, w_k, w_v)):
                    act.dma_start(w_st[:, :, i], w.rearrange("(k p) u -> p k u", p=P)).then_inc(w_loaded, 16)
                act.dma_start(wo[:], w_o).then_inc(w_loaded, 16)
                act.dma_start(bo[:], b_o.rearrange("(a c) -> a c", a=1).to_broadcast([P, C])).then_inc(w_loaded, 16)
                nc.scalar.preload_act_table_set("natural_log_exp_and_others")
                act.wait_ge(w_loaded, 16 * (NH + 6))
                all_images(act, run)

            @block.vector
            def _(dve):
                def spread(buf, st, m, v, ready):
                    dve.drain()
                    for i in range(QT):
                        nc.vector.bn_stats(st[:, i, :], buf[:, i, :])
                    dve.drain()
                    for i in range(QT):
                        nc.vector.bn_aggr(m[:, i, :], st[:, i, :])
                    dve.drain()
                    nc.vector.tensor_scalar(v, m[:, :, 1], 1e-5, None, ALU.add).then_inc(ready, 1)

                def scales(m, r, v, tm, sh, ready):
                    newton(nc, dve, r, v, tm)
                    nc.vector.scalar_tensor_tensor(sh, m[:, :, 0], -1.0, r, ALU.mult, ALU.mult).then_inc(ready, 1)

                def run(steps):
                    for what, k, n, s in steps:
                        if what == "scores":
                            dve.wait_ge(s_done, n * TT + k + 1)
                            nc.vector.tensor_reduce(nmax[:, k:k + 1], s_ps[:], axis=AX.X, op=ALU.max, negate=True).then_inc(max_ready, 1)
                        elif what == "values":
                            dve.wait_ge(exp_done, n * TT + (k + 1) * 2 + 1)
                            nc.vector.reciprocal(rsum[:, pair(k)], ssum[:, pair(k)])
                            dve.drain()
                        elif what == "mix":
                            dve.wait_ge(a_done, n * NA + a_at("mix", k) + 1)
                            dve.wait_ge(x_loaded[k // 2], n * 16 + 16)
                            nc.vector.tensor_tensor(xb[s][:, pair(k), :], by_tile(a_ps[:]), xb[s][:, pair(k), :], ALU.add).then_inc(a_read, 1)
                        elif what == "var":
                            spread(xb[s][:, k * QT:(k + 1) * QT, :], st6, mv, var[:, k], var_ready)
                        elif what == "vvar":
                            spread(t_sb[k], st6t, mvt, vart[:, k], vart_ready)
                        elif what == "apply":
                            dve.wait_ge(rstd_ready, n * 2 + k + 1)
                            scales(mv, rstd[:, k], var[:, k], tmp[:, k], shift[:, k], shift_ready)
                        elif what == "vapply":
                            dve.wait_ge(rstdt_ready, n * 2 + k + 1)
                            newton(nc, dve, rstdt[:, k], vart[:, k], tmpt[:, k])
                            for i in range(QT):
                                last = nc.vector.tensor_scalar(v2[:, i, :], t_sb[k][:, i, :], mvt[:, i, 0:1], rstdt[:, k, i:i + 1],
                                                               ALU.subtract, ALU.mult)
                            last.then_inc(v_ready, 1)
                        elif what == "ut":
                            dve.wait_ge(uhi_ready, n * PAIRS + k + 1)
                            nc.vector.tensor_tensor(uT_lo[:, :, cols(k)], by_chunk(a_ps[:]), bits(uT_hi[:, :, cols(k)]), ALU.subtract).then_inc(a_read, 1)
                        elif what in ("q", "k"):
                            dve.wait_ge(bhi_ready, n * len(HI_STEPS) + HI_STEPS.index((what, k)) + 1)
                            hi, lo = (q_hi, q_lo) if what == "q" else (k_hi, k_lo)
                            nc.vector.scalar_tensor_tensor(lo[s][:, half(k)], b_ps[:], SCALE if what == "q" else 1.0,
                                                           bits(hi[s][:, half(k)]), ALU.mult, ALU.subtract).then_inc(b_read, 1)
                        elif what == "out":
                            dve.wait_ge(c_done, n * NCS + c_at("out", k) + 1)
                            if k % 2 == 0:
                                dve.wait_ge(res_ready, n * 2 + k // 2 + 2)
                                dve.wait_ge(t_stored[k // 2], n * 16 + 16)
                            for t in range(2 * k, 2 * k + 2):
                                last = nc.vector.scalar_tensor_tensor(t_sb[k // 2][:, t % QT, :], by_tile(c_ps[:])[:, t % 2, :], rsum[:, t:t + 1],
                                                                      xb[s][:, t, :], ALU.mult, ALU.add)
                            last.then_inc(c_read, 1)

                dve.sem_inc(res_ready, 1)
                dve.wait_ge(sums_loaded[0], 16)
                nc.vector.reciprocal(rs[:, 0], rs[:, 0]).then_inc(sums_inv, 1)
                dve.wait_ge(w_loaded, 16 * (NH + 6))
                nc.vector.tensor_copy(w_hi[:], w_st[:])
                dve.drain()
                nc.vector.tensor_tensor(w_lo[:], w_st[:], bits(w_hi[:]), ALU.subtract).then_inc(w_split, 1)
                dve.wait_ge(sums_loaded[1], 16 * (B - 1))
                nc.vector.reciprocal(rs[:, 1:B], rs[:, 1:B]).then_inc(sums_inv, 1)
                all_images(dve, run)

            @block.tensor
            def _(pe):
                def run(steps):
                    for what, k, n, s in steps:
                        if what == "scores":
                            pe.wait_ge(exp_done, n * TT + k + 1)
                            if k == 0:
                                pe.wait_ge(b_read, n * NB + b_at("k", 1) + 2)
                            for j in range(2):
                                for i, (q, kk) in enumerate(((q_hi, k_hi), (q_hi, k_lo), (q_lo, k_hi))):
                                    m = nc.tensor.matmul(s_ps[:, half(j)], q[s][:, tile(k)], kk[s][:, half(j)], start=i == 0, stop=i == 2)
                            m.then_inc(s_done, 1)
                        elif what == "probs":
                            pe.wait_ge(exp_done, n * TT + k + 2)
                            pe.wait_ge(pT_ready, n * TT + k + 1)
                            for t in range(TT):
                                m = nc.tensor.transpose(pT_ps[:, tile(t)], probs[k % 2][:, tile(t)], ident[:])
                            m.then_inc(pT_done, 1)
                        elif what in ("half", "values"):
                            if what == "half":
                                pe.wait_ge(pT_ready, n * TT + (k + 1) * 2 + 1)
                                pe.wait_ge(o_read, n * PAIRS + k + 1)
                                pe.wait_ge(a_read, n * NA + NA + 1)
                            for t in range(QT) if what == "half" else range(QT, TT):
                                m = nc.tensor.matmul(o_ps[:], v_sb[s][:, t, :], pT[k % 2][:, t, :], start=t == 0, stop=t == TT - 1)
                            if what == "values":
                                m.then_inc(o_done, 1)
                        elif what == "proj":
                            pe.wait_ge(norm_ready, n * 2 + k + 1)
                            pe.wait_ge(b_read, n * NB + b_at("proj", k) + 1)
                            for g in range(GROUPS):
                                m = nc.tensor.matmul(b_ps[DK:P, :], wp[:, g, :], att[k][:, g, :], start=g == 0, stop=g == GROUPS - 1)
                            m.then_inc(b_done, 1)
                        elif what == "mix":
                            pe.wait_ge(a_read, n * NA + a_at("mix", k) + 1)
                            if k == 0:
                                pe.wait_ge(mix_loaded, n * 32 + 32)
                            pe.wait_ge(b_read, n * NB + b_at("proj", k // 2) + 2)
                            for t in range(2):
                                for c in range(KC):
                                    m = nc.tensor.transpose(by_tile(a_ps[:])[:, t, tile(c)], mixT[:, c, tile(2 * k + t)], ident[:])
                            m.then_inc(a_done, 1)
                        elif what == "ut":
                            pe.wait_ge(a_read, n * NA + a_at("ut", k) + 1)
                            pe.wait_ge(u_ready, n * 2 + k // 2 + 1)
                            for t in range(2):
                                for c in range(KC):
                                    m = nc.tensor.transpose(by_chunk(a_ps[:])[:, c, tile(t)], u[:, (2 * k + t) % QT, tile(c)], ident[:])
                            m.then_inc(a_done, 1)
                        elif what in W_OF:
                            pe.wait_ge(a_read, n * NA + a_at("ut", 2 * k + 1) + 2)
                            if what == "v":
                                bank, done = a_ps, a_done
                                pe.wait_ge(a_read, n * NA + a_at("v", k) + 1)
                            else:
                                bank, done = b_ps, b_done
                                pe.wait_ge(b_read, n * NB + b_at(what, k) + 1)
                            i, total = 0, 3 * KC
                            for c in range(KC):
                                for w, uT in ((w_hi, uT_hi), (w_hi, uT_lo), (w_lo, uT_hi)):
                                    m = nc.tensor.matmul(bank[:], w[:, c, W_OF[what], :], uT[:, c, half(k)], start=i == 0, stop=i == total - 1)
                                    i += 1
                            m.then_inc(done, 1)
                        elif what == "vt":
                            pe.wait_ge(a_read, n * NA + a_at("vt", k) + 1)
                            for t in range(QT):
                                m = nc.tensor.transpose(a_ps[:, tile(t)], vT32[:, tile(t)], ident[:])
                            m.then_inc(a_done, 1)
                        elif what == "out":
                            pe.wait_ge(o_read, n * PAIRS + k + 2)
                            pe.wait_ge(c_read, n * NCS + c_at("out", k) + 1)
                            for t in range(2):
                                m = nc.tensor.matmul(by_tile(c_ps[:])[:, t], oT[k % 2][:, tile(t)], wo[:], start=True, stop=True)
                            m.then_inc(c_done, 1)
                        elif what == "turn":
                            pe.wait_ge(v_ready, n * 2 + k // 2 + 1)
                            pe.wait_ge(c_read, n * NCS + c_at("turn", k) + 1)
                            for t in range(2):
                                for c in range(KC):
                                    m = nc.tensor.transpose(by_chunk(c_ps[:])[:, c, tile(t)], v2[:, (2 * k + t) % QT, tile(c)], ident[:])
                            m.then_inc(c_done, 1)

                pe.sem_inc(exp_done, 1)
                pe.sem_inc(pT_ready, 1)
                pe.sem_inc(o_read, 1)
                pe.sem_inc(a_read, 1)
                pe.sem_inc(b_read, 1)
                pe.sem_inc(c_read, 1)
                pe.wait_ge(consts, 2)
                pe.wait_ge(w_loaded, 16 * (NH + 6))
                pe.wait_ge(w_split, 1)
                all_images(pe, run)


def router_phase(nc, w_r, b_r, vsum_d, wts_d, idx_d):
    CAPACITY = float(-(-B * TOK * 5 // (4 * E)))
    with ExitStack() as ctx:
        sb = lambda name, shape, dt=f32: ctx.enter_context(nc.sbuf_tensor(name, shape, dt))
        sem = lambda name: ctx.enter_context(nc.semaphore(name))
        parts = sb("r2_parts", [P, B, KC, TT // 2])
        vm = sb("r2_vm", [P, KC, B])
        wr = sb("r2_wr", [P, KC, E])
        br = sb("r2_br", [B, E])
        ones = sb("r2_ones", [B, B])
        lg, rw, scale = sb("r2_lg", [B, E]), sb("r2_rw", [B, E]), sb("r2_scale", [B, E])
        nmax, total = sb("r2_nmax", [B, 1]), sb("r2_total", [B, 1])
        best, idx = sb("r2_best", [B, 8]), sb("r2_idx", [B, 8], mybir.dt.uint32)
        wts = sb("r2_wts", [B, TOPK])
        logits = ctx.enter_context(nc.psum_tensor("r2_logits", [B, E], f32))
        loads = ctx.enter_context(nc.psum_tensor("r2_loads", [B, E], f32))
        loaded, made, vm_ready, logits_done = sem("r2_loaded"), sem("r2_made"), sem("r2_vm_s"), sem("r2_logits_done")
        max_ready, exp_ready, rw_ready, loads_done = sem("r2_max_s"), sem("r2_exp_s"), sem("r2_rw_s"), sem("r2_loads_done")
        chosen, stored = sem("r2_chosen"), sem("r2_stored")

        with nc.Block() as block:
            @block.sync
            def _(sp):
                sp.dma_start(parts[:].rearrange("p b c f -> p b (c f)"), vsum_d.rearrange("b p c f -> p b (c f)")).then_inc(loaded, 16)
                sp.dma_start(wr[:], w_r.rearrange("(c p) e -> p c e", p=P)).then_inc(loaded, 16)
                sp.dma_start(br[:], b_r.rearrange("(a e) -> a e", a=1).to_broadcast([B, E])).then_inc(loaded, 16)
                sp.wait_ge(chosen, 1)
                sp.dma_start(wts_d, wts[:]).then_inc(stored, 16)
                sp.dma_start(idx_d, idx[:, 0:TOPK]).then_inc(stored, 16)
                sp.wait_ge(stored, 32)

            @block.scalar
            def _(act):
                for i, (out, in_) in enumerate(((rw, lg), (rw, lg), (wts, best[:, 0:TOPK]))):
                    act.wait_ge(max_ready, i + 1)
                    nc.scalar.activation(out[:], in_ if i == 2 else in_[:], ACT.Exp, bias=nmax[:], accum_out=total[:]
                                         ).then_inc(exp_ready, 1)

            @block.vector
            def _(dve):
                def softmax(out, in_, i):
                    nc.vector.tensor_reduce(nmax[:], in_, axis=AX.X, op=ALU.max, negate=True).then_inc(max_ready, 1)
                    dve.wait_ge(exp_ready, i + 1)
                    nc.vector.reciprocal(total[:], total[:])
                    dve.drain()
                    return nc.vector.tensor_scalar(out, out, total[:], None, ALU.mult)

                nc.vector.memset(ones[:], 1.0).then_inc(made, 1)
                dve.wait_ge(loaded, 48)
                nc.vector.tensor_reduce(vm[:].rearrange("p c b -> p b c"), parts[:], axis=AX.X, op=ALU.add).then_inc(vm_ready, 1)
                dve.wait_ge(logits_done, 1)
                nc.vector.scalar_tensor_tensor(lg[:], logits[:], 1.0 / TOK, br[:], ALU.mult, ALU.add)
                dve.drain()
                softmax(rw[:], lg[:], 0).then_inc(rw_ready, 1)
                dve.wait_ge(loads_done, 1)
                nc.vector.tensor_scalar(scale[:], loads[:], float(TOK), None, ALU.mult)
                dve.drain()
                nc.vector.reciprocal(scale[:], scale[:])
                dve.drain()
                nc.vector.tensor_scalar(scale[:], scale[:], CAPACITY, 1.0, ALU.mult, ALU.min)
                dve.drain()
                nc.vector.tensor_tensor(lg[:], rw[:], scale[:], ALU.mult)
                dve.drain()
                softmax(rw[:], lg[:], 1)
                dve.drain()
                nc.vector.max(best[:], rw[:])
                dve.drain()
                nc.vector.max_index(idx[:], best[:], rw[:])
                softmax(wts[:], best[:, 0:TOPK], 2).then_inc(chosen, 1)

            @block.tensor
            def _(pe):
                pe.wait_ge(vm_ready, 1)
                for c in range(KC):
                    m = nc.tensor.matmul(logits[:], vm[:, c, :], wr[:, c, :], start=c == 0, stop=c == KC - 1)
                m.then_inc(logits_done, 1)
                pe.wait_ge(made, 1)
                pe.wait_ge(rw_ready, 1)
                nc.tensor.matmul(loads[:], ones[:], rw[:], start=True, stop=True).then_inc(loads_done, 1)


def expert_phase(nc, w1, b1, w2, b2, gamma, beta, t_d, vT_d, wts_d, idx_d, out):
    with ExitStack() as ctx:
        sb = lambda name, shape, dt=f32: ctx.enter_context(nc.sbuf_tensor(name, shape, dt))
        ps = lambda name, n: ctx.enter_context(nc.psum_tensor(name, [P, n], f32))
        sem = lambda name: ctx.enter_context(nc.semaphore(name))
        HT = TT // 2
        UNITS = 2 * TOPK * FC
        LATE = 3
        NW = 2 * TOPK
        HB = 4
        ident = sb("x_ident", [P, P])
        gam, bet = sb("x_gam", [P, C]), sb("x_bet", [P, C])
        idx = sb("x_idx", [1, TOPK], mybir.dt.uint32)
        w1_st, w2_st = sb("x_w1_st", [P, TOPK, KC, F]), sb("x_w2_st", [P, TOPK, FC, C])
        w1_hi = [sb(f"x_w1_hi{s}", [P, TOPK, KC, F], f32r) for s in range(2)]
        w1_lo = [sb(f"x_w1_lo{s}", [P, TOPK, KC, F], f32r) for s in range(2)]
        w2_hi = [sb(f"x_w2_hi{s}", [P, TOPK, FC, C], f32r) for s in range(2)]
        w2_lo = [sb(f"x_w2_lo{s}", [P, TOPK, FC, C], f32r) for s in range(2)]
        b1_sb = [sb(f"x_b1{s}", [P, TOPK, FC]) for s in range(2)]
        b2_sb = [sb(f"x_b2{s}", [P, TOPK, KC]) for s in range(2)]
        wts = [sb(f"x_wts{s}", [P, TOPK]) for s in range(2)]
        b2w = [sb(f"x_b2w{s}", [P, KC]) for s in range(2)]
        vT = [sb(f"x_vT{s}", [P, KC, TOK]) for s in range(2)]
        v_hi = [sb(f"x_v_hi{s}", [P, KC, TOK], f32r) for s in range(2)]
        v_lo = [sb(f"x_v_lo{s}", [P, KC, TOK], f32r) for s in range(2)]
        t_sb = sb("x_t", [P, HT, C])
        hid = [sb(f"x_hid{i}", [P, HALF]) for i in range(2)]
        h_hi = [sb(f"x_h_hi{i}", [P, HALF], f32r) for i in range(HB)]
        h_lo = [sb(f"x_h_lo{i}", [P, HALF], f32r) for i in range(HB)]
        z = sb("x_z", [P, KC, HALF])
        zt = sb("x_zt", [P, HT, C])
        st6, mv = sb("x_st6", [P, HT, 6]), sb("x_mv", [P, HT, 2])
        var, rstd, tmp = sb("x_var", [P, HT]), sb("x_rstd", [P, HT]), sb("x_tmp", [P, HT])
        h_ps = [ps(f"x_h_ps{i}", HALF) for i in range(2)]
        y_ps = [[ps(f"x_y_ps{j}{c}", HALF) for c in range(KC)] for j in range(2)]
        z_ps = [ps(f"x_z_ps{i}", 2 * C) for i in range(2)]
        consts, idx_loaded, small_loaded, v_loaded = (sem(f"x_{n}") for n in ("consts", "idx_l", "small_l", "v_l"))
        w_loaded = [sem(f"x_w_loaded{i}") for i in range(NW)]
        rows_loaded, t_loaded = sem("x_rows_l"), sem("x_t_l")
        whi_ready, w_split, vhi_ready, v_split = sem("x_whi_s"), sem("x_w_split"), sem("x_vhi_s"), sem("x_v_split")
        h_done, hid_ready, h_split, y_done = sem("x_h_done"), sem("x_hid_s"), sem("x_h_split"), sem("x_y_done")
        z_ready, turned, zt_ready = sem("x_z_s"), sem("x_turned"), sem("x_zt_s")
        var_ready, rstd_ready, normed_ready, out_ready, out_stored = (sem(f"x_{n}") for n in ("var_s", "rstd_s", "normed_s", "out_s", "out_stored"))

        def period(b, s, before, after):
            steps = []
            for k in range(UNITS):
                steps.append(("hidden", k, b, s))
                if k >= LATE:
                    steps.append(("expert", k - LATE, b, s))
                elif before:
                    steps.append(("expert", UNITS - LATE + k, b - 1, 1 - s))
                j = k // (UNITS // 2)
                if before or j:
                    n, q = (b, s) if j else (b - 1, 1 - s)
                    what = {LATE - 1: "sum", LATE + 1: "turn", LATE + 2: "stats", LATE + 3: "rsqrt", LATE + 4: "norm"}.get(k % (UNITS // 2))
                    if what:
                        steps.append((what, 1 - j, n, q))
                if k == UNITS - 4 and after:
                    steps.append(("split", 0, b + 1, 1 - s))
                if 0 <= k - UNITS // 2 < NW and after:
                    steps.append(("weights", k - UNITS // 2, b + 1, 1 - s))
            return steps

        def all_images(eng, run):
            run([("split", 0, 0, 0)] + [("weights", i, 0, 0) for i in range(NW)])
            run(period(0, 0, False, True))
            with eng.Fori(1, B - 1, 2) as b:
                run(period(b, 1, True, True))
                run(period(b + 1, 0, True, True))
            run(period(B - 1, 1, True, False))
            run([("expert", UNITS - LATE + k, B - 1, 1) for k in range(LATE)])
            run([(what, 1, B - 1, 1) for what in ("sum", "turn", "stats", "rsqrt", "norm")])

        half = lambda j: slice(j * HALF, (j + 1) * HALF)
        tile = lambda t: slice(t * P, (t + 1) * P)
        def weight(i, s):
            k, second = i // 2, i % 2
            return [w[:, k] for w in ((w2_st, w2_hi[s], w2_lo[s]) if second else (w1_st, w1_hi[s], w1_lo[s]))]

        unit = lambda k: (k // (UNITS // 2), k // FC % TOPK, k % FC)

        with nc.Block() as block:
            @block.sync
            def _(sp):
                out_v = out.rearrange("b h w c -> b (h w) c").rearrange("b (t p) c -> b p t c", p=P)
                t_v = t_d.rearrange("b (t p) c -> b p t c", p=P)

                def load_tokens(n, s, first=False):
                    if not first:
                        sp.wait_ge(z_ready, n * 2)
                        sp.nop(nofuse=True)
                    sp.dma_start(vT[s][:], vT_d[n].rearrange("c p n -> p c n")).then_inc(v_loaded, 16)
                    sp.dma_start(wts[s][:], wts_d[n].rearrange("(a k) -> a k", a=1).to_broadcast([P, TOPK])).then_inc(small_loaded, 16)

                def load_experts(n, s, first=False):
                    sp.dma_start(idx[:], idx_d[n].rearrange("(a k) -> a k", a=1)).then_inc(idx_loaded, 16)
                    if first:
                        load_tokens(n, s, first)
                    sp.wait_ge(idx_loaded, n * 16 + 16)
                    sp.nop(nofuse=True)
                    chosen = [sp.value_load(idx[0:1, k:k + 1], min_val=0, max_val=E - 1) for k in range(TOPK)]
                    if not first:
                        sp.wait_ge(w_split, n * NW)
                        sp.nop(nofuse=True)
                    for k, e in enumerate(chosen):
                        sp.dma_start(w1_st[:, k], w1[e].rearrange("(c p) f -> p c f", p=P)).then_inc(w_loaded[2 * k], 16)
                        sp.dma_start(w2_st[:, k], w2[e].rearrange("(c p) d -> p c d", p=P)).then_inc(w_loaded[2 * k + 1], 16)
                    if not first:
                        load_tokens(n, s)
                    with nc.allow_non_contiguous_dma(reason="biases of an expert, a word per partition"):
                        for k, e in enumerate(chosen):
                            sp.dma_start(b1_sb[s][:, k], b1[e].rearrange("(c p) -> p c", p=P)).then_inc(small_loaded, 16)
                            sp.dma_start(b2_sb[s][:, k], b2[e].rearrange("(c p) -> p c", p=P)).then_inc(small_loaded, 16)

                def load_t(n, j, first=False):
                    if not first:
                        sp.wait_ge(out_stored, n * 32 + j * 16)
                        sp.nop(nofuse=True)
                    sp.dma_start(t_sb[:], t_v[n, :, j * HT:(j + 1) * HT, :]).then_inc(t_loaded, 16)

                def store(n, j):
                    sp.wait_ge(out_ready, n * 2 + j + 2)
                    sp.nop(nofuse=True)
                    sp.dma_start(out_v[n, :, j * HT:(j + 1) * HT, :], t_sb[:]).then_inc(out_stored, 16)

                def image(b, s, before, after):
                    if after:
                        load_experts(b + 1, 1 - s)
                    if before:
                        store(b - 1, 1)
                        load_t(b, 0)
                    store(b, 0)
                    load_t(b, 1)

                load_experts(0, 0, first=True)
                load_t(0, 0, first=True)
                sp.dma_start(gam[:], gamma.rearrange("(a c) -> a c", a=1).to_broadcast([P, C])).then_inc(rows_loaded, 16)
                sp.dma_start(bet[:], beta.rearrange("(a c) -> a c", a=1).to_broadcast([P, C])).then_inc(rows_loaded, 16)
                image(0, 0, False, True)
                with sp.Fori(1, B - 2, 2) as b:
                    image(b, 1, True, True)
                    image(b + 1, 0, True, True)
                image(B - 1, 1, True, False)
                store(B - 1, 1)
                sp.wait_ge(out_stored, 32 * B)

            @block.gpsimd
            def _(pool):
                wide = lambda row: row[:].rearrange("p (a c) -> p a c", a=1).to_broadcast([P, HT, C])

                def run(steps):
                    for what, k, n, s in steps:
                        if what == "weights":
                            pool.wait_ge(whi_ready, n * NW + k + 1)
                            st, hi, lo = weight(k, s)
                            nc.gpsimd.tensor_tensor(lo, st, bits(hi), ALU.subtract).then_inc(w_split, 1)
                        if what == "norm":
                            pool.wait_ge(normed_ready, n * 2 + k + 1)
                            nc.gpsimd.tensor_tensor(zt[:], zt[:], wide(gam), ALU.mult)
                            pool.drain()
                            nc.gpsimd.tensor_tensor(zt[:], zt[:], wide(bet), ALU.add)
                            pool.drain()
                            pool.wait_ge(t_loaded, n * 32 + k * 16 + 16)
                            nc.gpsimd.tensor_tensor(t_sb[:], t_sb[:], zt[:], ALU.add).then_inc(out_ready, 1)

                make_identity(nc, pool, ident[:], consts)
                pool.wait_ge(rows_loaded, 32)
                all_images(pool, run)

            @block.scalar
            def _(act):
                def run(steps):
                    for what, k, n, s in steps:
                        if what == "split":
                            act.wait_ge(v_loaded, n * 16 + 16)
                            if not (isinstance(n, int) and n == 0):
                                act.wait_ge(y_done, n * UNITS - UNITS + HB)
                            nc.scalar.activation(v_hi[s][:], vT[s][:], ACT.Copy).then_inc(vhi_ready, 1)
                        if what == "weights":
                            act.wait_ge(w_loaded[k], n * 16 + 16)
                            st, hi, lo = weight(k, s)
                            nc.scalar.activation(hi, st, ACT.Copy).then_inc(whi_ready, 1)
                        if what == "hidden":
                            j, e, f = unit(k)
                            act.wait_ge(h_done, n * UNITS + k + 1)
                            act.wait_ge(h_split, n * UNITS + k + 1)
                            if k == 0:
                                act.wait_ge(small_loaded, n * (16 * (2 * TOPK + 1)) + 16 * (2 * TOPK + 1))
                            nc.scalar.activation(hid[k % 2][:], h_ps[k % 2][:], ACT.Gelu, bias=b1_sb[s][:, e, f:f + 1]
                                                 ).then_inc(hid_ready, 1)
                        if what == "turn":
                            for i in range(2):
                                act.wait_ge(turned, n * 4 + k * 2 + i + 1)
                                if i == 0:
                                    act.wait_ge(out_ready, n * 2 + k + 1)
                                nc.scalar.activation(zt[:, 2 * i:2 * i + 2, :], z_ps[i][:].rearrange("p (t c) -> p t c", t=2),
                                                     ACT.Copy).then_inc(zt_ready, 1)
                        if what == "rsqrt":
                            nc.scalar.preload_act_table_set("natural_log_exp_and_others")
                            act.wait_ge(var_ready, n * 2 + k + 1)
                            nc.scalar.activation(rstd[:], var[:], ACT.Ln)
                            act.drain()
                            nc.scalar.activation(rstd[:], rstd[:], ACT.Exp, scale=-0.5).then_inc(rstd_ready, 1)

                all_images(act, run)

            @block.vector
            def _(dve):
                def run(steps):
                    for what, k, n, s in steps:
                        if what == "split":
                            dve.wait_ge(vhi_ready, n + 1)
                            nc.vector.tensor_tensor(v_lo[s][:], vT[s][:], bits(v_hi[s][:]), ALU.subtract).then_inc(v_split, 1)
                            dve.wait_ge(small_loaded, n * (16 * (2 * TOPK + 1)) + 16 * (2 * TOPK + 1))
                            nc.vector.tensor_scalar(b2w[s][:], b2_sb[s][:, 0], wts[s][:, 0:1], None, ALU.mult)
                            dve.drain()
                            nc.vector.scalar_tensor_tensor(b2w[s][:], b2_sb[s][:, 1], wts[s][:, 1:2], b2w[s][:], ALU.mult, ALU.add)
                        if what == "hidden":
                            j, e, f = unit(k)
                            dve.wait_ge(hid_ready, n * UNITS + k + 3)
                            dve.wait_ge(y_done, n * UNITS + k + 1)
                            nc.vector.tensor_scalar(h_hi[k % HB][:], hid[k % 2][:], wts[s][:, e:e + 1], None, ALU.mult)
                            dve.drain()
                            nc.vector.scalar_tensor_tensor(h_lo[k % HB][:], hid[k % 2][:], wts[s][:, e:e + 1], bits(h_hi[k % HB][:]),
                                                           ALU.mult, ALU.subtract).then_inc(h_split, 1)
                        if what == "sum":
                            dve.wait_ge(y_done, n * UNITS + (k + 1) * (UNITS // 2) + HB)
                            for c in range(KC):
                                last = nc.vector.scalar_tensor_tensor(z[:, c, :], y_ps[k][c][:], b2w[s][:, c:c + 1], vT[s][:, c, half(k)],
                                                                      ALU.add, ALU.add)
                            last.then_inc(z_ready, 1)
                        if what == "stats":
                            dve.wait_ge(zt_ready, n * 4 + k * 2 + 4)
                            for i in range(HT):
                                nc.vector.bn_stats(st6[:, i, :], zt[:, i, :])
                            dve.drain()
                            for i in range(HT):
                                nc.vector.bn_aggr(mv[:, i, :], st6[:, i, :])
                            dve.drain()
                            nc.vector.tensor_scalar(var[:], mv[:, :, 1], 1e-5, None, ALU.add).then_inc(var_ready, 1)
                        if what == "norm":
                            dve.wait_ge(rstd_ready, n * 2 + k + 1)
                            newton(nc, dve, rstd[:], var[:], tmp[:])
                            for i in range(HT):
                                last = nc.vector.tensor_scalar(zt[:, i, :], zt[:, i, :], mv[:, i, 0:1], rstd[:, i:i + 1], ALU.subtract, ALU.mult)
                            last.then_inc(normed_ready, 1)

                all_images(dve, run)

            @block.tensor
            def _(pe):
                def run(steps):
                    for what, k, n, s in steps:
                        if what == "hidden":
                            j, e, f = unit(k)
                            if k == 0:
                                pe.wait_ge(v_split, n + 1)
                            if j == f == 0:
                                pe.wait_ge(w_split, n * NW + 2 * e + 1)
                            pe.wait_ge(hid_ready, n * UNITS + k + 1)
                            i = 0
                            for c in range(KC):
                                for w, v in ((w1_hi, v_hi), (w1_hi, v_lo), (w1_lo, v_hi)):
                                    m = nc.tensor.matmul(h_ps[k % 2][:], w[s][:, e, c, tile(f)], v[s][:, c, half(j)],
                                                         start=i == 0, stop=i == 3 * KC - 1)
                                    i += 1
                            m.then_inc(h_done, 1)
                        if what == "expert":
                            j, e, f = unit(k)
                            pe.wait_ge(h_split, n * UNITS + k + 3)
                            if j == f == 0:
                                pe.wait_ge(w_split, n * NW + 2 * e + 2)
                            if k % (UNITS // 2) == 0:
                                pe.wait_ge(z_ready, n * 2 + j + 1)
                            first, last = e + f == 0, e == TOPK - 1 and f == FC - 1
                            for c in range(KC):
                                for i, (w, h) in enumerate(((w2_hi, h_hi), (w2_hi, h_lo), (w2_lo, h_hi))):
                                    m = nc.tensor.matmul(y_ps[j][c][:], w[s][:, e, f, tile(c)], h[k % HB][:],
                                                         start=first and i == 0, stop=last and i == 2)
                            m.then_inc(y_done, 1)
                        if what == "turn":
                            pe.wait_ge(z_ready, n * 2 + k + 3)
                            for i in range(2):
                                pe.wait_ge(zt_ready, n * 4 + k * 2 + i + 1)
                                for t in range(2):
                                    for c in range(KC):
                                        m = nc.tensor.transpose(z_ps[i][:, t * C + c * P:t * C + (c + 1) * P], z[:, c, tile(2 * i + t)], ident[:])
                                m.then_inc(turned, 1)

                pe.sem_inc(hid_ready, 2)
                pe.sem_inc(h_split, 2)
                pe.sem_inc(y_done, HB)
                pe.sem_inc(z_ready, 2)
                pe.sem_inc(zt_ready, 2)
                pe.sem_inc(out_ready, 1)
                pe.wait_ge(consts, 1)
                all_images(pe, run)


_INS = ["x"] + ["L0_conv_" + n for n in ("conv_w", "conv_b", "qkv_w", "qkv_b", "attn_w", "attn_b", "key_rel_w", "key_rel_h")] + \
    ["L1_attn_" + n for n in ("W_q", "W_k", "W_v", "W_o", "b_o")] + \
    ["L1_ffn_" + n for n in ("Wr", "br", "W1", "b1", "W2", "b2", "gamma", "beta")]


def build(nc, a, out):
    def scratch(name, shape, dt=f32):
        return nc.dram_tensor(name, shape, dt, kind="Internal").ap()

    mixT_d = scratch("mixT_d", (B, KC, P, TOK))
    kq_d = scratch("kq_d", (B, GROUPS, 2, 2, HG * DH, TOK))
    rel_d = scratch("rel_d", (B, GROUPS, 2, 2, P, TOK))
    va_d = scratch("va_d", (B, GROUPS, P, TT * HG * 32))
    att_d = scratch("att_d", (B, GROUPS, P, TOK))
    rsum_d = scratch("rsum_d", (B, GROUPS, HG, TOK))
    t_d = scratch("t_d", (B, TOK, C))
    vT_d = scratch("vT_d", (B, KC, P, TOK))
    vsum_d = scratch("vsum_d", (B, P, KC, TT // 2))
    wts_d, idx_d = scratch("wts_d", (B, TOPK)), scratch("idx_d", (B, TOPK), mybir.dt.uint32)
    front(nc, a["x"], *[a["L0_conv_" + n] for n in ("conv_w", "conv_b", "qkv_w", "qkv_b", "key_rel_w", "key_rel_h")],
          mixT_d, kq_d, rel_d, va_d)
    attention_phase(nc, kq_d, rel_d, va_d, att_d)
    self_attention_phase(nc, a["x"], a["L0_conv_attn_w"], a["L0_conv_attn_b"],
                         *[a["L1_attn_" + n] for n in ("W_q", "W_k", "W_v", "W_o", "b_o")],
                         mixT_d, att_d, rsum_d, t_d, vT_d, vsum_d)
    router_phase(nc, a["L1_ffn_Wr"], a["L1_ffn_br"], vsum_d, wts_d, idx_d)
    expert_phase(nc, *[a["L1_ffn_" + n] for n in ("W1", "b1", "W2", "b2", "gamma", "beta")], t_d, vT_d, wts_d, idx_d, out)


def kernel(**inputs):
    import numpy as _np
    import concourse.bacc as _bacc
    from concourse.bass_utils import run_bass_kernel_spmd as _run

    nc = _bacc.Bacc("TRN2", target_bir_lowering=False, num_devices=1)
    arrays, args = {}, {}
    for name in _INS:
        arrays["in_" + name] = _np.ascontiguousarray(inputs[name])
        args[name] = nc.dram_tensor("in_" + name, arrays["in_" + name].shape, f32, kind="ExternalInput").ap()
    out = nc.dram_tensor("out_0", (B, H, W, C), f32, kind="ExternalOutput").ap()
    build(nc, args, out)
    r = _run(nc, [arrays], core_ids=[0])
    return r.results[0]["out_0"]
```

```python
import concourse.bass as bass
from concourse import mybir
from contextlib import ExitStack

f32 = mybir.dt.float32
f32r = mybir.dt.float32r
ALU = mybir.AluOpType
ACT = mybir.ActivationFunctionType
AX = mybir.AxisListType

P = 128
B, H, W, C = 8, 32, 32, 256
TOK = H * W
TT = TOK // P
KC = C // P
NH, DH = 8, 8
DK = NH * DH
CONV_OUT = C - DK
TAPS = 9
HP, WP = H + 2, W + 2
HALF = TOK // 2
GROUPS = 2
HG = NH // GROUPS
REL = 2 * W - 1
GN_SIZE = 8
U = 128
E, F, TOPK = 8, 512, 2
FC = F // P
FIRST = B // 2


def bits(ap):
    return ap.bitcast(f32)


def make_identity(nc, pool, ident, made):
    nc.gpsimd.memset(ident, 0.0)
    pool.drain()
    nc.gpsimd.affine_select(out=ident, in_=ident, compare_op=ALU.not_equal, fill=1.0, base=0,
                            pattern=[[-1, P]], channel_multiplier=1).then_inc(made, 1)


def newton(nc, dve, rstd, var, tmp):
    nc.vector.tensor_tensor(tmp, rstd, rstd, ALU.mult)
    dve.drain()
    nc.vector.tensor_tensor(tmp, tmp, var, ALU.mult)
    dve.drain()
    nc.vector.tensor_scalar(tmp, tmp, -0.5, 1.5, ALU.mult, ALU.add)
    dve.drain()
    nc.vector.tensor_tensor(rstd, rstd, tmp, ALU.mult)
    dve.drain()


def conv_phase(nc, x, conv_w, conv_b, qkv_w, qkv_b, rel_w, rel_h, q_all, bd_hi, bd_lo, hl, rel_stored, mixT_d, kq_d, rel_d, va_d):
    with ExitStack() as ctx:
        sb = lambda name, shape, dt=f32: ctx.enter_context(nc.sbuf_tensor(name, shape, dt))
        sem = lambda name: ctx.enter_context(nc.semaphore(name))
        ident = sb("c_ident", [P, P])
        gavg = sb("c_gavg", [P, P])
        fold = sb("c_fold", [P, DK])
        w_st = bits(hl[:]).rearrange("p a b n -> p (a b n)")[:, 0:KC * TAPS * CONV_OUT].rearrange(
            "p (k t o) -> p k t o", k=KC, t=TAPS)
        w0_hi = sb("c_w0_hi", [P, KC, TAPS, P], f32r)
        w0_lo = sb("c_w0_lo", [P, KC, TAPS, P], f32r)
        w1_hl = sb("c_w1_hl", [P, KC, TAPS, P], f32r)
        q_st = sb("c_q_st", [P, KC, 3 * DK])
        wkq_hi = sb("c_wkq_hi", [P, KC, P], f32r)
        wkq_lo = sb("c_wkq_lo", [P, KC, P], f32r)
        wv_hl = sb("c_wv_hl", [P, KC, P], f32r)
        cb0, cb1 = sb("c_cb0", [P, 1]), sb("c_cb1", [DK, 1])
        kqb, kqs = sb("c_kqb", [P, 1]), sb("c_kqs", [P, 1])
        vb = sb("c_vb", [P, TT, DK])
        krT = sb("c_krT", [DH, 2, REL])
        kr_rows = sb("c_kr_rows", [P, 2, REL])
        own = sb("c_own", [P, 2, GROUPS, HG])
        bd = sb("c_bd", [P, REL, HG])
        xtok = sb("c_xtok", [P, TT, C])
        xT = sb("c_xT", [P, KC, TOK])
        y32 = sb("c_y32", [P, KC, TOK])
        y_hi = [sb(f"c_y_hi{i}", [P, KC, HP, WP], f32r) for i in range(2)]
        y_lo = [sb(f"c_y_lo{i}", [P, KC, HP, WP], f32r) for i in range(2)]
        st6 = sb("c_st6", [P, KC, 2, 6])
        cms = sb("c_cms", [P, 2, KC])
        cm2 = sb("c_cm2", [P, KC, 2])
        gms = sb("c_gms", [P, 2, KC])
        dev = sb("c_dev", [P, KC])
        gvar = sb("c_gvar", [P, KC])
        sd = sb("c_sd", [P, KC])
        rstd = sb("c_rstd", [P, KC])
        tmp = sb("c_tmp", [P, KC])
        cst = sb("c_cst", [P, KC, TOK])
        c1lo = sb("c_c1lo", [DK, 2, HALF])
        kq32 = sb("c_kq32", [P, TOK])
        kq_hi, kq_lo = sb("c_kq_hi", [P, TOK], f32r), sb("c_kq_lo", [P, TOK], f32r)
        vT = sb("c_vT", [P, TOK])
        va = sb("c_va", [P, TT, NH, 32])
        acc = [ctx.enter_context(nc.psum_tensor(f"c_acc{i}", [P, HALF], f32)) for i in range(4)]
        wide = [ctx.enter_context(nc.psum_tensor(f"c_wide{i}", [P, TOK], f32)) for i in range(2)]
        w_loaded, w_split, consts = sem("c_w_loaded"), sem("c_w_split"), sem("c_consts")
        w0_high, w0_split = [sem(f"c_w0_high{k}") for k in range(KC)], sem("c_w0_split")
        kr_loaded, rows_loaded, masks = sem("c_kr_loaded"), sem("c_rows_loaded"), sem("c_masks")
        x_loaded, x_turned, xT_ready = sem("c_x_loaded"), sem("c_x_turned"), sem("c_xT_ready")
        stats_ready, gmean_ready, dev_ready, gdev_ready = sem("c_stats"), sem("c_gmean"), sem("c_dev_s"), sem("c_gdev")
        gvar_ready, sd_ready = sem("c_gvar_s"), sem("c_sd_s")
        y32_ready, yhi_ready, y_ready = sem("c_y32_s"), sem("c_yhi_s"), sem("c_y_s")
        unit_done = sem("c_unit_done")
        unit_read = [sem(f"c_unit_read{i}") for i in range(4)]
        c1lo_ready, cst_stored = sem("c_c1lo_s"), sem("c_cst_stored")
        kqhi_ready, kq_ready, kq_stored = sem("c_kqhi"), sem("c_kq_s"), sem("c_kq_stored")
        va_turned, va_ready, va_stored = sem("c_va_turned"), sem("c_va_s"), sem("c_va_stored")
        q_ready, bd_ready = sem("c_q_s"), sem("c_bd_s")
        rel_hi = sem("c_rel_hi")

        UNITS = [("kq", 0), ("conv0", 0), ("kq", 1), ("conv0", 1), ("v", 0), ("conv1", 0), ("v", 1), ("conv1", 1)]
        UNITS_REL = UNITS[:5] + [("rel", 0), ("rel", 1), UNITS[5], ("rel", 2), ("rel", 3), UNITS[6], ("rel", 4), ("rel", 5),
                                 UNITS[7], ("rel", 6), ("rel", 7)]
        RU = len(UNITS_REL) - len(UNITS)
        later = lambda b: isinstance(b, int) and b >= FIRST
        units = lambda b: UNITS_REL if later(b) else UNITS
        before = lambda b: FIRST * len(UNITS) + (b - FIRST) * len(UNITS_REL) if later(b) else b * len(UNITS)
        done = lambda b, what, t: before(b) + units(b).index((what, t)) + 1
        bank = lambda b, what, t: units(b).index((what, t)) % 4
        read = lambda b, what, t: before(b) // 4 + units(b).index((what, t)) // 4 + 2
        KQ_DMAS = 4 * GROUPS
        x_v = x.rearrange("b h w c -> b (h w) c").rearrange("b (t p) c -> b p t c", p=P)

        def rel_target(part, wh, n):
            if wh == 0:
                return part.rearrange("p b (y x) -> p x b y", x=W)[:, 4 * n:4 * n + 4]
            return part.rearrange("p b (y x) -> p y b x", x=W)[:, 4 * n:4 * n + 4]

        def rel_bank(u):
            return acc[u][:].rearrange("p (i b n) -> p i b n", i=4, b=FIRST)

        def image_rows(ap):
            return ap.rearrange("p (y x) -> p y x", x=W)

        def all_images(eng, image):
            with eng.Fori(0, FIRST, 2) as b:
                image(b, 0, True)
                image(b + 1, 1, True)
            for b in range(FIRST, B):
                image(b, b % 2, b + 1 < B)

        with nc.Block() as block:
            @block.sync
            def _(sp):
                def load(p):
                    sp.wait_ge(x_turned, p * KC)
                    sp.dma_start(xtok[:], x_v[p]).then_inc(x_loaded, 16)

                sp.dma_start(xtok[:], x_v[0]).then_inc(x_loaded, 16)
                for k in range(KC):
                    sp.dma_start(w_st[:, k], conv_w.rearrange("a b (k p) o -> p k (a b) o", p=P)[:, k]).then_inc(w_loaded, 16)
                sp.dma_start(q_st[:], qkv_w.rearrange("(k p) o -> p k o", p=P)).then_inc(w_loaded, 16)
                sp.dma_start(cb0[:], conv_b[0:P].rearrange("(p a) -> p a", a=1)).then_inc(w_loaded, 16)
                sp.dma_start(cb1[:], conv_b[P:CONV_OUT].rearrange("(p a) -> p a", a=1)).then_inc(w_loaded, 16)
                sp.dma_start(kqb[:], qkv_b[0:P].rearrange("(p a) -> p a", a=1)).then_inc(w_loaded, 16)
                sp.dma_start(vb[:], bass.AP(tensor=qkv_b.tensor, offset=P, ap=[[0, P], [0, TT], [1, DK]])).then_inc(w_loaded, 16)
                load(1)
                with nc.allow_non_contiguous_dma(reason="two small tables, transposed once"):
                    sp.dma_start(krT[:, 0, :], rel_w.rearrange("m d -> d m")).then_inc(kr_loaded, 16)
                    sp.dma_start(krT[:, 1, :], rel_h.rearrange("m d -> d m")).then_inc(kr_loaded, 16)
                sp.wait_ge(kr_loaded, 32)
                for h in range(P // DH):
                    sp.dma_start(kr_rows[DH * h:DH * (h + 1)], krT[:]).then_inc(rows_loaded, 16)
                sp.sem_inc(kq_stored, KQ_DMAS * 16)
                sp.sem_inc(cst_stored, 32)
                sp.sem_inc(va_stored, 16 * GROUPS)

                def image(b, ahead):
                    sp.wait_ge(kq_ready, b + 1)
                    for part, buf in enumerate((kq_hi, kq_lo)):
                        for kq in range(2):
                            for g in range(GROUPS):
                                rows = kq * DK + g * HG * DH
                                sp.dma_start(kq_d[b, g, part, kq], bits(buf[rows:rows + HG * DH])).then_inc(kq_stored, 16)
                    if ahead:
                        load(b + 2)
                    sp.wait_ge(unit_read[bank(b, "conv1", 1)], read(b, "conv1", 1))
                    sp.dma_start(mixT_d[b, 0], cst[:, 0, :]).then_inc(cst_stored, 16)
                    sp.dma_start(mixT_d[b, 1, 0:CONV_OUT - P], cst[0:CONV_OUT - P, 1, :]).then_inc(cst_stored, 16)
                    sp.wait_ge(va_ready, b + 2)
                    for g in range(GROUPS):
                        sp.dma_start(va_d[b, g].rearrange("p (t c) -> p t c", t=TT),
                                     va[:, :, HG * g:HG * (g + 1), :].rearrange("p t h c -> p t (h c)")).then_inc(va_stored, 16)
                    if later(b):
                        sp.wait_ge(unit_read[bank(b, "rel", RU - 1)], read(b, "rel", RU - 1))
                        wh, g = (b - FIRST) % 2, (b - FIRST) // 2
                        for part in range(2):
                            sp.dma_start(rel_d[0:FIRST, g, wh, part].rearrange("b p n -> p b n"), bits(hl[:, part])).then_inc(rel_stored, 16)

                with sp.Fori(0, FIRST) as b:
                    image(b, True)
                for b in range(FIRST, B):
                    image(b, b + 2 < B)
                sp.wait_ge(kq_stored, KQ_DMAS * 16 * (B + 1))
                sp.wait_ge(cst_stored, 32 * (B + 1))
                sp.wait_ge(va_stored, 16 * GROUPS * (B + 1))

            @block.gpsimd
            def _(pool):
                nc.gpsimd.memset(gavg[:], 1.0 / GN_SIZE)
                nc.gpsimd.memset(fold[:], 0.0)
                nc.gpsimd.memset(va[:], 0.0)
                make_identity(nc, pool, ident[:], consts)
                g3 = gavg[:].rearrange("p (g c) -> p g c", c=GN_SIZE)
                for base, sign in ((0, 1), (GN_SIZE - 1, -1)):
                    nc.gpsimd.affine_select(out=g3, in_=g3, compare_op=ALU.is_ge, fill=0.0, base=base,
                                            pattern=[[-sign * GN_SIZE, P // GN_SIZE], [0, GN_SIZE]],
                                            channel_multiplier=sign)
                    nc.gpsimd.affine_select(out=fold[:], in_=fold[:], compare_op=ALU.not_equal, fill=1.0,
                                            base=-DK if base else 0, pattern=[[-1, DK]], channel_multiplier=1)
                    pool.drain()
                nc.gpsimd.memset(va[:, :, :, DH:DH + 1], 1.0).then_inc(consts, 1)
                nc.gpsimd.memset(own[:], 1.0)
                pool.drain()
                for base, sign in ((0, 1), (DH - 1, -1)):
                    nc.gpsimd.affine_select(out=own[:], in_=own[:], compare_op=ALU.is_ge, fill=0.0, base=base,
                                            pattern=[[-sign * DK, 2], [-sign * HG * DH, GROUPS], [-sign * DH, HG]],
                                            channel_multiplier=sign)
                    pool.drain()
                nc.gpsimd.tensor_tensor(own[:, 0], own[:, 0], own[:, 1], ALU.add).then_inc(masks, 1)
                for k in range(KC):
                    pool.wait_ge(w0_high[k], 1)
                    nc.gpsimd.tensor_tensor(w0_lo[:, k], w_st[:, k, :, 0:P], bits(w0_hi[:, k]), ALU.subtract).then_inc(w0_split, 1)

            @block.scalar
            def _(act):
                def prep(p, first=False):
                    for c in range(KC):
                        act.wait_ge(x_turned, p * KC + c + 1)
                        if not first:
                            act.wait_ge(y32_ready, p * KC)
                        nc.scalar.activation(xT[:, c, :], wide[c][:], ACT.Copy).then_inc(xT_ready, 1)

                def round_y(p, s, first=False):
                    for c in range(KC):
                        act.wait_ge(y32_ready, p * KC + c + 1)
                        if not first:
                            act.wait_ge(va_turned, p)
                        nc.scalar.activation(y_hi[s][:, c, 1:H + 1, 1:W + 1], image_rows(y32[:, c, :]),
                                             ACT.Copy).then_inc(yhi_ready, 1)

                def spread(p):
                    act.wait_ge(gvar_ready, p + 1)
                    nc.scalar.activation(sd[:], gvar[:], ACT.Sqrt).then_inc(sd_ready, 1)

                def image(b, s, prefetch):
                    if prefetch:
                        prep(b + 1)
                    act.wait_ge(unit_read[bank(b, "kq", 1)], read(b, "kq", 1))
                    act.wait_ge(kq_stored, (b + 1) * (KQ_DMAS * 16))
                    nc.scalar.activation(kq_hi[:], kq32[:], ACT.Copy).then_inc(kqhi_ready, 1)
                    nc.scalar.activation(q_all[DK:P, b, :], kq32[DK:P, :], ACT.Copy)
                    act.wait_ge(kq_ready, b + 1)
                    nc.scalar.activation(q_all[0:DK, b, :], bits(kq_lo[DK:P, :]), ACT.Copy).then_inc(q_ready, 1)
                    if prefetch:
                        spread(b + 1)
                    for what, t in units(b)[units(b).index(("v", 0)):]:
                        act.wait_ge(unit_done, done(b, what, t))
                        u = bank(b, what, t)
                        if what == "v":
                            nc.scalar.activation(vT[:, t * HALF:(t + 1) * HALF], acc[u][:], ACT.Copy).then_inc(unit_read[u], 1)
                            if t == 0 and prefetch:
                                round_y(b + 1, 1 - s)
                        elif what == "conv1":
                            nc.scalar.activation(c1lo[:, t, :], acc[u][DK:P, :], ACT.Copy).then_inc(c1lo_ready, 1)
                        else:
                            if t == 0 and b > FIRST:
                                act.wait_ge(rel_stored, 32 * (b - FIRST))
                            nc.scalar.activation(rel_target(hl[:, 0], (b - FIRST) % 2, t), rel_bank(u), ACT.Copy).then_inc(rel_hi, 1)

                prep(0, first=True)
                spread(0)
                act.wait_ge(w_loaded, 16 * (KC + 5))
                nc.scalar.activation(w0_hi[:, 1], w_st[:, 1, :, 0:P], ACT.Copy).then_inc(w0_high[1], 1)
                round_y(0, 0, first=True)
                all_images(act, image)

            @block.vector
            def _(dve):
                def prep_stats(p):
                    for c in range(KC):
                        dve.wait_ge(xT_ready, p * KC + c + 1)
                        for s in range(2):
                            nc.vector.bn_stats(st6[:, c, s, :], xT[:, c, s * HALF:(s + 1) * HALF])
                    dve.drain()
                    for c in range(KC):
                        nc.vector.bn_aggr(cm2[:, c, :], st6[:, c].rearrange("p s d -> p (s d)"))
                    dve.drain()
                    nc.vector.tensor_copy(cms[:].rearrange("p s c -> p c s"), cm2[:]).then_inc(stats_ready, 1)

                def prep_mean(p):
                    dve.wait_ge(gmean_ready, p + 1)
                    nc.vector.tensor_copy(gms[:].rearrange("p s c -> p (s c)"), wide[0][:, 0:2 * KC])
                    dve.drain()
                    nc.vector.tensor_tensor(dev[:], cms[:, 0, :], gms[:, 0, :], ALU.subtract)
                    dve.drain()
                    nc.vector.tensor_tensor(dev[:], dev[:], dev[:], ALU.mult).then_inc(dev_ready, 1)

                def prep_var(p):
                    dve.wait_ge(gdev_ready, p + 1)
                    nc.vector.scalar_tensor_tensor(gvar[:], wide[1][:, 0:KC], 1e-5, gms[:, 1, :], ALU.add, ALU.add
                                                   ).then_inc(gvar_ready, 1)

                def prep_y(p):
                    dve.wait_ge(sd_ready, p + 1)
                    nc.vector.reciprocal(rstd[:], sd[:])
                    dve.drain()
                    newton(nc, dve, rstd[:], gvar[:], tmp[:])
                    for c in range(KC):
                        nc.vector.tensor_scalar(y32[:, c, :], xT[:, c, :], gms[:, 0, c:c + 1], rstd[:, c:c + 1],
                                                ALU.subtract, ALU.mult).then_inc(y32_ready, 1)

                def low_y(p, s):
                    for c in range(KC):
                        dve.wait_ge(yhi_ready, p * KC + c + 1)
                        nc.vector.tensor_tensor(y_lo[s][:, c, 1:H + 1, 1:W + 1], image_rows(y32[:, c, :]),
                                                bits(y_hi[s][:, c, 1:H + 1, 1:W + 1]), ALU.subtract).then_inc(y_ready, 1)

                def relative_keys():
                    dve.wait_ge(masks, 1)
                    dve.wait_ge(rows_loaded, 16 * (P // DH))
                    for wh in range(2):
                        for g in range(GROUPS):
                            for h in range(HG):
                                nc.vector.tensor_scalar(bd[:, :, h], kr_rows[:, wh, :], own[:, 0, g, h:h + 1], None, ALU.mult)
                            dve.drain()
                            flat = bd[:].rearrange("p m h -> p (m h)")
                            nc.vector.tensor_copy(bd_hi[:, wh, g], flat)
                            dve.drain()
                            nc.vector.tensor_tensor(bd_lo[:, wh, g], flat, bits(bd_hi[:, wh, g]), ALU.subtract).then_inc(bd_ready, 1)
                            dve.drain()

                def kq(b, t):
                    dve.wait_ge(unit_done, done(b, "kq", t))
                    if t == 0:
                        dve.wait_ge(q_ready, b + 1)
                    nc.vector.tensor_scalar(kq32[:, t * HALF:(t + 1) * HALF], acc[bank(b, "kq", t)][:], kqb[:], kqs[:],
                                            ALU.add, ALU.mult).then_inc(unit_read[bank(b, "kq", t)], 1)

                def conv0(b, t):
                    dve.wait_ge(unit_done, done(b, "conv0", t))
                    if t == 0:
                        dve.wait_ge(cst_stored, b * 32 + 32)
                    nc.vector.tensor_scalar(cst[:, 0, t * HALF:(t + 1) * HALF], acc[bank(b, "conv0", t)][:], cb0[:], None,
                                            ALU.add).then_inc(unit_read[bank(b, "conv0", t)], 1)

                def conv1(b, t):
                    dve.wait_ge(c1lo_ready, b * 2 + t + 1)
                    nc.vector.scalar_tensor_tensor(cst[0:DK, 1, t * HALF:(t + 1) * HALF], acc[bank(b, "conv1", t)][0:DK, :],
                                                   cb1[:], c1lo[:, t, :], ALU.add, ALU.add
                                                   ).then_inc(unit_read[bank(b, "conv1", t)], 1)

                def relative(b, n):
                    wh, u = (b - FIRST) % 2, bank(b, "rel", n)
                    dve.wait_ge(rel_hi, (b - FIRST) * RU + n + 1)
                    nc.vector.tensor_tensor(rel_target(hl[:, 1], wh, n), rel_bank(u), rel_target(bits(hl[:, 0]), wh, n), ALU.subtract
                                            ).then_inc(unit_read[u], 1)

                def image(b, s, prefetch):
                    kq(b, 0)
                    if prefetch:
                        prep_stats(b + 1)
                    conv0(b, 0)
                    if prefetch:
                        prep_mean(b + 1)
                    kq(b, 1)
                    dve.wait_ge(kqhi_ready, b + 1)
                    nc.vector.tensor_tensor(kq_lo[:], kq32[:], bits(kq_hi[:]), ALU.subtract).then_inc(kq_ready, 1)
                    conv0(b, 1)
                    if prefetch:
                        prep_var(b + 1)
                        prep_y(b + 1)
                        low_y(b + 1, 1 - s)
                    for what, t in units(b)[units(b).index(("v", 0)):]:
                        if what == "conv1":
                            conv1(b, t)
                        if what == "rel":
                            relative(b, t)
                    dve.wait_ge(va_turned, b + 2)
                    dve.wait_ge(va_stored, (b + 1) * (16 * GROUPS))
                    nc.vector.tensor_tensor(va[:, :, :, 0:DH],
                                            wide[1][:, 0:TT * DK].rearrange("p (t h d) -> p t h d", h=NH, d=DH),
                                            vb[:].rearrange("p t (h d) -> p t h d", d=DH), ALU.add).then_inc(va_ready, 1)

                def high(src, hi):
                    for k in range(KC):
                        nc.vector.tensor_copy(hi[:, k], src[:, k])

                def low(src, hi, lo):
                    for k in range(KC):
                        last = nc.vector.tensor_tensor(lo[:, k], src[:, k], bits(hi[:, k]), ALU.subtract)
                    last.then_inc(w_split, 1)

                def clear(s):
                    for buf in (y_hi[s], y_lo[s]):
                        nc.vector.memset(bits(buf[:]), 0.0)

                nc.vector.memset(kqs[0:DK], 1.0)
                nc.vector.memset(kqs[DK:P], DH ** -0.5)
                clear(0)
                dve.sem_inc(va_ready, 1)
                dve.sem_inc(q_ready, 1)
                prep_stats(0)
                prep_mean(0)
                dve.wait_ge(w_loaded, 16 * (KC + 5))
                wkq = q_st[:, :, 0:P], wkq_hi[:], wkq_lo[:]
                high(*wkq[:2])
                prep_var(0)
                nc.vector.tensor_copy(w0_hi[:, 0], w_st[:, 0, :, 0:P]).then_inc(w0_high[0], 1)
                prep_y(0)
                low(*wkq)
                low_y(0, 0)
                for split in ((q_st[:, :, P:3 * DK], wv_hl[:, :, 0:DK], wv_hl[:, :, DK:P]),
                              (w_st[:, :, :, P:CONV_OUT], w1_hl[:, :, :, 0:DK], w1_hl[:, :, :, DK:P])):
                    high(*split[:2])
                    dve.drain()
                    low(*split)
                clear(1)
                relative_keys()
                all_images(dve, image)

            @block.tensor
            def _(pe):
                def turn(p, first=False):
                    pe.wait_ge(x_loaded, p * 16 + 16)
                    for c in range(KC):
                        if c == 1 and not first:
                            pe.wait_ge(va_ready, p)
                        for t in range(TT):
                            m = nc.tensor.transpose(wide[c][:, t * P:(t + 1) * P], xtok[:, t, c * P:(c + 1) * P], ident[:])
                        m.then_inc(x_turned, 1)

                def group_mean(p):
                    pe.wait_ge(stats_ready, p + 1)
                    nc.tensor.matmul(wide[0][:, 0:2 * KC], gavg[:], cms[:].rearrange("p s c -> p (s c)"),
                                     start=True, stop=True).then_inc(gmean_ready, 1)

                def group_dev(p):
                    pe.wait_ge(dev_ready, p + 1)
                    nc.tensor.matmul(wide[1][:, 0:KC], gavg[:], dev[:], start=True, stop=True).then_inc(gdev_ready, 1)

                all_taps = [(t // 3, t % 3, t) for t in range(TAPS)]
                centre = [(1, 1, None)]

                HI, LO = y_hi, y_lo
                parts = {"kq": (((wkq_hi, HI), (wkq_hi, LO), (wkq_lo, HI)), centre),
                         "conv0": (((w0_hi, HI), (w0_hi, LO), (w0_lo, HI)), all_taps),
                         "v": (((wv_hl, HI), (wv_hl, LO)), centre),
                         "conv1": (((w1_hl, HI), (w1_hl, LO)), all_taps)}

                weights_split = {"kq": (w_split, 1), "conv0": (w0_split, KC), "v": (w_split, 2), "conv1": (w_split, 3)}

                def relative(b, n, u):
                    wh, g = (b - FIRST) % 2, (b - FIRST) // 2
                    pe.wait_ge(q_ready, FIRST + 1)
                    pe.wait_ge(bd_ready, 2 * GROUPS)
                    for j in range(4):
                        i = 4 * n + j
                        q = q_all[:, 0:FIRST, i::W] if wh == 0 else q_all[:, 0:FIRST, i * W:(i + 1) * W]
                        for k, bdp in enumerate((bd_hi, bd_lo)):
                            m = nc.tensor.matmul(rel_bank(u)[:, j], bdp[:, wh, g, HG * (W - 1 - i):HG * (2 * W - 1 - i)], q,
                                                 start=k == 0, stop=k == 1, skip_group_check=True)
                    m.then_inc(unit_done, 1)

                def unit(b, s, what, t):
                    u = bank(b, what, t)
                    pe.wait_ge(unit_read[u], read(b, what, t) - 1)
                    if what == "rel":
                        relative(b, t, u)
                        return
                    pe.wait_ge(*weights_split[what])
                    pairs, taps = parts[what]
                    n, total = 0, len(pairs) * KC * len(taps)
                    rows = t * (H // 2)
                    for k in range(KC):
                        for dy, dx, tap in taps:
                            for wt, y in pairs:
                                m = nc.tensor.matmul(image_rows(acc[u][:]), wt[:, k, :] if tap is None else wt[:, k, tap, :],
                                                     y[s][:, k, rows + dy:rows + dy + H // 2, dx:dx + W],
                                                     start=n == 0, stop=n == total - 1)
                                n += 1
                    m.then_inc(unit_done, 1)

                def image(b, s, prefetch):
                    pe.wait_ge(y_ready, b * KC + KC)
                    for what, t in units(b):
                        unit(b, s, what, t)
                        if prefetch and (what, t) == ("kq", 0):
                            turn(b + 1)
                        if prefetch and (what, t) == ("conv0", 0):
                            group_mean(b + 1)
                        if prefetch and (what, t) == ("conv0", 1):
                            group_dev(b + 1)
                    pe.wait_ge(unit_read[bank(b, "v", 1)], read(b, "v", 1))
                    if prefetch:
                        pe.wait_ge(gvar_ready, b + 2)
                    for t in range(TT):
                        m = nc.tensor.matmul(wide[1][:, t * DK:(t + 1) * DK], vT[:, t * P:(t + 1) * P], fold[:],
                                             start=True, stop=True)
                    m.then_inc(va_turned, 1)

                for free in unit_read:
                    pe.sem_inc(free, 1)
                pe.sem_inc(va_turned, 1)
                pe.wait_ge(consts, 2)
                turn(0, first=True)
                group_mean(0)
                group_dev(0)
                all_images(pe, image)


def attention_phase(nc, q_all, bd_hi, bd_lo, shared, first_stored, kq_d, rel_d, va_d, att_d):
    NG = B * GROUPS
    BUFS = 3
    ROW_W, ROW_H = (0, W), (2 * W, 2 * W + H // 2)
    ROW_Q = 2 * W + H
    ROW_M = ROW_Q + 3 * DH
    with ExitStack() as ctx:
        sb = lambda name, shape, dt=f32: ctx.enter_context(nc.sbuf_tensor(name, shape, dt))
        sem = lambda name: ctx.enter_context(nc.semaphore(name))
        ident = sb("a_ident", [P, P])
        ones_hot = sb("a_ones_hot", [P, HALF])
        qf = [sb(f"a_qf{i}", [P, HG, 2, TOK], f32r) for i in range(BUFS - 1)]
        qf.append(q_all[:].rearrange("p (h a) n -> p h a n", a=2))
        kf = [sb(f"a_kf{i}", [P, HG, TOK], f32r) for i in range(BUFS - 1)]
        nmax = sb("a_nmax", [P, HG, TT])
        mrow = sb("a_mrow", [2 * TT, HG // 2, P], f32r)
        sm = [ctx.enter_context(nc.psum_tensor(f"a_sm{i}", [P, TOK], f32)) for i in range(2)]
        made = sem("a_made")
        built = [sem(f"a_built{i}") for i in range(BUFS)]
        loaded = [sem(f"a_loaded{i}") for i in range(BUFS)]
        max_loaded = [sem(f"a_max_loaded{h}") for h in range(HG)]
        rel_done, rel_hi, rel_lo = sem("a_rel_done"), sem("a_rel_hi"), sem("a_rel_lo")
        sm_done, sm_read = sem("a_sm_done"), sem("a_sm_read")
        st_done, exp_done, pv_done = sem("a_st_done"), sem("a_exp_done"), sem("a_pv_done")
        out_ready, out_stored = sem("a_out_s"), sem("a_out_stored")
        LOADS = 4 + 4 + 6 + 3 + 1

        AHEAD = TT // 2
        def first_pass_units(whole):
            units, step = [], 0
            for d, h, t in [(0, h, t) for h in range(HG) for t in range(TT)][AHEAD:] + [(1, 0, t) for t in range(AHEAD) if whole]:
                if t == 0 and h % 2 == 0:
                    units.append((step, "turn", 0, (h - 1) % HG, 0))
                units.append((step, "logits", d, h, t))
                step += 1
            return units if whole else units + [(step, "turn", 0, HG - 1, 0)]
        first_pass_of = {whole: first_pass_units(whole) for whole in (True, False)}
        NU = len(first_pass_of[True])
        unit_at = {whole: {unit[1:]: k for k, unit in enumerate(units)} for whole, units in first_pass_of.items()}
        units_before = lambda n: AHEAD + n * NU
        STEPS = TT * HG
        NS = 2 * STEPS

        def all_groups(eng, period):
            steps = (NG - 3) // BUFS
            period(0, 0, True, True)
            with eng.Fori(1, (steps - 1) * BUFS + 2, BUFS) as n:
                for i in range(BUFS):
                    period(n + i, (1 + i) % BUFS, True, True)
            for n in range(1 + steps * BUFS, NG):
                period(n, n % BUFS, n < NG - 1, n + 2 < NG)

        both_halves = ones_hot[:].rearrange("p (a n) -> p a n", a=1).to_broadcast([P, 2, HALF])

        def load_queries(sp, n, j):
            kq_g = kq_d.rearrange("b g a k (h d) n -> (b g) a k d h n", d=DH)[n]
            rel_g = rel_d.rearrange("b g w a (j h) n -> (b g) w a j h n", h=HG)[n]
            for part in range(2):
                for half in range(2):
                    dst = bits(qf[j][:])
                    r = ROW_W[part]
                    sp.dma_start(dst[r:r + W, :, half, :], rel_g[0, part]).then_inc(loaded[j], 16)
                    r = ROW_H[part]
                    sp.dma_start(dst[r:r + H // 2, :, half, :], rel_g[1, part, half * H // 2:(half + 1) * H // 2]
                                 ).then_inc(loaded[j], 16)
            for row, qpart in enumerate((0, 0, 1)):
                r = ROW_Q + DH * row
                for half in range(2):
                    sp.dma_start(bits(qf[j][:])[r:r + DH, :, half, :], kq_g[qpart, 1]).then_inc(loaded[j], 16)

        def load_keys(sp, n, j):
            kq_g = kq_d.rearrange("b g a k (h d) n -> (b g) a k d h n", d=DH)[n]
            for row, kpart in enumerate((0, 1, 0)):
                r = ROW_Q + DH * row
                sp.dma_start(bits(kf[j][:])[r:r + DH], kq_g[kpart, 0]).then_inc(loaded[j], 16)

        def maxima(sp, n, j, whole):
            for h in range(HG):
                for half in range(2):
                    if half == 0:
                        sp.wait_ge(sm_read, units_before(n) + unit_at[whole]["turn", 0, h | 1, 0] + 1)
                    sp.dma_start(bits(qf[j][:])[ROW_M:ROW_M + 1, h, half, :].rearrange("a (t p) -> a t p", p=P),
                                 bits(mrow[h % 2 * TT:(h % 2 + 1) * TT, h // 2, :])).then_inc(max_loaded[h], 16)

        def logits_max(dve, before, k, h, t):
            dve.wait_ge(sm_done, before + k + 1)
            nc.vector.tensor_reduce(nmax[:, h, t:t + 1], sm[k % 2][:], axis=AX.X, op=ALU.max, negate=True).then_inc(sm_read, 1)

        def first_pass_maxima(dve, n, whole, only=None):
            for k, (step, what, d, h, t) in enumerate(first_pass_of[whole]):
                if only not in (None, step):
                    continue
                if what == "logits":
                    logits_max(dve, units_before(n), k, h, t)
                else:
                    dve.wait_ge(sm_done, units_before(n) + k + 1)
                    if not (isinstance(n, int) and n == 0):
                        for head in (h - 1, h):
                            dve.wait_ge(max_loaded[head], n * 32)
                    nc.vector.tensor_copy(mrow[:, h // 2, :], sm[k % 2][0:2 * TT, 0:P]).then_inc(sm_read, 1)

        def logits(pe, j, before, k, h, t, half):
            if half == 0 and not (isinstance(before, int) and before + k < 2):
                pe.wait_ge(sm_read, before + k - 1)
            cols = slice(half * HALF, (half + 1) * HALF)
            m = nc.tensor.matmul(sm[k % 2][:, cols], qf[j][0:ROW_M, h, half, t * P:(t + 1) * P],
                                 kf[j][0:ROW_M, h, cols], start=True, stop=True)
            if half == 1:
                m.then_inc(sm_done, 1)

        def first_pass(pe, n, j, whole, s, half, va_after=0):
            for k, (step, what, d, h, t) in enumerate(first_pass_of[whole]):
                if step == s and what == "logits":
                    if d == 1 and t == half == 0:
                        pe.wait_ge(loaded[(j + 1) % BUFS], times_loaded(n + 1, (j + 1) % BUFS) - va_after)
                    logits(pe, (j + d) % BUFS, units_before(n), k, h, t, half)
                elif step == s and half == 0:
                    pe.wait_ge(sm_read, units_before(n) + k - 1)
                    pe.wait_ge(sm_read, units_before(n) + unit_at[whole]["logits", 0, h, TT - 1] + 1)
                    nc.tensor.transpose(sm[k % 2][0:2 * TT, 0:P], nmax[:, h - 1:h + 1, :].rearrange("p h t -> p (h t)"), ident[:]).then_inc(sm_done, 1)

        def times_loaded(n, j):
            return (n - j + BUFS) * (16 * LOADS // BUFS)

        LAST = B - FIRST
        RELS = [(wh, g) for g in range(GROUPS) for wh in range(2)]
        RU = W // 4
        BANKS = 4
        LOAD_UNITS = 9
        rels = [("rel", r, n) for r in range(len(RELS)) for n in range(RU)]
        passes = [("logits", 0, t) for t in range(AHEAD)] + [("pass", s, None) for s in range(STEPS)]
        order = rels[:LOAD_UNITS]
        for i in range(max(len(rels) - LOAD_UNITS, len(passes))):
            order += passes[i:i + 1] + rels[LOAD_UNITS + i:LOAD_UNITS + i + 1]
        rel_stored = [sem(f"a_rel_stored{r}") for r in range(len(RELS))]

        def rel_target(buf, wh, n):
            if wh == 0:
                return buf.rearrange("p b (y x) -> p x b y", x=W)[:, 4 * n:4 * n + 4]
            return buf.rearrange("p b (y x) -> p y b x", x=W)[:, 4 * n:4 * n + 4]

        with (nc.sbuf_tensor("a_hl", [P, 2, LAST, TOK], f32r) as own_hl, nc.psum_tensor("a_rel0", [P, 4, LAST, W], f32) as r0,
              nc.psum_tensor("a_rel1", [P, 4, LAST, W], f32) as r1, nc.psum_tensor("a_rel2", [P, 4, LAST, W], f32) as r2,
              nc.psum_tensor("a_rel3", [P, 4, LAST, W], f32) as r3, nc.Block() as block):
            rel_ps = r0, r1, r2, r3
            hl = own_hl, shared

            @block.sync
            def _(sp):
                load_queries(sp, 0, 0)
                sp.wait_ge(built[0], 1)
                load_keys(sp, 0, 0)
                sp.wait_ge(first_stored, 32 * len(RELS))
                load_queries(sp, 1, 1)
                sp.wait_ge(built[1], 1)
                load_keys(sp, 1, 1)
                for r, (wh, g) in enumerate(RELS):
                    sp.wait_ge(rel_lo, RU * (r + 1))
                    for part in range(2):
                        sp.dma_start(rel_d[FIRST:B, g, wh, part].rearrange("b p n -> p b n"), bits(hl[r % 2][:, part])).then_inc(rel_stored[r], 16)
                maxima(sp, 0, 0, True)
                for stored in rel_stored:
                    sp.wait_ge(stored, 32)

            @block.gpsimd
            def _(pool):
                nc.gpsimd.memset(ones_hot[:], 0.0)
                pool.drain()
                xs, ys = [[0, H // 2], [-1, W]], [[-1, H // 2], [0, W]]
                for base, pattern in ((ROW_W[0], xs), (ROW_W[1], xs), (ROW_H[0], ys), (ROW_H[1], ys), (ROW_M, [[0, HALF]])):
                    nc.gpsimd.affine_select(out=ones_hot[:], in_=ones_hot[:], compare_op=ALU.not_equal, fill=1.0, base=-base,
                                            pattern=pattern, channel_multiplier=1)
                    pool.drain()
                nc.gpsimd.sem_inc(made, 1)
                make_identity(nc, pool, ident[:], made)

            @block.scalar
            def _(act):
                for r, (wh, g) in enumerate(RELS):
                    if r == 1:
                        act.wait_ge(made, 1)
                        for h in range(HG):
                            last = nc.scalar.activation(kf[1][:, h].rearrange("p (a n) -> p a n", a=2), both_halves, ACT.Copy)
                        last.then_inc(built[1], 1)
                        act.wait_ge(first_stored, 32 * len(RELS))
                    elif r:
                        act.wait_ge(rel_stored[r - 2], 32)
                    for n in range(RU):
                        act.wait_ge(rel_done, r * RU + n + 1)
                        nc.scalar.activation(rel_target(hl[r % 2][:, 0], wh, n), rel_ps[n % BANKS][:], ACT.Copy).then_inc(rel_hi, 1)

            @block.vector
            def _(dve):
                dve.wait_ge(made, 1)
                for h in range(HG):
                    last = nc.vector.tensor_copy(kf[0][:, h].rearrange("p (a n) -> p a n", a=2), both_halves)
                last.then_inc(built[0], 1)
                for what, i, n in order:
                    if what == "rel":
                        dve.wait_ge(rel_hi, i * RU + n + 1)
                        wh = RELS[i][0]
                        nc.vector.tensor_tensor(rel_target(hl[i % 2][:, 1], wh, n), rel_ps[n % BANKS][:],
                                                rel_target(bits(hl[i % 2][:, 0]), wh, n), ALU.subtract).then_inc(rel_lo, 1)
                    elif what == "logits":
                        logits_max(dve, 0, n, 0, n)
                    else:
                        first_pass_maxima(dve, 0, True, i)

            @block.tensor
            def _(pe):
                for what, i, n in order:
                    if what == "rel":
                        if i * RU + n >= BANKS:
                            pe.wait_ge(rel_lo, i * RU + n + 1 - BANKS)
                        wh, g = RELS[i]
                        for j in range(4):
                            c = 4 * n + j
                            q = q_all[:, FIRST:B, c::W] if wh == 0 else q_all[:, FIRST:B, c * W:(c + 1) * W]
                            for k, bdp in enumerate((bd_hi, bd_lo)):
                                m = nc.tensor.matmul(rel_ps[n % BANKS][:, j], bdp[:, wh, g, HG * (W - 1 - c):HG * (2 * W - 1 - c)], q,
                                                     start=k == 0, stop=k == 1, skip_group_check=True)
                        m.then_inc(rel_done, 1)
                        continue
                    if what == "logits" and n == 0:
                        pe.wait_ge(made, 2)
                        pe.wait_ge(loaded[0], 16 * (LOADS - 1))
                    for half in range(2):
                        if what == "logits":
                            logits(pe, 0, 0, n, 0, n, half)
                        else:
                            first_pass(pe, 0, 0, True, i, half, va_after=16)

        kf.append(sb(f"a_kf{BUFS - 1}", [P, HG, TOK], f32r))
        va = [sb(f"a_va{i}", [P, TT, HG, 32]) for i in range(BUFS)]
        probs = bits(shared[:])
        out = sb("a_out", [P, TOK])
        st = [ctx.enter_context(nc.psum_tensor(f"a_st{i}", [P, HALF], f32)) for i in range(2)]
        pv = ctx.enter_context(nc.psum_tensor("a_pv", [P, TOK], f32))

        with nc.Block() as block:
            @block.sync
            def _(sp):
                def load(n, j):
                    if not (isinstance(n, int) and n < BUFS):
                        sp.wait_ge(pv_done, n * 2 * TT - 4 * TT + 4)
                    load_queries(sp, n, j)
                    load_v(n, j)
                    if isinstance(n, int) and n == BUFS - 1:
                        sp.wait_ge(built[j], 16)
                    load_keys(sp, n, j)

                def load_v(n, j):
                    sp.dma_start(va[j][:].rearrange("p t h c -> p (t h c)"), va_d.rearrange("b g p c -> (b g) p c")[n]).then_inc(loaded[j], 16)

                def period(n, j, more, ahead):
                    if ahead:
                        load(n + 2, (j + 2) % BUFS)
                    if not (isinstance(n, int) and n == 0):
                        store(n - 1)
                    if more:
                        maxima(sp, n + 1, (j + 1) % BUFS, ahead)

                def store(n):
                    sp.wait_ge(out_ready, n * 2 + 4)
                    sp.dma_start(att_d.rearrange("b g p n -> (b g) p n")[n], out[:]).then_inc(out_stored, 16)

                sp.sem_inc(out_stored, 16)
                for n in range(BUFS - 1):
                    load_v(n, n)
                sp.dma_start(bits(kf[BUFS - 1][:]).rearrange("p h (a n) -> p (h a) n", a=2),
                             ones_hot[:].rearrange("p (a n) -> p a n", a=1).to_broadcast([P, 2 * HG, HALF])).then_inc(built[BUFS - 1], 16)
                all_groups(sp, period)
                store(NG - 1)
                sp.wait_ge(out_stored, 16 * (NG + 1))

            @block.scalar
            def _(act):
                def copy_out(n, half):
                    cols = slice(half * HALF, (half + 1) * HALF)
                    act.wait_ge(pv_done, n * 2 * TT + 2 * TT + 3 + half)
                    if half == 0:
                        act.wait_ge(out_stored, n * 16 + 16)
                    nc.scalar.activation(out[:, cols], pv[:, cols], ACT.Copy).then_inc(out_ready, 1)

                def period(n, j, more, ahead):
                    for u in range(NS):
                        t, h, half = u // (2 * HG), u // 2 % HG, u % 2
                        act.wait_ge(st_done, n * NS + u + 1)
                        if h == half == 0:
                            act.wait_ge(pv_done, n * 2 * TT + 2 * t + 2)
                        nc.scalar.activation(probs[:, t % 2, h, half * HALF:(half + 1) * HALF], st[half][:], ACT.Exp
                                             ).then_inc(exp_done, 1)
                        if u in (3, 7) and not (isinstance(n, int) and n == 0):
                            copy_out(n - 1, u // 4)

                all_groups(act, period)
                for half in range(2):
                    copy_out(NG - 1, half)

            @block.vector
            def _(dve):
                def period(n, j, more, ahead):
                    if more:
                        first_pass_maxima(dve, n + 1, ahead)

                all_groups(dve, period)

            @block.tensor
            def _(pe):
                def scores(n, j, s, half):
                    t, h = s // HG, s % HG
                    pe.wait_ge(exp_done, n * NS + 2 * s + half + 1)
                    if t == half == 0:
                        pe.wait_ge(max_loaded[h], n * 32 + 32)
                    nc.tensor.matmul(st[half][:], kf[j][0:ROW_M + 1, h, t * P:(t + 1) * P],
                                     qf[j][0:ROW_M + 1, h, 2 * t // TT, half * HALF:(half + 1) * HALF],
                                     start=True, stop=True).then_inc(st_done, 1)

                def weighted(n, j, t, half):
                    if half == 0:
                        pe.wait_ge(exp_done, n * NS + 2 * HG * (t + 1) + 2)
                    if t == half == 0:
                        pe.wait_ge(loaded[j], times_loaded(n, j))
                    if t == 0:
                        pe.wait_ge(out_ready, n * 2 + half + 1)
                    cols = slice(half * HALF, (half + 1) * HALF)
                    for h in range(HG):
                        m = nc.tensor.matmul(pv[32 * h:32 * h + 32, cols], va[j][:, t, h, :], probs[:, t % 2, h, cols],
                                             start=t == 0, stop=t == TT - 1, skip_group_check=True)
                    m.then_inc(pv_done, 1)

                def period(n, j, more, ahead):
                    for s in range(0, STEPS, 2):
                        t, h = s // HG, s % HG
                        for half in range(2):
                            scores(n, j, s, half)
                        if t:
                            weighted(n, j, t - 1, h // 2)
                        elif not (isinstance(n, int) and n == 0):
                            weighted(n - 1, (j - 1) % BUFS, TT - 1, h // 2)
                        for half in range(2):
                            scores(n, j, s + 1, half)
                        if more:
                            for step in (s, s + 1):
                                for half in range(2):
                                    first_pass(pe, n + 1, (j + 1) % BUFS, ahead, step, half)

                pe.sem_inc(exp_done, 2)
                pe.sem_inc(pv_done, 4)
                pe.sem_inc(out_ready, 2)
                all_groups(pe, period)
                for half in range(2):
                    weighted(NG - 1, (NG - 1) % BUFS, TT - 1, half)


def self_attention_phase(nc, x, attn_w, attn_b, w_q, w_k, w_v, w_o, b_o, mixT_d, att_d, rsum_d, t_d, vT_d, vsum_d):
    with ExitStack() as ctx:
        sb = lambda name, shape, dt=f32: ctx.enter_context(nc.sbuf_tensor(name, shape, dt))
        ps = lambda name, n: ctx.enter_context(nc.psum_tensor(name, [P, n], f32))
        sem = lambda name: ctx.enter_context(nc.semaphore(name))
        QT = TT // 2
        ident = sb("b_ident", [P, P])
        wp = sb("b_wp", [P, GROUPS, DK])
        pb = sb("b_pb", [P, 1])
        w_st = sb("b_w_st", [P, KC, 3, U])
        w_hi, w_lo = sb("b_w_hi", [P, KC, 3, U], f32r), sb("b_w_lo", [P, KC, 3, U], f32r)
        wo = sb("b_wo", [P, C])
        bo = sb("b_bo", [P, C])
        rs = sb("b_rs", [P, B, TOK // 16])
        att = [sb(f"b_att{j}", [P, GROUPS, HALF]) for j in range(2)]
        rsb = [sb(f"b_rsb{j}", [P, GROUPS, HALF]) for j in range(2)]
        mixT = sb("b_mixT", [P, KC, TOK])
        xb = [sb(f"b_xb{s}", [P, TT, C]) for s in range(2)]
        st6, mv = sb("b_st6", [P, QT, 6]), sb("b_mv", [P, QT, 2])
        var, rstd, tmp, shift = (sb(f"b_{n}", [P, 2, QT]) for n in ("var", "rstd", "tmp", "shift"))
        u = sb("b_u", [P, QT, C])
        uT_hi, uT_lo = sb("b_uT_hi", [P, KC, TOK], f32r), sb("b_uT_lo", [P, KC, TOK], f32r)
        q_hi = [sb(f"b_q_hi{s}", [P, TOK], f32r) for s in range(2)]
        q_lo = [sb(f"b_q_lo{s}", [P, TOK], f32r) for s in range(2)]
        k_hi = [sb(f"b_k_hi{s}", [P, TOK], f32r) for s in range(2)]
        k_lo = [sb(f"b_k_lo{s}", [P, TOK], f32r) for s in range(2)]
        vT32 = sb("b_vT32", [P, HALF])
        v_sb = [sb(f"b_v{s}", [P, TT, U]) for s in range(2)]
        nmax, ssum, rsum = sb("b_nmax", [P, TT]), sb("b_ssum", [P, TT]), sb("b_rsum", [P, TT])
        probs = [sb(f"b_probs{i}", [P, TOK]) for i in range(2)]
        pT = [sb(f"b_pT{i}", [P, TT, 2 * P]) for i in range(2)]
        oT = [sb(f"b_oT{i}", [P, 2 * P]) for i in range(2)]
        t_sb = [sb(f"b_t{j}", [P, QT, C]) for j in range(2)]
        st6t, mvt = sb("b_st6t", [P, QT, 6]), sb("b_mvt", [P, QT, 2])
        vart, rstdt, tmpt = (sb(f"b_{n}", [P, 2, QT]) for n in ("vart", "rstdt", "tmpt"))
        v2 = sb("b_v2", [P, QT, C])
        v2T = sb("b_v2T", [P, KC, HALF])
        vsum = sb("b_vsum", [P, KC, TT // 2])
        s_ps, pT_ps, o_ps = ps("b_s_ps", TOK), ps("b_pT_ps", TOK), ps("b_o_ps", 2 * P)
        a_ps, b_ps, c_ps = ps("b_a_ps", 2 * C), ps("b_b_ps", HALF), ps("b_c_ps", 2 * C)
        consts, proj_loaded, w_loaded, w_split = sem("b_consts"), sem("b_proj_loaded"), sem("b_w_loaded"), sem("b_w_split")
        sums_loaded = [sem(f"b_sums_loaded{i}") for i in range(2)]
        sums_inv, sums_stored = sem("b_sums_inv"), sem("b_sums_stored")
        att_loaded = [sem(f"b_att_loaded{j}") for j in range(2)]
        x_loaded = [sem(f"b_x_loaded{j}") for j in range(2)]
        mix_loaded, norm_ready = sem("b_mix_loaded"), sem("b_norm_s")
        a_done, a_read, b_done, b_read, c_done = (sem(f"b_{n}") for n in ("a_done", "a_read", "b_done", "b_read", "c_done"))
        c_read = sem("b_c_read")
        var_ready, rstd_ready, shift_ready, u_ready, res_ready = (sem(f"b_{n}_s") for n in ("var", "rstd", "shift", "u", "res"))
        uhi_ready, bhi_ready = sem("b_uhi_s"), sem("b_bhi_s")
        s_done, max_ready, exp_done = sem("b_s_done"), sem("b_max_s"), sem("b_exp_done")
        pT_done, pT_ready = sem("b_pT_done"), sem("b_pT_s")
        o_done, o_read = sem("b_o_done"), sem("b_o_read")
        vart_ready, rstdt_ready, v_ready = (sem(f"b_{n}_s") for n in ("vart", "rstdt", "v"))
        t_stored = [sem(f"b_t_stored{j}") for j in range(2)]
        vT_stored, vsum_stored = sem("b_vT_stored"), sem("b_vsum_stored")

        A_STEPS = [("mix", 0), ("mix", 1), ("mix", 2), ("mix", 3), ("ut", 0), ("ut", 1), ("v", 0), ("vt", 0),
                   ("ut", 2), ("ut", 3), ("v", 1), ("vt", 1)]
        B_STEPS = [("proj", 0), ("proj", 1), ("q", 0), ("k", 0), ("q", 1), ("k", 1)]
        HI_STEPS = B_STEPS[2:]
        C_STEPS = [("out", 0), ("out", 1), ("out", 2), ("turn", 0), ("turn", 1), ("out", 3), ("turn", 2), ("turn", 3)]
        PAIRS = TT // 2
        NA, NB, NCS = len(A_STEPS), len(B_STEPS), len(C_STEPS)
        a_at = lambda what, j: A_STEPS.index((what, j))
        b_at = lambda what, j: B_STEPS.index((what, j))
        c_at = lambda what, t: C_STEPS.index((what, t))
        W_OF = {"q": 0, "k": 1, "v": 2}
        SCALE = U ** -0.5

        BETWEEN = [
            [("out", 2, -1), ("probs", 7, -1), ("proj", 0, 1), ("vt", 1, 0), ("turn", 0, -1)],
            [("probs", 0, 0), ("half", 3, -1), ("turn", 1, -1), ("mix", 0, 1)],
            [("mix", 1, 1), ("values", 3, -1), ("probs", 1, 0), ("out", 3, -1), ("vvar", 1, -1), ("proj", 1, 1), ("var", 0, 1)],
            [("probs", 2, 0), ("half", 0, 0), ("mix", 2, 1), ("apply", 0, 1), ("values", 0, 0), ("mix", 3, 1)],
            [("vapply", 1, -1), ("ut", 0, 1), ("probs", 3, 0), ("ut", 1, 1),
             ("probs", 4, 0), ("turn", 2, -1), ("var", 1, 1), ("q", 0, 1), ("v", 0, 1)],
            [("turn", 3, -1), ("k", 0, 1), ("half", 1, 0), ("vt", 0, 1), ("apply", 1, 1)],
            [("out", 0, 0), ("values", 1, 0), ("ut", 2, 1), ("probs", 5, 0), ("out", 1, 0), ("ut", 3, 1)],
            [("q", 1, 1), ("probs", 6, 0), ("vvar", 0, 0), ("half", 2, 0), ("k", 1, 1), ("vapply", 0, 0), ("v", 1, 1), ("values", 2, 0)]]

        FRONT = [("proj", 0), ("proj", 1), ("mix", 0), ("mix", 1), ("mix", 2), ("var", 0), ("mix", 3), ("apply", 0), ("var", 1),
                 ("ut", 0), ("ut", 1), ("apply", 1), ("sums", 0), ("q", 0), ("k", 0), ("v", 0), ("vt", 0), ("ut", 2), ("ut", 3), ("q", 1), ("k", 1), ("v", 1)]

        def period(b, s, before, after):
            steps = []
            for i in range(TT):
                steps.append(("scores", i, b, s))
                steps += [(what, k, b + d, s if d == 0 else 1 - s) for what, k, d in BETWEEN[i]
                          if d == 0 or (d == 1 and after) or (d == -1 and before)]
            return steps

        def all_images(eng, run):
            run([(what, k, 0, 0) for what, k in FRONT])
            run(period(0, 0, False, True))
            with eng.Fori(1, B - 1, 2) as b:
                run(period(b, 1, True, True))
                run(period(b + 1, 0, True, True))
            run(period(B - 1, 1, True, False))
            run([(what, k, B - 1, 1) for slot in BETWEEN for what, k, d in slot if d == -1])

        half = lambda j: slice(j * HALF, (j + 1) * HALF)
        tile = lambda t: slice(t * P, (t + 1) * P)
        pair = lambda t: slice(2 * t, 2 * t + 2)
        cols = lambda t: slice(2 * t * P, 2 * (t + 1) * P)
        by_tile = lambda ap: ap.rearrange("p (t c) -> p t c", t=2)
        by_chunk = lambda ap: ap.rearrange("p (c n) -> p c n", c=KC)

        with nc.Block() as block:
            @block.sync
            def _(sp):
                x_v = x.rearrange("b h w c -> b (h w) c").rearrange("b (t p) c -> b p t c", p=P)
                t_v = t_d.rearrange("b (t p) c -> b p t c", p=P)
                vT_v = vT_d.rearrange("b c p n -> b p c n")
                def load_att(n, j):
                    sp.wait_ge(b_done, n * NB - NB + j + 1)
                    sp.nop(nofuse=True)
                    load_weighted(n, j)
                    load_rsum(n, j)

                def load_weighted(n, j):
                    sp.dma_start(att[j][:], att_d[n].rearrange("g p n -> p g n")[:, :, half(j)]).then_inc(att_loaded[j], 16)

                def load_rsum(n, j):
                    for g in range(GROUPS):
                        src = rsum_d[n, g].rearrange("h (a n) -> h a n", a=1)[:, :, half(j)]
                        sp.dma_start(rsb[j][:, g], src.to_broadcast([HG, 32, HALF])).then_inc(att_loaded[j], 16)

                def load_mix(n, wait=True):
                    if wait:
                        sp.wait_ge(a_done, n * NA - NA + a_at("mix", 3) + 1)
                        sp.nop(nofuse=True)
                    sp.dma_start(mixT[:, 0, :], mixT_d[n, 0]).then_inc(mix_loaded, 16)
                    sp.dma_start(mixT[0:CONV_OUT - P, 1, :], mixT_d[n, 1, 0:CONV_OUT - P]).then_inc(mix_loaded, 16)

                def load_x(n, s, j, wait=True):
                    if wait:
                        sp.wait_ge(c_read, (n - 2) * NCS + c_at("out", 2 * j + 1) + 2)
                        sp.nop(nofuse=True)
                    sp.dma_start(xb[s][:, j * QT:(j + 1) * QT, :], x_v[n, :, j * QT:(j + 1) * QT, :]).then_inc(x_loaded[j], 16)

                def store_t(n, j):
                    sp.wait_ge(c_read, n * NCS + c_at("out", 2 * j + 1) + 2)
                    sp.nop(nofuse=True)
                    sp.dma_start(t_v[n, :, j * QT:(j + 1) * QT, :], t_sb[j][:]).then_inc(t_stored[j], 16)

                def store_v(n, j):
                    sp.wait_ge(c_read, n * NCS + c_at("turn", 2 * j + 1) + 2)
                    sp.nop(nofuse=True)
                    sp.dma_start(vT_v[n, :, :, half(j)], v2T[:]).then_inc(vT_stored, 16)
                    if j == 1:
                        sp.dma_start(vsum_d[n], vsum[:]).then_inc(vsum_stored, 16)

                def image(b, s, before, after, ahead):
                    if before:
                        store_v(b - 1, 0)
                        if after:
                            load_x(b + 1, 1 - s, 1)
                        store_t(b - 1, 1)
                    if ahead:
                        load_att(b + 2, 0)
                        load_att(b + 2, 1)
                        load_mix(b + 2)
                    if before:
                        store_v(b - 1, 1)
                    store_t(b, 0)
                    if ahead:
                        load_x(b + 2, s, 0)

                def load_sums(b):
                    src = att_d[b].rearrange("g (h r) n -> (g h) r n", r=32)[:, DH].rearrange("q (j c) -> q j c", j=16)
                    sp.dma_start(rs[:, b], src).then_inc(sums_loaded[min(b, 1)], 16)

                load_sums(0)
                sp.wait_ge(sums_inv, 1)
                sp.dma_start(rsum_d[0].rearrange("g h (j c) -> (g h j) c", j=16), rs[:, 0]).then_inc(sums_stored, 16)
                load_weighted(0, 0)
                sp.wait_ge(sums_stored, 16)
                load_rsum(0, 0)
                load_weighted(0, 1)
                load_rsum(0, 1)
                load_mix(0, False)
                for j in range(2):
                    load_x(0, 0, j, False)
                for b in range(1, B):
                    load_sums(b)
                for stored in t_stored:
                    sp.sem_inc(stored, 16)
                sp.sem_inc(vT_stored, 16)
                sp.sem_inc(vsum_stored, 16)
                sp.wait_ge(sums_inv, 2)
                sp.dma_start(rsum_d[1:B].rearrange("b g h (j c) -> (g h j) b c", j=16), rs[:, 1:B]).then_inc(sums_stored, 16)
                for j in range(2):
                    sp.wait_ge(x_loaded[j], 16)
                    load_x(1, 1, j, False)
                sp.wait_ge(sums_stored, 32)
                for j in range(2):
                    load_att(1, j)
                load_mix(1)
                image(0, 0, False, True, True)
                with sp.Fori(1, B - 3, 2) as b:
                    image(b, 1, True, True, True)
                    image(b + 1, 0, True, True, True)
                image(B - 3, 1, True, True, True)
                image(B - 2, 0, True, True, False)
                image(B - 1, 1, True, False, False)
                store_v(B - 1, 0)
                store_t(B - 1, 1)
                store_v(B - 1, 1)
                for stored in t_stored:
                    sp.wait_ge(stored, 16 * (B + 1))
                sp.wait_ge(vT_stored, 16 * (2 * B + 1))
                sp.wait_ge(vsum_stored, 16 * (B + 1))

            @block.gpsimd
            def _(pool):
                nc.gpsimd.memset(wp[:], 0.0).then_inc(consts, 1)
                make_identity(nc, pool, ident[:], consts)

                def run(steps):
                    for what, k, n, s in steps:
                        if what == "proj":
                            pool.wait_ge(att_loaded[k], n * (16 * (1 + GROUPS)) + 16 * (1 + GROUPS))
                            nc.gpsimd.tensor_tensor(att[k][:], att[k][:], rsb[k][:], ALU.mult).then_inc(norm_ready, 1)
                        if what == "apply":
                            x1 = xb[s][:, k * QT:(k + 1) * QT, :]
                            pool.wait_ge(u_ready, n * 2 + k + 1)
                            nc.gpsimd.tensor_tensor(x1, x1, u[:], ALU.add)
                            pool.drain()
                            pool.wait_ge(w_loaded, 16 * 5)
                            nc.gpsimd.tensor_tensor(x1, x1, bo_all, ALU.add).then_inc(res_ready, 1)

                bo_all = bo[:].rearrange("p (a c) -> p a c", a=1).to_broadcast([P, QT, C])
                all_images(pool, run)

            @block.scalar
            def _(act):
                def rsqrt(out, in_):
                    nc.scalar.activation(out, in_, ACT.Ln)
                    act.drain()
                    return nc.scalar.activation(out, out, ACT.Exp, scale=-0.5)

                def run(steps):
                    for what, k, n, s in steps:
                        if what == "scores":
                            act.wait_ge(max_ready, n * TT + k + 1)
                            nc.scalar.activation(probs[k % 2][:], s_ps[:], ACT.Exp, bias=nmax[:, k:k + 1], accum_out=ssum[:, k:k + 1]
                                                 ).then_inc(exp_done, 1)
                        elif what == "probs":
                            act.wait_ge(pT_done, n * TT + k + 1)
                            nc.scalar.activation(pT[k // 2 % 2][:, :, tile(k % 2)], pT_ps[:].rearrange("p (t q) -> p t q", t=TT),
                                                 ACT.Copy).then_inc(pT_ready, 1)
                        elif what == "values":
                            act.wait_ge(o_done, n * PAIRS + k + 1)
                            nc.scalar.activation(oT[k % 2][:], o_ps[:], ACT.Copy).then_inc(o_read, 1)
                        elif what == "proj":
                            act.wait_ge(b_done, n * NB + b_at("proj", k) + 1)
                            nc.scalar.activation(mixT[DK:P, 1, half(k)], b_ps[DK:P, :], ACT.Identity, bias=pb[DK:P]
                                                 ).then_inc(b_read, 1)
                        elif what == "var":
                            act.wait_ge(var_ready, n * 2 + k + 1)
                            rsqrt(rstd[:, k], var[:, k]).then_inc(rstd_ready, 1)
                        elif what == "vvar":
                            act.wait_ge(vart_ready, n * 2 + k + 1)
                            rsqrt(rstdt[:, k], vart[:, k]).then_inc(rstdt_ready, 1)
                        elif what == "apply":
                            act.wait_ge(shift_ready, n * 2 + k + 1)
                            act.wait_ge(res_ready, n * 2 + k + 1)
                            if k:
                                act.wait_ge(a_done, n * NA + a_at("ut", 1) + 1)
                            for i in range(QT):
                                last = nc.scalar.activation(u[:, i, :], xb[s][:, k * QT + i, :], ACT.Identity,
                                                            bias=shift[:, k, i:i + 1], scale=rstd[:, k, i:i + 1])
                            last.then_inc(u_ready, 1)
                        elif what == "ut":
                            act.wait_ge(a_done, n * NA + a_at("ut", k) + 1)
                            nc.scalar.activation(uT_hi[:, :, cols(k)], by_chunk(a_ps[:]), ACT.Copy).then_inc(uhi_ready, 1)
                        elif what in ("q", "k"):
                            act.wait_ge(b_done, n * NB + b_at(what, k) + 1)
                            hi = q_hi if what == "q" else k_hi
                            nc.scalar.activation(hi[s][:, half(k)], b_ps[:], ACT.Copy, scale=SCALE if what == "q" else 1.0
                                                 ).then_inc(bhi_ready, 1)
                        elif what == "v":
                            act.wait_ge(a_done, n * NA + a_at("v", k) + 1)
                            nc.scalar.activation(vT32[:], a_ps[:], ACT.Copy).then_inc(a_read, 1)
                        elif what == "vt":
                            act.wait_ge(a_done, n * NA + a_at("vt", k) + 1)
                            nc.scalar.activation(v_sb[s][:, k * QT:(k + 1) * QT, :], a_ps[:].rearrange("p (t u) -> p t u", u=U),
                                                 ACT.Copy).then_inc(a_read, 1)
                        elif what == "turn":
                            act.wait_ge(c_done, n * NCS + c_at("turn", k) + 1)
                            if k % 2 == 0:
                                act.wait_ge(vT_stored, n * 32 + 16 * (k // 2) + 16)
                            if k == 0:
                                act.wait_ge(vsum_stored, n * 16 + 16)
                            for c in range(KC):
                                last = nc.scalar.activation(v2T[:, c, cols(k % 2)], by_chunk(c_ps[:])[:, c], ACT.Copy,
                                                            accum_out=vsum[:, c, k:k + 1])
                            last.then_inc(c_read, 1)

                act.wait_ge(consts, 2)
                for g in range(GROUPS):
                    for h in range(HG):
                        act.dma_start(wp[32 * h:32 * h + DH, g], attn_w[(g * HG + h) * DH:(g * HG + h + 1) * DH]).then_inc(proj_loaded, 16)
                act.dma_start(pb[DK:P], attn_b.rearrange("(p a) -> p a", a=1)).then_inc(proj_loaded, 16)
                for i, w in enumerate((w_q, w_k, w_v)):
                    act.dma_start(w_st[:, :, i], w.rearrange("(k p) u -> p k u", p=P)).then_inc(w_loaded, 16)
                act.dma_start(wo[:], w_o).then_inc(w_loaded, 16)
                act.dma_start(bo[:], b_o.rearrange("(a c) -> a c", a=1).to_broadcast([P, C])).then_inc(w_loaded, 16)
                nc.scalar.preload_act_table_set("natural_log_exp_and_others")
                act.wait_ge(proj_loaded, 16 * (NH + 1))
                all_images(act, run)

            @block.vector
            def _(dve):
                def spread(buf, st, m, v, ready):
                    dve.drain()
                    for i in range(QT):
                        nc.vector.bn_stats(st[:, i, :], buf[:, i, :])
                    dve.drain()
                    for i in range(QT):
                        nc.vector.bn_aggr(m[:, i, :], st[:, i, :])
                    dve.drain()
                    nc.vector.tensor_scalar(v, m[:, :, 1], 1e-5, None, ALU.add).then_inc(ready, 1)

                def scales(m, r, v, tm, sh, ready):
                    newton(nc, dve, r, v, tm)
                    nc.vector.scalar_tensor_tensor(sh, m[:, :, 0], -1.0, r, ALU.mult, ALU.mult).then_inc(ready, 1)

                def run(steps):
                    for what, k, n, s in steps:
                        if what == "scores":
                            dve.wait_ge(s_done, n * TT + k + 1)
                            nc.vector.tensor_reduce(nmax[:, k:k + 1], s_ps[:], axis=AX.X, op=ALU.max, negate=True).then_inc(max_ready, 1)
                        elif what == "values":
                            dve.wait_ge(exp_done, n * TT + (k + 1) * 2 + 1)
                            nc.vector.reciprocal(rsum[:, pair(k)], ssum[:, pair(k)])
                            dve.drain()
                        elif what == "mix":
                            dve.wait_ge(a_done, n * NA + a_at("mix", k) + 1)
                            dve.wait_ge(x_loaded[k // 2], n * 16 + 16)
                            nc.vector.tensor_tensor(xb[s][:, pair(k), :], by_tile(a_ps[:]), xb[s][:, pair(k), :], ALU.add).then_inc(a_read, 1)
                        elif what == "var":
                            spread(xb[s][:, k * QT:(k + 1) * QT, :], st6, mv, var[:, k], var_ready)
                        elif what == "vvar":
                            spread(t_sb[k], st6t, mvt, vart[:, k], vart_ready)
                        elif what == "apply":
                            dve.wait_ge(rstd_ready, n * 2 + k + 1)
                            scales(mv, rstd[:, k], var[:, k], tmp[:, k], shift[:, k], shift_ready)
                        elif what == "vapply":
                            dve.wait_ge(rstdt_ready, n * 2 + k + 1)
                            newton(nc, dve, rstdt[:, k], vart[:, k], tmpt[:, k])
                            for i in range(QT):
                                last = nc.vector.tensor_scalar(v2[:, i, :], t_sb[k][:, i, :], mvt[:, i, 0:1], rstdt[:, k, i:i + 1],
                                                               ALU.subtract, ALU.mult)
                            last.then_inc(v_ready, 1)
                        elif what == "sums":
                            dve.wait_ge(sums_loaded[1], 16 * (B - 1))
                            nc.vector.reciprocal(rs[:, 1:B], rs[:, 1:B]).then_inc(sums_inv, 1)
                        elif what == "ut":
                            dve.wait_ge(uhi_ready, n * PAIRS + k + 1)
                            nc.vector.tensor_tensor(uT_lo[:, :, cols(k)], by_chunk(a_ps[:]), bits(uT_hi[:, :, cols(k)]), ALU.subtract).then_inc(a_read, 1)
                        elif what in ("q", "k"):
                            dve.wait_ge(bhi_ready, n * len(HI_STEPS) + HI_STEPS.index((what, k)) + 1)
                            hi, lo = (q_hi, q_lo) if what == "q" else (k_hi, k_lo)
                            nc.vector.scalar_tensor_tensor(lo[s][:, half(k)], b_ps[:], SCALE if what == "q" else 1.0,
                                                           bits(hi[s][:, half(k)]), ALU.mult, ALU.subtract).then_inc(b_read, 1)
                        elif what == "out":
                            dve.wait_ge(c_done, n * NCS + c_at("out", k) + 1)
                            if k % 2 == 0:
                                dve.wait_ge(res_ready, n * 2 + k // 2 + 2)
                                dve.wait_ge(t_stored[k // 2], n * 16 + 16)
                            for t in range(2 * k, 2 * k + 2):
                                last = nc.vector.scalar_tensor_tensor(t_sb[k // 2][:, t % QT, :], by_tile(c_ps[:])[:, t % 2, :], rsum[:, t:t + 1],
                                                                      xb[s][:, t, :], ALU.mult, ALU.add)
                            last.then_inc(c_read, 1)

                dve.sem_inc(res_ready, 1)
                dve.wait_ge(sums_loaded[0], 16)
                nc.vector.reciprocal(rs[:, 0], rs[:, 0]).then_inc(sums_inv, 1)
                dve.wait_ge(w_loaded, 16 * 5)
                nc.vector.tensor_copy(w_hi[:], w_st[:])
                dve.drain()
                nc.vector.tensor_tensor(w_lo[:], w_st[:], bits(w_hi[:]), ALU.subtract).then_inc(w_split, 1)
                all_images(dve, run)

            @block.tensor
            def _(pe):
                def run(steps):
                    for what, k, n, s in steps:
                        if what == "scores":
                            pe.wait_ge(exp_done, n * TT + k + 1)
                            if k == 0:
                                pe.wait_ge(b_read, n * NB + b_at("k", 1) + 2)
                            for j in range(2):
                                for i, (q, kk) in enumerate(((q_hi, k_hi), (q_hi, k_lo), (q_lo, k_hi))):
                                    m = nc.tensor.matmul(s_ps[:, half(j)], q[s][:, tile(k)], kk[s][:, half(j)], start=i == 0, stop=i == 2)
                            m.then_inc(s_done, 1)
                        elif what == "probs":
                            pe.wait_ge(exp_done, n * TT + k + 2)
                            pe.wait_ge(pT_ready, n * TT + k + 1)
                            for t in range(TT):
                                m = nc.tensor.transpose(pT_ps[:, tile(t)], probs[k % 2][:, tile(t)], ident[:])
                            m.then_inc(pT_done, 1)
                        elif what in ("half", "values"):
                            if what == "half":
                                pe.wait_ge(pT_ready, n * TT + (k + 1) * 2 + 1)
                                pe.wait_ge(o_read, n * PAIRS + k + 1)
                                pe.wait_ge(a_read, n * NA + NA + 1)
                            for t in range(QT) if what == "half" else range(QT, TT):
                                m = nc.tensor.matmul(o_ps[:], v_sb[s][:, t, :], pT[k % 2][:, t, :], start=t == 0, stop=t == TT - 1)
                            if what == "values":
                                m.then_inc(o_done, 1)
                        elif what == "proj":
                            pe.wait_ge(norm_ready, n * 2 + k + 1)
                            pe.wait_ge(b_read, n * NB + b_at("proj", k) + 1)
                            for g in range(GROUPS):
                                m = nc.tensor.matmul(b_ps[DK:P, :], wp[:, g, :], att[k][:, g, :], start=g == 0, stop=g == GROUPS - 1)
                            m.then_inc(b_done, 1)
                        elif what == "mix":
                            pe.wait_ge(a_read, n * NA + a_at("mix", k) + 1)
                            if k == 0:
                                pe.wait_ge(mix_loaded, n * 32 + 32)
                            pe.wait_ge(b_read, n * NB + b_at("proj", k // 2) + 2)
                            for t in range(2):
                                for c in range(KC):
                                    m = nc.tensor.transpose(by_tile(a_ps[:])[:, t, tile(c)], mixT[:, c, tile(2 * k + t)], ident[:])
                            m.then_inc(a_done, 1)
                        elif what == "ut":
                            pe.wait_ge(a_read, n * NA + a_at("ut", k) + 1)
                            pe.wait_ge(u_ready, n * 2 + k // 2 + 1)
                            for t in range(2):
                                for c in range(KC):
                                    m = nc.tensor.transpose(by_chunk(a_ps[:])[:, c, tile(t)], u[:, (2 * k + t) % QT, tile(c)], ident[:])
                            m.then_inc(a_done, 1)
                        elif what in W_OF:
                            pe.wait_ge(w_split, 1)
                            pe.wait_ge(a_read, n * NA + a_at("ut", 2 * k + 1) + 2)
                            if what == "v":
                                bank, done = a_ps, a_done
                                pe.wait_ge(a_read, n * NA + a_at("v", k) + 1)
                            else:
                                bank, done = b_ps, b_done
                                pe.wait_ge(b_read, n * NB + b_at(what, k) + 1)
                            i, total = 0, 3 * KC
                            for c in range(KC):
                                for w, uT in ((w_hi, uT_hi), (w_hi, uT_lo), (w_lo, uT_hi)):
                                    m = nc.tensor.matmul(bank[:], w[:, c, W_OF[what], :], uT[:, c, half(k)], start=i == 0, stop=i == total - 1)
                                    i += 1
                            m.then_inc(done, 1)
                        elif what == "vt":
                            pe.wait_ge(a_read, n * NA + a_at("vt", k) + 1)
                            for t in range(QT):
                                m = nc.tensor.transpose(a_ps[:, tile(t)], vT32[:, tile(t)], ident[:])
                            m.then_inc(a_done, 1)
                        elif what == "out":
                            pe.wait_ge(o_read, n * PAIRS + k + 2)
                            pe.wait_ge(c_read, n * NCS + c_at("out", k) + 1)
                            for t in range(2):
                                m = nc.tensor.matmul(by_tile(c_ps[:])[:, t], oT[k % 2][:, tile(t)], wo[:], start=True, stop=True)
                            m.then_inc(c_done, 1)
                        elif what == "turn":
                            pe.wait_ge(v_ready, n * 2 + k // 2 + 1)
                            pe.wait_ge(c_read, n * NCS + c_at("turn", k) + 1)
                            for t in range(2):
                                for c in range(KC):
                                    m = nc.tensor.transpose(by_chunk(c_ps[:])[:, c, tile(t)], v2[:, (2 * k + t) % QT, tile(c)], ident[:])
                            m.then_inc(c_done, 1)

                pe.sem_inc(exp_done, 1)
                pe.sem_inc(pT_ready, 1)
                pe.sem_inc(o_read, 1)
                pe.sem_inc(a_read, 1)
                pe.sem_inc(b_read, 1)
                pe.sem_inc(c_read, 1)
                pe.wait_ge(consts, 2)
                pe.wait_ge(proj_loaded, 16 * (NH + 1))
                all_images(pe, run)


def router_phase(nc, w_r, b_r, vsum_d, wts_d, idx_d):
    CAPACITY = float(-(-B * TOK * 5 // (4 * E)))
    with ExitStack() as ctx:
        sb = lambda name, shape, dt=f32: ctx.enter_context(nc.sbuf_tensor(name, shape, dt))
        sem = lambda name: ctx.enter_context(nc.semaphore(name))
        parts = sb("r2_parts", [P, B, KC, TT // 2])
        vm = sb("r2_vm", [P, KC, B])
        wr = sb("r2_wr", [P, KC, E])
        br = sb("r2_br", [B, E])
        ones = sb("r2_ones", [B, B])
        lg, rw, scale = sb("r2_lg", [B, E]), sb("r2_rw", [B, E]), sb("r2_scale", [B, E])
        nmax, total = sb("r2_nmax", [B, 1]), sb("r2_total", [B, 1])
        best, idx = sb("r2_best", [B, 8]), sb("r2_idx", [B, 8], mybir.dt.uint32)
        wts = sb("r2_wts", [B, TOPK])
        logits = ctx.enter_context(nc.psum_tensor("r2_logits", [B, E], f32))
        loads = ctx.enter_context(nc.psum_tensor("r2_loads", [B, E], f32))
        loaded, made, vm_ready, logits_done = sem("r2_loaded"), sem("r2_made"), sem("r2_vm_s"), sem("r2_logits_done")
        max_ready, exp_ready, rw_ready, loads_done = sem("r2_max_s"), sem("r2_exp_s"), sem("r2_rw_s"), sem("r2_loads_done")
        chosen, stored = sem("r2_chosen"), sem("r2_stored")

        with nc.Block() as block:
            @block.sync
            def _(sp):
                sp.dma_start(parts[:].rearrange("p b c f -> p b (c f)"), vsum_d.rearrange("b p c f -> p b (c f)")).then_inc(loaded, 16)
                sp.dma_start(wr[:], w_r.rearrange("(c p) e -> p c e", p=P)).then_inc(loaded, 16)
                sp.dma_start(br[:], b_r.rearrange("(a e) -> a e", a=1).to_broadcast([B, E])).then_inc(loaded, 16)
                sp.wait_ge(chosen, 1)
                sp.dma_start(wts_d, wts[:]).then_inc(stored, 16)
                sp.dma_start(idx_d, idx[:, 0:TOPK]).then_inc(stored, 16)
                sp.wait_ge(stored, 32)

            @block.scalar
            def _(act):
                for i, (out, in_) in enumerate(((rw, lg), (rw, lg), (wts, best[:, 0:TOPK]))):
                    act.wait_ge(max_ready, i + 1)
                    nc.scalar.activation(out[:], in_ if i == 2 else in_[:], ACT.Exp, bias=nmax[:], accum_out=total[:]
                                         ).then_inc(exp_ready, 1)

            @block.vector
            def _(dve):
                def softmax(out, in_, i):
                    nc.vector.tensor_reduce(nmax[:], in_, axis=AX.X, op=ALU.max, negate=True).then_inc(max_ready, 1)
                    dve.wait_ge(exp_ready, i + 1)
                    nc.vector.reciprocal(total[:], total[:])
                    dve.drain()
                    return nc.vector.tensor_scalar(out, out, total[:], None, ALU.mult)

                nc.vector.memset(ones[:], 1.0).then_inc(made, 1)
                dve.wait_ge(loaded, 48)
                nc.vector.tensor_reduce(vm[:].rearrange("p c b -> p b c"), parts[:], axis=AX.X, op=ALU.add).then_inc(vm_ready, 1)
                dve.wait_ge(logits_done, 1)
                nc.vector.scalar_tensor_tensor(lg[:], logits[:], 1.0 / TOK, br[:], ALU.mult, ALU.add)
                dve.drain()
                softmax(rw[:], lg[:], 0).then_inc(rw_ready, 1)
                dve.wait_ge(loads_done, 1)
                nc.vector.tensor_scalar(scale[:], loads[:], float(TOK), None, ALU.mult)
                dve.drain()
                nc.vector.reciprocal(scale[:], scale[:])
                dve.drain()
                nc.vector.tensor_scalar(scale[:], scale[:], CAPACITY, 1.0, ALU.mult, ALU.min)
                dve.drain()
                nc.vector.tensor_tensor(lg[:], rw[:], scale[:], ALU.mult)
                dve.drain()
                softmax(rw[:], lg[:], 1)
                dve.drain()
                nc.vector.max(best[:], rw[:])
                dve.drain()
                nc.vector.max_index(idx[:], best[:], rw[:])
                softmax(wts[:], best[:, 0:TOPK], 2).then_inc(chosen, 1)

            @block.tensor
            def _(pe):
                pe.wait_ge(vm_ready, 1)
                for c in range(KC):
                    m = nc.tensor.matmul(logits[:], vm[:, c, :], wr[:, c, :], start=c == 0, stop=c == KC - 1)
                m.then_inc(logits_done, 1)
                pe.wait_ge(made, 1)
                pe.wait_ge(rw_ready, 1)
                nc.tensor.matmul(loads[:], ones[:], rw[:], start=True, stop=True).then_inc(loads_done, 1)


def expert_phase(nc, w1, b1, w2, b2, gamma, beta, t_d, vT_d, wts_d, idx_d, out):
    with ExitStack() as ctx:
        sb = lambda name, shape, dt=f32: ctx.enter_context(nc.sbuf_tensor(name, shape, dt))
        ps = lambda name, n: ctx.enter_context(nc.psum_tensor(name, [P, n], f32))
        sem = lambda name: ctx.enter_context(nc.semaphore(name))
        HT = TT // 2
        UNITS = 2 * TOPK * FC
        LATE = 3
        NW = 2 * TOPK
        HB = 4
        ident = sb("x_ident", [P, P])
        gam, bet = sb("x_gam", [P, C]), sb("x_bet", [P, C])
        idx = sb("x_idx", [1, TOPK], mybir.dt.uint32)
        w1_st, w2_st = sb("x_w1_st", [P, TOPK, KC, F]), sb("x_w2_st", [P, TOPK, FC, C])
        w1_hi = [sb(f"x_w1_hi{s}", [P, TOPK, KC, F], f32r) for s in range(2)]
        w1_lo = [sb(f"x_w1_lo{s}", [P, TOPK, KC, F], f32r) for s in range(2)]
        w2_hi = [sb(f"x_w2_hi{s}", [P, TOPK, FC, C], f32r) for s in range(2)]
        w2_lo = [sb(f"x_w2_lo{s}", [P, TOPK, FC, C], f32r) for s in range(2)]
        b1_sb = [sb(f"x_b1{s}", [P, TOPK, FC]) for s in range(2)]
        b2_sb = [sb(f"x_b2{s}", [P, TOPK, KC]) for s in range(2)]
        wts = [sb(f"x_wts{s}", [P, TOPK]) for s in range(2)]
        b2w = [sb(f"x_b2w{s}", [P, KC]) for s in range(2)]
        vT = [sb(f"x_vT{s}", [P, KC, TOK]) for s in range(2)]
        v_hi = [sb(f"x_v_hi{s}", [P, KC, TOK], f32r) for s in range(2)]
        v_lo = [sb(f"x_v_lo{s}", [P, KC, TOK], f32r) for s in range(2)]
        t_sb = sb("x_t", [P, HT, C])
        hid = [sb(f"x_hid{i}", [P, HALF]) for i in range(2)]
        h_hi = [sb(f"x_h_hi{i}", [P, HALF], f32r) for i in range(HB)]
        h_lo = [sb(f"x_h_lo{i}", [P, HALF], f32r) for i in range(HB)]
        z = sb("x_z", [P, KC, HALF])
        zt = sb("x_zt", [P, HT, C])
        st6, mv = sb("x_st6", [P, HT, 6]), sb("x_mv", [P, HT, 2])
        var, rstd, tmp = sb("x_var", [P, HT]), sb("x_rstd", [P, HT]), sb("x_tmp", [P, HT])
        h_ps = [ps(f"x_h_ps{i}", HALF) for i in range(2)]
        y_ps = [[ps(f"x_y_ps{j}{c}", HALF) for c in range(KC)] for j in range(2)]
        z_ps = [ps(f"x_z_ps{i}", 2 * C) for i in range(2)]
        consts, idx_loaded, small_loaded, v_loaded = (sem(f"x_{n}") for n in ("consts", "idx_l", "small_l", "v_l"))
        w_loaded = [sem(f"x_w_loaded{i}") for i in range(NW)]
        rows_loaded, t_loaded = sem("x_rows_l"), sem("x_t_l")
        whi_ready, w_split, vhi_ready, v_split = sem("x_whi_s"), sem("x_w_split"), sem("x_vhi_s"), sem("x_v_split")
        h_done, hid_ready, h_split, y_done = sem("x_h_done"), sem("x_hid_s"), sem("x_h_split"), sem("x_y_done")
        z_ready, turned, zt_ready = sem("x_z_s"), sem("x_turned"), sem("x_zt_s")
        var_ready, rstd_ready, normed_ready, out_ready, out_stored = (sem(f"x_{n}") for n in ("var_s", "rstd_s", "normed_s", "out_s", "out_stored"))

        def period(b, s, before, after):
            steps = []
            for k in range(UNITS):
                steps.append(("hidden", k, b, s))
                if k >= LATE:
                    steps.append(("expert", k - LATE, b, s))
                elif before:
                    steps.append(("expert", UNITS - LATE + k, b - 1, 1 - s))
                j = k // (UNITS // 2)
                if before or j:
                    n, q = (b, s) if j else (b - 1, 1 - s)
                    what = {LATE - 1: "sum", LATE + 1: "turn", LATE + 2: "stats", LATE + 3: "rsqrt", LATE + 4: "norm"}.get(k % (UNITS // 2))
                    if what:
                        steps.append((what, 1 - j, n, q))
                if k == UNITS - 4 and after:
                    steps.append(("split", 0, b + 1, 1 - s))
                if 0 <= k - UNITS // 2 < NW and after:
                    steps.append(("weights", k - UNITS // 2, b + 1, 1 - s))
            return steps

        def all_images(eng, run):
            run([("split", 0, 0, 0)] + [("weights", i, 0, 0) for i in range(NW)])
            run(period(0, 0, False, True))
            with eng.Fori(1, B - 1, 2) as b:
                run(period(b, 1, True, True))
                run(period(b + 1, 0, True, True))
            run(period(B - 1, 1, True, False))
            run([("expert", UNITS - LATE + k, B - 1, 1) for k in range(LATE)])
            run([(what, 1, B - 1, 1) for what in ("sum", "turn", "stats", "rsqrt", "norm")])

        half = lambda j: slice(j * HALF, (j + 1) * HALF)
        tile = lambda t: slice(t * P, (t + 1) * P)
        def weight(i, s):
            k, second = i // 2, i % 2
            return [w[:, k] for w in ((w2_st, w2_hi[s], w2_lo[s]) if second else (w1_st, w1_hi[s], w1_lo[s]))]

        unit = lambda k: (k // (UNITS // 2), k // FC % TOPK, k % FC)

        with nc.Block() as block:
            @block.sync
            def _(sp):
                out_v = out.rearrange("b h w c -> b (h w) c").rearrange("b (t p) c -> b p t c", p=P)
                t_v = t_d.rearrange("b (t p) c -> b p t c", p=P)

                def load_tokens(n, s, first=False):
                    if not first:
                        sp.wait_ge(z_ready, n * 2)
                        sp.nop(nofuse=True)
                    sp.dma_start(vT[s][:], vT_d[n].rearrange("c p n -> p c n")).then_inc(v_loaded, 16)
                    sp.dma_start(wts[s][:], wts_d[n].rearrange("(a k) -> a k", a=1).to_broadcast([P, TOPK])).then_inc(small_loaded, 16)

                def load_experts(n, s, first=False):
                    sp.dma_start(idx[:], idx_d[n].rearrange("(a k) -> a k", a=1)).then_inc(idx_loaded, 16)
                    if first:
                        load_tokens(n, s, first)
                    sp.wait_ge(idx_loaded, n * 16 + 16)
                    sp.nop(nofuse=True)
                    chosen = [sp.value_load(idx[0:1, k:k + 1], min_val=0, max_val=E - 1) for k in range(TOPK)]
                    if not first:
                        sp.wait_ge(w_split, n * NW)
                        sp.nop(nofuse=True)
                    for k, e in enumerate(chosen):
                        sp.dma_start(w1_st[:, k], w1[e].rearrange("(c p) f -> p c f", p=P)).then_inc(w_loaded[2 * k], 16)
                        sp.dma_start(w2_st[:, k], w2[e].rearrange("(c p) d -> p c d", p=P)).then_inc(w_loaded[2 * k + 1], 16)
                    if not first:
                        sp.wait_ge(small_loaded, n * (16 * (2 * TOPK + 1)))
                        sp.nop(nofuse=True)
                        load_tokens(n, s)
                    with nc.allow_non_contiguous_dma(reason="biases of an expert, a word per partition"):
                        for k, e in enumerate(chosen):
                            sp.dma_start(b1_sb[s][:, k], b1[e].rearrange("(c p) -> p c", p=P)).then_inc(small_loaded, 16)
                            sp.dma_start(b2_sb[s][:, k], b2[e].rearrange("(c p) -> p c", p=P)).then_inc(small_loaded, 16)

                def load_t(n, j, first=False):
                    if not first:
                        sp.wait_ge(out_stored, n * 32 + j * 16)
                        sp.nop(nofuse=True)
                    sp.dma_start(t_sb[:], t_v[n, :, j * HT:(j + 1) * HT, :]).then_inc(t_loaded, 16)

                def store(n, j):
                    sp.wait_ge(out_ready, n * 2 + j + 2)
                    sp.nop(nofuse=True)
                    sp.dma_start(out_v[n, :, j * HT:(j + 1) * HT, :], t_sb[:]).then_inc(out_stored, 16)

                def image(b, s, before, after):
                    if after:
                        load_experts(b + 1, 1 - s)
                    if before:
                        store(b - 1, 1)
                        load_t(b, 0)
                    store(b, 0)
                    load_t(b, 1)

                load_experts(0, 0, first=True)
                load_t(0, 0, first=True)
                sp.dma_start(gam[:], gamma.rearrange("(a c) -> a c", a=1).to_broadcast([P, C])).then_inc(rows_loaded, 16)
                sp.dma_start(bet[:], beta.rearrange("(a c) -> a c", a=1).to_broadcast([P, C])).then_inc(rows_loaded, 16)
                image(0, 0, False, True)
                with sp.Fori(1, B - 2, 2) as b:
                    image(b, 1, True, True)
                    image(b + 1, 0, True, True)
                image(B - 1, 1, True, False)
                store(B - 1, 1)
                sp.wait_ge(out_stored, 32 * B)

            @block.gpsimd
            def _(pool):
                wide = lambda row: row[:].rearrange("p (a c) -> p a c", a=1).to_broadcast([P, HT, C])

                def run(steps):
                    for what, k, n, s in steps:
                        if what == "weights":
                            pool.wait_ge(whi_ready, n * NW + k + 1)
                            st, hi, lo = weight(k, s)
                            nc.gpsimd.tensor_tensor(lo, st, bits(hi), ALU.subtract).then_inc(w_split, 1)
                        if what == "norm":
                            pool.wait_ge(rows_loaded, 32)
                            pool.wait_ge(normed_ready, n * 2 + k + 1)
                            nc.gpsimd.tensor_tensor(zt[:], zt[:], wide(gam), ALU.mult)
                            pool.drain()
                            nc.gpsimd.tensor_tensor(zt[:], zt[:], wide(bet), ALU.add)
                            pool.drain()
                            pool.wait_ge(t_loaded, n * 32 + k * 16 + 16)
                            nc.gpsimd.tensor_tensor(t_sb[:], t_sb[:], zt[:], ALU.add).then_inc(out_ready, 1)

                make_identity(nc, pool, ident[:], consts)
                all_images(pool, run)

            @block.scalar
            def _(act):
                def run(steps):
                    for what, k, n, s in steps:
                        if what == "split":
                            act.wait_ge(v_loaded, n * 16 + 16)
                            if not (isinstance(n, int) and n == 0):
                                act.wait_ge(y_done, n * UNITS - UNITS + HB)
                            nc.scalar.activation(v_hi[s][:], vT[s][:], ACT.Copy).then_inc(vhi_ready, 1)
                        if what == "weights":
                            act.wait_ge(w_loaded[k], n * 16 + 16)
                            st, hi, lo = weight(k, s)
                            nc.scalar.activation(hi, st, ACT.Copy).then_inc(whi_ready, 1)
                        if what == "hidden":
                            j, e, f = unit(k)
                            act.wait_ge(h_done, n * UNITS + k + 1)
                            act.wait_ge(h_split, n * UNITS + k + 1)
                            if k == 0:
                                act.wait_ge(small_loaded, n * (16 * (2 * TOPK + 1)) + 16 * (2 * TOPK + 1))
                            nc.scalar.activation(hid[k % 2][:], h_ps[k % 2][:], ACT.Gelu, bias=b1_sb[s][:, e, f:f + 1]
                                                 ).then_inc(hid_ready, 1)
                        if what == "turn":
                            for i in range(2):
                                act.wait_ge(turned, n * 4 + k * 2 + i + 1)
                                if i == 0:
                                    act.wait_ge(out_ready, n * 2 + k + 1)
                                nc.scalar.activation(zt[:, 2 * i:2 * i + 2, :], z_ps[i][:].rearrange("p (t c) -> p t c", t=2),
                                                     ACT.Copy).then_inc(zt_ready, 1)
                        if what == "rsqrt":
                            nc.scalar.preload_act_table_set("natural_log_exp_and_others")
                            act.wait_ge(var_ready, n * 2 + k + 1)
                            nc.scalar.activation(rstd[:], var[:], ACT.Ln)
                            act.drain()
                            nc.scalar.activation(rstd[:], rstd[:], ACT.Exp, scale=-0.5).then_inc(rstd_ready, 1)

                all_images(act, run)

            @block.vector
            def _(dve):
                def run(steps):
                    for what, k, n, s in steps:
                        if what == "split":
                            dve.wait_ge(vhi_ready, n + 1)
                            nc.vector.tensor_tensor(v_lo[s][:], vT[s][:], bits(v_hi[s][:]), ALU.subtract).then_inc(v_split, 1)
                            dve.wait_ge(small_loaded, n * (16 * (2 * TOPK + 1)) + 16 * (2 * TOPK + 1))
                            nc.vector.tensor_scalar(b2w[s][:], b2_sb[s][:, 0], wts[s][:, 0:1], None, ALU.mult)
                            dve.drain()
                            nc.vector.scalar_tensor_tensor(b2w[s][:], b2_sb[s][:, 1], wts[s][:, 1:2], b2w[s][:], ALU.mult, ALU.add)
                        if what == "hidden":
                            j, e, f = unit(k)
                            dve.wait_ge(hid_ready, n * UNITS + k + 3)
                            dve.wait_ge(y_done, n * UNITS + k + 1)
                            nc.vector.tensor_scalar(h_hi[k % HB][:], hid[k % 2][:], wts[s][:, e:e + 1], None, ALU.mult)
                            dve.drain()
                            nc.vector.scalar_tensor_tensor(h_lo[k % HB][:], hid[k % 2][:], wts[s][:, e:e + 1], bits(h_hi[k % HB][:]),
                                                           ALU.mult, ALU.subtract).then_inc(h_split, 1)
                        if what == "sum":
                            dve.wait_ge(y_done, n * UNITS + (k + 1) * (UNITS // 2) + HB)
                            for c in range(KC):
                                last = nc.vector.scalar_tensor_tensor(z[:, c, :], y_ps[k][c][:], b2w[s][:, c:c + 1], vT[s][:, c, half(k)],
                                                                      ALU.add, ALU.add)
                            last.then_inc(z_ready, 1)
                        if what == "stats":
                            dve.wait_ge(zt_ready, n * 4 + k * 2 + 4)
                            for i in range(HT):
                                nc.vector.bn_stats(st6[:, i, :], zt[:, i, :])
                            dve.drain()
                            for i in range(HT):
                                nc.vector.bn_aggr(mv[:, i, :], st6[:, i, :])
                            dve.drain()
                            nc.vector.tensor_scalar(var[:], mv[:, :, 1], 1e-5, None, ALU.add).then_inc(var_ready, 1)
                        if what == "norm":
                            dve.wait_ge(rstd_ready, n * 2 + k + 1)
                            newton(nc, dve, rstd[:], var[:], tmp[:])
                            for i in range(HT):
                                last = nc.vector.tensor_scalar(zt[:, i, :], zt[:, i, :], mv[:, i, 0:1], rstd[:, i:i + 1], ALU.subtract, ALU.mult)
                            last.then_inc(normed_ready, 1)

                all_images(dve, run)

            @block.tensor
            def _(pe):
                def run(steps):
                    for what, k, n, s in steps:
                        if what == "hidden":
                            j, e, f = unit(k)
                            if k == 0:
                                pe.wait_ge(v_split, n + 1)
                            if j == f == 0:
                                pe.wait_ge(w_split, n * NW + 2 * e + 1)
                            pe.wait_ge(hid_ready, n * UNITS + k + 1)
                            i = 0
                            for c in range(KC):
                                for w, v in ((w1_hi, v_hi), (w1_hi, v_lo), (w1_lo, v_hi)):
                                    m = nc.tensor.matmul(h_ps[k % 2][:], w[s][:, e, c, tile(f)], v[s][:, c, half(j)],
                                                         start=i == 0, stop=i == 3 * KC - 1)
                                    i += 1
                            m.then_inc(h_done, 1)
                        if what == "expert":
                            j, e, f = unit(k)
                            pe.wait_ge(h_split, n * UNITS + k + 3)
                            if j == f == 0:
                                pe.wait_ge(w_split, n * NW + 2 * e + 2)
                            if k % (UNITS // 2) == 0:
                                pe.wait_ge(z_ready, n * 2 + j + 1)
                            first, last = e + f == 0, e == TOPK - 1 and f == FC - 1
                            for c in range(KC):
                                for i, (w, h) in enumerate(((w2_hi, h_hi), (w2_hi, h_lo), (w2_lo, h_hi))):
                                    m = nc.tensor.matmul(y_ps[j][c][:], w[s][:, e, f, tile(c)], h[k % HB][:],
                                                         start=first and i == 0, stop=last and i == 2)
                            m.then_inc(y_done, 1)
                        if what == "turn":
                            pe.wait_ge(z_ready, n * 2 + k + 3)
                            for i in range(2):
                                pe.wait_ge(zt_ready, n * 4 + k * 2 + i + 1)
                                for t in range(2):
                                    for c in range(KC):
                                        m = nc.tensor.transpose(z_ps[i][:, t * C + c * P:t * C + (c + 1) * P], z[:, c, tile(2 * i + t)], ident[:])
                                m.then_inc(turned, 1)

                pe.sem_inc(hid_ready, 2)
                pe.sem_inc(h_split, 2)
                pe.sem_inc(y_done, HB)
                pe.sem_inc(z_ready, 2)
                pe.sem_inc(zt_ready, 2)
                pe.sem_inc(out_ready, 1)
                pe.wait_ge(consts, 1)
                all_images(pe, run)


_INS = ["x"] + ["L0_conv_" + n for n in ("conv_w", "conv_b", "qkv_w", "qkv_b", "attn_w", "attn_b", "key_rel_w", "key_rel_h")] + \
    ["L1_attn_" + n for n in ("W_q", "W_k", "W_v", "W_o", "b_o")] + \
    ["L1_ffn_" + n for n in ("Wr", "br", "W1", "b1", "W2", "b2", "gamma", "beta")]


def build(nc, a, out):
    def scratch(name, shape, dt=f32):
        return nc.dram_tensor(name, shape, dt, kind="Internal").ap()

    mixT_d = scratch("mixT_d", (B, KC, P, TOK))
    kq_d = scratch("kq_d", (B, GROUPS, 2, 2, HG * DH, TOK))
    rel_d = scratch("rel_d", (B, GROUPS, 2, 2, P, TOK))
    va_d = scratch("va_d", (B, GROUPS, P, TT * HG * 32))
    att_d = scratch("att_d", (B, GROUPS, P, TOK))
    rsum_d = scratch("rsum_d", (B, GROUPS, HG, TOK))
    t_d = scratch("t_d", (B, TOK, C))
    vT_d = scratch("vT_d", (B, KC, P, TOK))
    vsum_d = scratch("vsum_d", (B, P, KC, TT // 2))
    wts_d, idx_d = scratch("wts_d", (B, TOPK)), scratch("idx_d", (B, TOPK), mybir.dt.uint32)
    with (nc.sbuf_tensor("shared", [P, 2, FIRST, TOK], f32r) as shared,
          nc.sbuf_tensor("q_all", [P, B, TOK], f32r) as q_all,
          nc.sbuf_tensor("bd_hi", [P, 2, GROUPS, REL * HG], f32r) as bd_hi,
          nc.sbuf_tensor("bd_lo", [P, 2, GROUPS, REL * HG], f32r) as bd_lo,
          nc.semaphore("rel_first_stored") as first_stored):
        conv_phase(nc, a["x"], *[a["L0_conv_" + n] for n in ("conv_w", "conv_b", "qkv_w", "qkv_b", "key_rel_w", "key_rel_h")],
                   q_all, bd_hi, bd_lo, shared, first_stored, mixT_d, kq_d, rel_d, va_d)
        attention_phase(nc, q_all, bd_hi, bd_lo, shared, first_stored, kq_d, rel_d, va_d, att_d)
    self_attention_phase(nc, a["x"], a["L0_conv_attn_w"], a["L0_conv_attn_b"],
                         *[a["L1_attn_" + n] for n in ("W_q", "W_k", "W_v", "W_o", "b_o")],
                         mixT_d, att_d, rsum_d, t_d, vT_d, vsum_d)
    router_phase(nc, a["L1_ffn_Wr"], a["L1_ffn_br"], vsum_d, wts_d, idx_d)
    expert_phase(nc, *[a["L1_ffn_" + n] for n in ("W1", "b1", "W2", "b2", "gamma", "beta")], t_d, vT_d, wts_d, idx_d, out)


def kernel(**inputs):
    import numpy as _np
    import concourse.bacc as _bacc
    from concourse.bass_utils import run_bass_kernel_spmd as _run

    nc = _bacc.Bacc("TRN2", target_bir_lowering=False, num_devices=1)
    arrays, args = {}, {}
    for name in _INS:
        arrays["in_" + name] = _np.ascontiguousarray(inputs[name])
        args[name] = nc.dram_tensor("in_" + name, arrays["in_" + name].shape, f32, kind="ExternalInput").ap()
    out = nc.dram_tensor("out_0", (B, H, W, C), f32, kind="ExternalOutput").ap()
    build(nc, args, out)
    r = _run(nc, [arrays], core_ids=[0])
    return r.results[0]["out_0"]
```
